# Optimizing a Trainium2 kernel written in Bass

```python
import numpy as np
import jax
import jax.numpy as jnp

def _softmax(x, axis=-1):
    return jax.nn.softmax(x, axis=axis)

def _gelu(x):
    return jax.nn.gelu(x, approximate=True)

def _silu(x):
    return jax.nn.silu(x)

def _sigmoid(x):
    return jax.nn.sigmoid(x)

def _layernorm(x, axis=-1, eps=1e-05):
    m = jnp.mean(x, axis=axis, keepdims=True)
    v = jnp.var(x, axis=axis, keepdims=True)
    return (x - m) / jnp.sqrt(v + eps)

def _scatter_add(tgt, idx, src, axis=0):
    return tgt.at[idx].add(src)

def _segment_sum(src, seg, n):
    return jax.ops.segment_sum(src, seg, n)
kernel_name = 'mk_seq_preln_d1_jaxref_r8_f879c2'

def setup_inputs(seed: int=0):
    np.random.seed(seed)
    _w = jnp.asarray

    def _L0_attn_setup():
        import jax, jax.numpy as jnp
        import numpy as np
        DIM = 128
        N_HEADS = 16
        HEAD_DIM = DIM // N_HEADS
        B, T = (2, 256)
        ROPE_THETA = 32.0
        EPS = 1e-06

        def precompute_freqs_1d(dim, seq_len, theta):
            freqs = theta ** (-jnp.arange(0, dim, 2, dtype=jnp.float32) / dim)
            t = jnp.arange(seq_len, dtype=jnp.float32)
            ang = t[:, None] * freqs[None, :]
            return (jnp.cos(ang), jnp.sin(ang))

        def _rms_norm(t, w):
            var = jnp.mean(t * t, axis=-1, keepdims=True)
            return t * jax.lax.rsqrt(var + EPS) * w

        def _rope(q, k, cos, sin):
            cos = cos[None, None]
            sin = sin[None, None]
            q1, q2 = jnp.split(q, 2, axis=-1)
            k1, k2 = jnp.split(k, 2, axis=-1)
            q_out = jnp.concatenate([q1 * cos - q2 * sin, q2 * cos + q1 * sin], axis=-1)
            k_out = jnp.concatenate([k1 * cos - k2 * sin, k2 * cos + k1 * sin], axis=-1)
            return (q_out, k_out)
        key = jax.random.key(seed)
        k1, k2, k3, k4, k5 = jax.random.split(key, 5)
        x = jax.random.normal(k1, (B, T, DIM), dtype=jnp.float32)
        w_qkv = jax.random.normal(k2, (3 * DIM, DIM), dtype=jnp.float32) * DIM ** (-0.5)
        w_proj = jax.random.normal(k3, (DIM, DIM), dtype=jnp.float32) * DIM ** (-0.5)
        q_norm_w = 1.0 + 0.1 * jax.random.normal(k4, (HEAD_DIM,), dtype=jnp.float32)
        k_norm_w = 1.0 + 0.1 * jax.random.normal(k5, (HEAD_DIM,), dtype=jnp.float32)
        return {'x': x, 'w_qkv': w_qkv, 'w_proj': w_proj, 'q_norm_w': q_norm_w, 'k_norm_w': k_norm_w}
    _L0_attn_in = _L0_attn_setup()

    def _L0_ffn_setup():
        import jax, jax.numpy as jnp
        import numpy as np
        D_MODEL = 128
        NUM_TILES = 64
        TPC = 8
        NUM_CLUSTERS = NUM_TILES // TPC
        GRID = 16
        COMP_H = 32
        NUM_KNOTS = 8
        EPS_LN = 1e-05

        def _calibrate(scores, knots, temperature):
            K = knots.shape[0]
            normalized = jax.nn.sigmoid(scores / (temperature[0] + 1e-06))
            idx_float = normalized * (K - 1)
            idx_low = jnp.clip(idx_float.astype(jnp.int32), 0, K - 2)
            idx_high = idx_low + 1
            t = idx_float - idx_low.astype(scores.dtype)
            val_low = knots[idx_low]
            val_high = knots[idx_high]
            return val_low + t * (val_high - val_low)

        def _forward(x, signatures_raw, knot_values, temperature, compress_w1, compress_b1, compress_w2, compress_b2, spline_w1, spline_b1, spline_w2, spline_b2, directions, norm_gamma, norm_beta, output_scale):
            B, T, D = x.shape
            xf = x.reshape(-1, D)
            q = jnp.where(signatures_raw > 0.3, 1.0, jnp.where(signatures_raw < -0.3, -1.0, 0.0)).astype(signatures_raw.dtype)
            sigs = signatures_raw + jax.lax.stop_gradient(q - signatures_raw)
            cluster_sigs = jnp.sign(sigs.reshape(NUM_CLUSTERS, TPC, D).mean(axis=1))
            cluster_scores = xf @ cluster_sigs.T
            cluster_gates = _calibrate(cluster_scores, knot_values, temperature)
            cluster_idx = jnp.argmax(cluster_gates, axis=-1)
            tile_scores = xf @ sigs.T
            tile_gates = _calibrate(tile_scores, knot_values, temperature)
            gates_by_cluster = tile_gates.reshape(-1, NUM_CLUSTERS, TPC)
            sel_gates = jnp.take_along_axis(gates_by_cluster, cluster_idx[:, None, None], axis=1)[:, 0, :]
            local_idx = jnp.argmax(sel_gates, axis=-1)
            tile_idx = cluster_idx * TPC + local_idx
            h = jax.nn.gelu(xf @ compress_w1 + compress_b1, approximate=False)
            comp = jnp.tanh(h @ compress_w2 + compress_b2)
            w1 = spline_w1[tile_idx]
            b1 = spline_b1[tile_idx]
            hh = jax.nn.relu(jnp.einsum('ni,nig->ng', comp, w1) + b1)
            w2 = spline_w2[tile_idx]
            b2 = spline_b2[tile_idx]
            mag = jnp.einsum('ng,ngo->no', hh, w2) + b2
            ffn_out = mag * directions[tile_idx] * output_scale[0]
            y = xf + ffn_out
            mu = y.mean(axis=-1, keepdims=True)
            var = ((y - mu) ** 2).mean(axis=-1, keepdims=True)
            y = (y - mu) / jnp.sqrt(var + EPS_LN) * norm_gamma + norm_beta
            return y.reshape(B, T, D)
        key = jax.random.key(seed)
        ks = jax.random.split(key, 12)
        B, T = (4, 512)
        x = jax.random.normal(ks[0], (B, T, D_MODEL), dtype=jnp.float32)
        signatures_raw = jax.random.normal(ks[1], (NUM_TILES, D_MODEL), dtype=jnp.float32) * 0.5
        knot_values = jax.nn.sigmoid(jnp.linspace(-3.0, 3.0, NUM_KNOTS).astype(jnp.float32))
        temperature = jnp.ones((1,), dtype=jnp.float32)
        compress_w1 = jax.random.normal(ks[2], (D_MODEL, COMP_H), dtype=jnp.float32) * (1.0 / np.sqrt(D_MODEL))
        compress_b1 = jnp.zeros((COMP_H,), dtype=jnp.float32)
        compress_w2 = jax.random.normal(ks[3], (COMP_H, 2), dtype=jnp.float32) * (1.0 / np.sqrt(COMP_H))
        compress_b2 = jnp.zeros((2,), dtype=jnp.float32)
        spline_w1 = jax.random.normal(ks[4], (NUM_TILES, 2, GRID), dtype=jnp.float32) * (1.0 / np.sqrt(2.0))
        spline_b1 = jnp.zeros((NUM_TILES, GRID), dtype=jnp.float32)
        spline_w2 = jax.random.normal(ks[5], (NUM_TILES, GRID, 1), dtype=jnp.float32) * (1.0 / np.sqrt(GRID))
        spline_b2 = jnp.zeros((NUM_TILES, 1), dtype=jnp.float32)
        directions = jax.random.normal(ks[6], (NUM_TILES, D_MODEL), dtype=jnp.float32) * 0.02
        norm_gamma = jnp.ones((D_MODEL,), dtype=jnp.float32)
        norm_beta = jnp.zeros((D_MODEL,), dtype=jnp.float32)
        output_scale = jnp.ones((1,), dtype=jnp.float32) * 0.1
        return dict(x=x, signatures_raw=signatures_raw, knot_values=knot_values, temperature=temperature, compress_w1=compress_w1, compress_b1=compress_b1, compress_w2=compress_w2, compress_b2=compress_b2, spline_w1=spline_w1, spline_b1=spline_b1, spline_w2=spline_w2, spline_b2=spline_b2, directions=directions, norm_gamma=norm_gamma, norm_beta=norm_beta, output_scale=output_scale)
    _L0_ffn_in = _L0_ffn_setup()
    _d = {'L0_attn_x': _L0_attn_in['x'], 'L0_attn_w_qkv': _L0_attn_in['w_qkv'], 'L0_attn_w_proj': _L0_attn_in['w_proj'], 'L0_attn_q_norm_w': _L0_attn_in['q_norm_w'], 'L0_attn_k_norm_w': _L0_attn_in['k_norm_w'], 'L0_ffn_signatures_raw': _L0_ffn_in['signatures_raw'], 'L0_ffn_knot_values': _L0_ffn_in['knot_values'], 'L0_ffn_temperature': _L0_ffn_in['temperature'], 'L0_ffn_compress_w1': _L0_ffn_in['compress_w1'], 'L0_ffn_compress_b1': _L0_ffn_in['compress_b1'], 'L0_ffn_compress_w2': _L0_ffn_in['compress_w2'], 'L0_ffn_compress_b2': _L0_ffn_in['compress_b2'], 'L0_ffn_spline_w1': _L0_ffn_in['spline_w1'], 'L0_ffn_spline_b1': _L0_ffn_in['spline_b1'], 'L0_ffn_spline_w2': _L0_ffn_in['spline_w2'], 'L0_ffn_spline_b2': _L0_ffn_in['spline_b2'], 'L0_ffn_directions': _L0_ffn_in['directions'], 'L0_ffn_norm_gamma': _L0_ffn_in['norm_gamma'], 'L0_ffn_norm_beta': _L0_ffn_in['norm_beta'], 'L0_ffn_output_scale': _L0_ffn_in['output_scale']}
    _x0 = _d['L0_attn_x']
    _d['L0_attn_x'] = jax.random.normal(jax.random.fold_in(jax.random.key(seed), 1), (8, 512, 128), dtype=_x0.dtype)
    del _x0
    return _d

def reference(L0_attn_x, L0_attn_w_qkv, L0_attn_w_proj, L0_attn_q_norm_w, L0_attn_k_norm_w, L0_ffn_signatures_raw, L0_ffn_knot_values, L0_ffn_temperature, L0_ffn_compress_w1, L0_ffn_compress_b1, L0_ffn_compress_w2, L0_ffn_compress_b2, L0_ffn_spline_w1, L0_ffn_spline_b1, L0_ffn_spline_w2, L0_ffn_spline_b2, L0_ffn_directions, L0_ffn_norm_gamma, L0_ffn_norm_beta, L0_ffn_output_scale):

    def _L0_attn_ref(x, w_qkv, w_proj, q_norm_w, k_norm_w):
        import jax, jax.numpy as jnp
        import numpy as np
        DIM = 128
        N_HEADS = 16
        HEAD_DIM = DIM // N_HEADS
        B, T = (2, 256)
        ROPE_THETA = 32.0
        EPS = 1e-06

        def precompute_freqs_1d(dim, seq_len, theta):
            freqs = theta ** (-jnp.arange(0, dim, 2, dtype=jnp.float32) / dim)
            t = jnp.arange(seq_len, dtype=jnp.float32)
            ang = t[:, None] * freqs[None, :]
            return (jnp.cos(ang), jnp.sin(ang))

        def _rms_norm(t, w):
            var = jnp.mean(t * t, axis=-1, keepdims=True)
            return t * jax.lax.rsqrt(var + EPS) * w

        def _rope(q, k, cos, sin):
            cos = cos[None, None]
            sin = sin[None, None]
            q1, q2 = jnp.split(q, 2, axis=-1)
            k1, k2 = jnp.split(k, 2, axis=-1)
            q_out = jnp.concatenate([q1 * cos - q2 * sin, q2 * cos + q1 * sin], axis=-1)
            k_out = jnp.concatenate([k1 * cos - k2 * sin, k2 * cos + k1 * sin], axis=-1)
            return (q_out, k_out)
        Bc, Tc, C = x.shape
        scale = HEAD_DIM ** (-0.5)
        qkv = x @ w_qkv.T
        qkv = qkv.reshape(Bc, Tc, 3, N_HEADS, HEAD_DIM).transpose(2, 0, 3, 1, 4)
        q, k, v = (qkv[0], qkv[1], qkv[2])
        q = _rms_norm(q, q_norm_w)
        k = _rms_norm(k, k_norm_w)
        cos, sin = precompute_freqs_1d(HEAD_DIM, Tc, ROPE_THETA)
        q, k = _rope(q, k, cos, sin)
        attn = jnp.einsum('bhqd,bhkd->bhqk', q, k) * scale
        causal = jnp.triu(jnp.ones((Tc, Tc), dtype=bool), k=1)
        attn = jnp.where(causal, -jnp.inf, attn)
        attn = jax.nn.softmax(attn, axis=-1)
        out = jnp.einsum('bhqk,bhkd->bhqd', attn, v)
        out = out.transpose(0, 2, 1, 3).reshape(Bc, Tc, C)
        return out @ w_proj.T

    def _L0_ffn_ref(x, signatures_raw, knot_values, temperature, compress_w1, compress_b1, compress_w2, compress_b2, spline_w1, spline_b1, spline_w2, spline_b2, directions, norm_gamma, norm_beta, output_scale):
        import jax, jax.numpy as jnp
        import numpy as np
        D_MODEL = 128
        NUM_TILES = 64
        TPC = 8
        NUM_CLUSTERS = NUM_TILES // TPC
        GRID = 16
        COMP_H = 32
        NUM_KNOTS = 8
        EPS_LN = 1e-05

        def _calibrate(scores, knots, temperature):
            K = knots.shape[0]
            normalized = jax.nn.sigmoid(scores / (temperature[0] + 1e-06))
            idx_float = normalized * (K - 1)
            idx_low = jnp.clip(idx_float.astype(jnp.int32), 0, K - 2)
            idx_high = idx_low + 1
            t = idx_float - idx_low.astype(scores.dtype)
            val_low = knots[idx_low]
            val_high = knots[idx_high]
            return val_low + t * (val_high - val_low)

        def _forward(x, signatures_raw, knot_values, temperature, compress_w1, compress_b1, compress_w2, compress_b2, spline_w1, spline_b1, spline_w2, spline_b2, directions, norm_gamma, norm_beta, output_scale):
            B, T, D = x.shape
            xf = x.reshape(-1, D)
            q = jnp.where(signatures_raw > 0.3, 1.0, jnp.where(signatures_raw < -0.3, -1.0, 0.0)).astype(signatures_raw.dtype)
            sigs = signatures_raw + jax.lax.stop_gradient(q - signatures_raw)
            cluster_sigs = jnp.sign(sigs.reshape(NUM_CLUSTERS, TPC, D).mean(axis=1))
            cluster_scores = xf @ cluster_sigs.T
            cluster_gates = _calibrate(cluster_scores, knot_values, temperature)
            cluster_idx = jnp.argmax(cluster_gates, axis=-1)
            tile_scores = xf @ sigs.T
            tile_gates = _calibrate(tile_scores, knot_values, temperature)
            gates_by_cluster = tile_gates.reshape(-1, NUM_CLUSTERS, TPC)
            sel_gates = jnp.take_along_axis(gates_by_cluster, cluster_idx[:, None, None], axis=1)[:, 0, :]
            local_idx = jnp.argmax(sel_gates, axis=-1)
            tile_idx = cluster_idx * TPC + local_idx
            h = jax.nn.gelu(xf @ compress_w1 + compress_b1, approximate=False)
            comp = jnp.tanh(h @ compress_w2 + compress_b2)
            w1 = spline_w1[tile_idx]
            b1 = spline_b1[tile_idx]
            hh = jax.nn.relu(jnp.einsum('ni,nig->ng', comp, w1) + b1)
            w2 = spline_w2[tile_idx]
            b2 = spline_b2[tile_idx]
            mag = jnp.einsum('ng,ngo->no', hh, w2) + b2
            ffn_out = mag * directions[tile_idx] * output_scale[0]
            y = xf + ffn_out
            mu = y.mean(axis=-1, keepdims=True)
            var = ((y - mu) ** 2).mean(axis=-1, keepdims=True)
            y = (y - mu) / jnp.sqrt(var + EPS_LN) * norm_gamma + norm_beta
            return y.reshape(B, T, D)
        return _forward(x, signatures_raw, knot_values, temperature, compress_w1, compress_b1, compress_w2, compress_b2, spline_w1, spline_b1, spline_w2, spline_b2, directions, norm_gamma, norm_beta, output_scale)
    x = L0_attn_x
    x = x + _L0_attn_ref(_layernorm(x, axis=-1), L0_attn_w_qkv, L0_attn_w_proj, L0_attn_q_norm_w, L0_attn_k_norm_w)
    x = x + _L0_ffn_ref(_layernorm(x, axis=-1), L0_ffn_signatures_raw, L0_ffn_knot_values, L0_ffn_temperature, L0_ffn_compress_w1, L0_ffn_compress_b1, L0_ffn_compress_w2, L0_ffn_compress_b2, L0_ffn_spline_w1, L0_ffn_spline_b1, L0_ffn_spline_w2, L0_ffn_spline_b2, L0_ffn_directions, L0_ffn_norm_gamma, L0_ffn_norm_beta, L0_ffn_output_scale)
    return x

_drawn_inputs = setup_inputs


def setup_inputs(seed=0):
    import zlib

    import numpy as np

    out = dict(_drawn_inputs(seed))
    spreads = {'L0_ffn_compress_b1': (0.0, 0.8),
     'L0_ffn_compress_b2': (0.0, 2.0),
     'L0_ffn_spline_b1': (0.0, 2.0),
     'L0_ffn_spline_b2': (0.0, 2.0),
     'L0_ffn_norm_gamma': (1.0, 0.2),
     'L0_ffn_norm_beta': (0.0, 0.1)}
    factors = {'L0_attn_q_norm_w': 4.015,
     'L0_attn_k_norm_w': 3.495,
     'L0_ffn_signatures_raw': 8.0,
     'L0_ffn_knot_values': 8.0,
     'L0_ffn_compress_w1': 8.0,
     'L0_ffn_compress_w2': 8.0,
     'L0_ffn_spline_w1': 8.0,
     'L0_ffn_spline_w2': 8.0,
     'L0_ffn_directions': 8.0}
    for name, (base, spread) in spreads.items():
        noise = np.random.default_rng([zlib.crc32(name.encode()), seed]).standard_normal(out[name].shape)
        drawn = base * np.exp(spread * noise) if base else spread * noise
        out[name] = jnp.asarray(drawn.astype(out[name].dtype))
    for name, factor in factors.items():
        out[name] = (out[name] * factor).astype(out[name].dtype)
    return out
```

```python
from contextlib import ExitStack

import numpy as np

import concourse.bass as bass
from concourse import mybir

F32 = mybir.dt.float32
BF16 = mybir.dt.bfloat16
ALU = mybir.AluOpType
ACT = mybir.ActivationFunctionType
AX = mybir.AxisListType

P = 128
B, T, D = 8, 512, 128
H, HD = 16, 8
TT = T // P
NT = B * TT
NQ = H // 4
NP = 3
ROWS = 6 * HD
SROWS = ROWS + NP
Q_PARTS = (0, 0, 0, 1, 1, 2)
K_PARTS = (0, 1, 2, 0, 1, 0)
SLOTS = 5
SW = 1024
VW = 32
NTILE, TPC, NCL = 64, 8, 8
GRID, COMP, KNOTS = 16, 32, 8
NSC = NCL + NTILE + COMP
TABW = 4 * GRID + 1 + D
EPS_LN, EPS_RMS = 1e-5, 1e-6
SCALE = HD ** -0.5
THETA = 32.0
BIG = 3.0e38
MASKED = -1.0e30
SAFE = 64.0
G = 16

C_ID = 0
C_MIN = C_ID + P
C_COS = C_MIN + P
C_SIN = C_COS + TT * HD
C_STEP = C_SIN + TT * HD
C_J = C_STEP + KNOTS
C_PREF = C_J + KNOTS
C_EPS = C_PREF + 8
NCONST = C_EPS + 2

V_QW = 0
V_KW = V_QW + HD
V_KNOT = V_KW + HD
V_TEMP = V_KNOT + KNOTS
V_B1 = V_TEMP + 1
V_W2 = V_B1 + COMP
V_B2 = V_W2 + 2 * COMP
V_GAM = V_B2 + 2
V_BET = V_GAM + D
V_OS = V_BET + D
NVEC = V_OS + 1


def unit_of(kb, c):
    hh, gg = c // 2, c % 2
    if kb == 0:
        return 3 * gg, 512 * hh
    if kb == 2:
        return 2, 512 * hh + 256 * gg
    return 3 * gg + 1, 512 * hh + (384 if kb == 3 else 0)


def build(nc, x_d, wqkv_d, wproj_d, sig_d, cw1_d, tab_d, vec_d, const_d, out_d):
    with ExitStack() as ctx:
        def sb(name, shape, dt=F32):
            return ctx.enter_context(nc.sbuf_tensor(name, shape, dt))

        def psum(name, shape):
            return ctx.enter_context(nc.psum_tensor(name, shape, F32))

        def sem(name):
            return ctx.enter_context(nc.semaphore(name))

        xs = sb("xs", [P, B, TT, D])
        xf = sb("xf", [P, B, TT, D])
        sc = sb("sc", [P, NT, NSC])
        vtok = sb("vtok", [P, B, TT, D])
        const = sb("const", [P, NCONST])
        vec = sb("vec", [P, NVEC])
        wqkv = sb("wqkv", [P, 3 * D])
        wproj = sb("wproj", [P, D])
        wsc = sb("wsc", [P, NSC])
        sig = sb("sig", [P, NTILE])
        sg = sb("sg", [P, 3, NTILE])
        csum = sb("csum", [P, 2, NCL])
        cwt = sb("cwt", [P, TT, 2, HD])
        swt = sb("swt", [P, TT, 2, HD])
        wsq = sb("wsq", [P, 2, HD])
        tab = sb("tab", [NTILE, TABW])
        st6 = sb("st6", [P, TT, 6])
        mv = sb("mv", [P, TT, 2])
        lnr = sb("lnr", [P, 6, TT])
        xn = sb("xn", [P, TT, D])
        xnT = sb("xnT", [P, T])
        zqk = sb("zqk", [P, TT, 2 * D])
        sq = sb("sq", [P, TT, 2 * D])
        rr = sb("rr", [P, 6, TT * 2 * H])
        zn = sb("zn", [P, TT, 2 * D])
        rb = sb("rb", [P, TT, 2 * D])
        qkr = sb("qkr", [P, TT, 2, D])
        parts = sb("parts", [P, 2, NP, T], BF16)
        rest = sb("rest", [P, 2, T])
        stq = sb("stq", [P, NQ, 2, T], BF16)
        stk = sb("stk", [P, NQ, 2, T], BF16)
        vaug = sb("vaug", [P, TT, H, VW])
        pt = sb("pt", [P, 2, SLOTS * SW])
        oT = sb("oT", [P, 2, T])
        rec = sb("rec", [P, TT, 4])
        on = sb("on", [P, TT, D])
        onT = sb("onT", [P, T])
        st6b = sb("st6b", [P, TT, 6])
        mvb = sb("mvb", [P, TT, 2])
        lnrb = sb("lnrb", [P, 6, TT])
        xf1 = sb("xf1", [P, TT, D])
        xfT = sb("xfT", [P, T])

        gap = sb("gap", [P, 1])
        wabs = sb("wabs", [P, 4])
        beyond = sb("beyond", [P, 1], mybir.dt.int32)
        ident_b = sb("ident_b", [P, P], BF16)
        above_b = sb("above_b", [P, P], BF16)
        nmax = sb("nmax", [P, 2, TT * 4])
        nmax_b = sb("nmax_b", [P, 2, TT * 4], BF16)
        nparts = sb("nparts", [P, TT * 4, NP])
        shift = sb("shift", [4 * NP, T], BF16)
        nrt = sb("nrt", [P, 2])
        dk = sb("dk", [P, KNOTS - 1])
        top = sb("top", [P, NT])
        comp = sb("comp", [P, 2, NT])
        mag = sb("mag", [P, NT])
        st6c = sb("st6c", [P, NT, 6])
        mvc = sb("mvc", [P, NT, 2])
        lnrc = sb("lnrc", [P, 6, NT])

        psS = psum("psS", [P, 2, SW])
        psO = psum("psO", [P, 2, 512])
        psA = psum("psA", [P, 512])
        psC = psum("psC", [P, 512])

        scratch = nc.dram_tensor("stacks", [B, 2, H, 6, HD, T], BF16, kind="Internal").ap()

        (const_in, w_in, x0_in, x1_in, xr_in, out_done, scr_done,
         wsc_ready, rope_ready, zeros_ready,
         stat1, mv1, ln1, r01, nw1, xn_ready, t1_done, xnT_done, z_done, z_copied, sq_done,
         ss_done, lnq, rq0, nwq, rq_done, zn_done, rope_a, rope_b, qkr_done,
         kt_done, p1_done, rest_done, p2_done, parts_done,
         s_ready, exp_done, mask_done, v_ready, pv_done, o_copied, ot_done, rec_done, on_done,
         op_done, onT_done, pr_done, x1_done,
         stat2, mv2, ln2, r02, nw2, xf1_ready, xf_stored, xt_done, xfT_done, sc_done, sc_copied,
         beyond_ready, smax_ready, smax_read, nmax_step, nmax_ready, shift_ps, shift_ready, shift_in,
         prep_dve, tail_dve, tail_pool, ex_done, u7_ready, line_ready, sel_ready, hot_ready, hot_done,
         hotT_ready, got_done, got_copied, hid_ready, gelu_done, prod_ready, cpre_ready, tanh_done,
         stat3, mv3, ln3, r03, nw3, yn_ready, ygb_ready, out_ready) = [sem(n) for n in (
            "const_in w_in x0_in x1_in xr_in out_done scr_done "
            "wsc_ready rope_ready zeros_ready "
            "stat1 mv1 ln1 r01 nw1 xn_ready t1_done xnT_done z_done z_copied sq_done "
            "ss_done lnq rq0 nwq rq_done zn_done rope_a rope_b qkr_done "
            "kt_done p1_done rest_done p2_done parts_done "
            "s_ready exp_done mask_done v_ready pv_done o_copied ot_done rec_done on_done "
            "op_done onT_done pr_done x1_done "
            "stat2 mv2 ln2 r02 nw2 xf1_ready xf_stored xt_done xfT_done sc_done sc_copied "
            "beyond_ready smax_ready smax_read nmax_step nmax_ready shift_ps shift_ready shift_in "
            "prep_dve tail_dve tail_pool ex_done u7_ready line_ready sel_ready hot_ready hot_done "
            "hotT_ready got_done got_copied hid_ready gelu_done prod_ready cpre_ready tanh_done "
            "stat3 mv3 ln3 r03 nw3 yn_ready ygb_ready out_ready").split()]
        stack_in = [sem(f"stack_in{j}") for j in range(NQ)]

        NG = NT * NCL
        ptf = pt[:, :, :].rearrange("p a n -> p (a n)")
        got = ptf[:, 0:NT * TABW].rearrange("p (t n) -> p t n", n=TABW)
        step = ptf[:, 0:NG * KNOTS].rearrange("p (g k) -> p g k", k=KNOTS)
        cell = ptf[:, 2048:2048 + NG * (KNOTS - 1)].rearrange("p (g k) -> p g k", k=KNOTS - 1)
        line = ptf[:, 4096:4096 + NG * (KNOTS - 1)].rearrange("p (g k) -> p g k", k=KNOTS - 1)
        hot = ptf[:, 8192:8192 + NT * NTILE].rearrange("p (t n) -> p t n", n=NTILE)
        hotT = vtok[:, :, :, :].rearrange("p b t d -> p (b t d)")[0:NTILE, :]
        zf = zqk[:, :, :].rearrange("p t d -> p (t d)")
        sf = sq[:, :, :].rearrange("p t d -> p (t d)")
        ex, u7, gate, eq = (zf[:, n * NG:(n + 1) * NG] for n in range(4))
        pref, hot_c, sel, hot_t = (sf[:, n * NG:(n + 1) * NG] for n in range(4))
        hid = zn[:, :, :].rearrange("p t (a n) -> p (t a) n", n=COMP)
        prod0 = rb[:, :, :].rearrange("p t (a n) -> p (t a) n", n=COMP)
        prod1 = qkr[:, :, :, :].rearrange("p t k (a n) -> p (t k a) n", n=COMP)
        m01 = rest[:, :, :].rearrange("p a (t n) -> p a t n", n=GRID)
        xsf = xs[:, :, :, :].rearrange("p b t d -> p (b t) d")
        xff = xf[:, :, :, :].rearrange("p b t d -> p (b t) d")
        ident = const[:, C_ID:C_ID + P]
        eps_ln = const[:, C_EPS:C_EPS + 1]
        eps_rms = const[:, C_EPS + 1:C_EPS + 2]
        block = ctx.enter_context(nc.Block())

        def over_batches(eng, body):
            body(0)
            with eng.Fori(1, B - 3) as b:
                body(b)
            for b in range(B - 3, B + 1):
                body(b)

        def either(eng, main):
            eng.wait_ge(beyond_ready, 1)
            far = eng.value_load(beyond[0:1, 0:1], min_val=0, max_val=1)
            with eng.If(far > 0):
                main(True)
            with eng.Else():
                main(False)

        def place(b):
            return b if isinstance(b, int) else 1

        def later(i, n):
            return i >= n if isinstance(i, int) else True

        @block.sync
        def _(sp):
            sp.dma_start(const[:, :], const_d).then_inc(const_in, 16)
            sp.dma_start(xs[:, 0], x_d[0].rearrange("(t p) d -> p t d", p=P)).then_inc(x0_in, 16)
            sp.dma_start(vec[:, :], vec_d.broadcast_to([P, NVEC])).then_inc(w_in, 16)
            sp.dma_start(wqkv[:, :], wqkv_d).then_inc(w_in, 16)
            sp.dma_start(xs[:, 1], x_d[1].rearrange("(t p) d -> p t d", p=P)).then_inc(x1_in, 16)
            sp.dma_start(sig[:, :], sig_d).then_inc(w_in, 16)
            sp.dma_start(wproj[:, :], wproj_d).then_inc(w_in, 16)
            sp.dma_start(wsc[:, NCL + NTILE:NSC], cw1_d).then_inc(w_in, 16)
            sp.dma_start(tab[:, :], tab_d).then_inc(w_in, 16)
            for i in range(2, B):
                sp.dma_start(xs[:, i], x_d[i].rearrange("(t p) d -> p t d", p=P)).then_inc(xr_in, 16)

            def store_parts(i):
                sp.wait_ge(parts_done, (i + 1) * 2)
                for r in range(6):
                    sp.dma_start(scratch[i, 0, :, r], parts[:, 0, Q_PARTS[r], :]).then_inc(scr_done, 16)
                    sp.dma_start(scratch[i, 1, :, r], parts[:, 1, K_PARTS[r], :]).then_inc(scr_done, 16)

            def load_stack(i, j):
                if later(i, 1):
                    sp.wait_ge(s_ready, (i - 1) * (NQ * SLOTS) + (j + 1) * SLOTS)
                for qk, st in ((0, stq), (1, stk)):
                    for hh in range(2):
                        h = 4 * j + 2 * hh
                        sp.dma_start(st[64 * hh:64 * hh + ROWS, j],
                                     scratch[i, qk, h:h + 2].rearrange("g r d t -> (r d) g t"))\
                          .then_inc(stack_in[j], 16)

            store_parts(0)
            sp.wait_ge(zeros_ready, 2)
            sp.wait_ge(scr_done, 12 * 16)
            for j in range(NQ):
                load_stack(0, j)
            store_parts(1)

            def body(b):
                k = place(b)
                if k < B - 1:
                    sp.wait_ge(scr_done, (b + 2) * (12 * 16))
                    for j in range(NQ):
                        load_stack(b + 1, j)
                if k < B - 2:
                    store_parts(b + 2)

            over_batches(sp, body)
            for k in range(NT // G):
                sp.wait_ge(out_ready, k + 1)
                nb = G // TT
                for i in range(k * nb, (k + 1) * nb):
                    sp.dma_start(out_d[i].rearrange("(t p) d -> p t d", p=P), xs[:, i]).then_inc(out_done, 16)
            sp.wait_ge(out_done, B * 16)

        @block.tensor
        def _(pe):
            def transposes(dst, srcs):
                for t, s in enumerate(srcs):
                    ins = nc.tensor.transpose(dst[:, t * P:(t + 1) * P], s, ident)
                return ins

            def norm_transposed(i):
                pe.wait_ge(xn_ready, i + 1)
                if later(i, 2):
                    pe.wait_ge(rest_done, 2 * i - 2)
                elif i == 1:
                    pe.wait_ge(z_copied, TT)
                transposes(psA, [xn[:, t, :] for t in range(TT)]).then_inc(t1_done, 1)

            def project(i, t):
                if t == 0:
                    pe.wait_ge(xnT_done, i + 1)
                else:
                    pe.wait_ge(z_copied, i * TT + t)
                nc.tensor.matmul(psA[:, 0:3 * D], xnT[:, t * P:(t + 1) * P], wqkv[:, :],
                                 start=True, stop=True).then_inc(z_done, 1)

            def qk_transposed(i, qk):
                if qk == 0:
                    pe.wait_ge(qkr_done, i + 1)
                    nxt = min(i + 2, B) if isinstance(i, int) else i + 2
                    pe.wait_ge(z_copied, nxt * TT)
                else:
                    pe.wait_ge(rest_done, 2 * i + 1)
                transposes(psA, [qkr[:, t, qk, :] for t in range(TT)]).then_inc(kt_done, 1)

            def maxima(b, j):
                n = b * NQ + j
                pe.wait_ge(stack_in[j], (b + 1) * 64)
                if later(n, 1):
                    pe.wait_ge(exp_done, n * SLOTS - 1)
                for e in range(4 * TT):
                    c, qb = e // TT, e % TT
                    hh, gg = c // 2, c % 2
                    if later(n, 1) or e >= 2:
                        pe.wait_ge(smax_read, n * (4 * TT) + (e - 1))
                    bank = psS[:, j % 2, (e % 2) * 512:(e % 2) * 512 + 512]
                    nc.tensor.matmul(bank[:, 0:(qb + 1) * P],
                                     stq[64 * hh:64 * hh + ROWS, j, gg, qb * P:(qb + 1) * P],
                                     stk[64 * hh:64 * hh + ROWS, j, gg, 0:(qb + 1) * P], start=True, stop=False)
                    nc.tensor.matmul(bank[:, qb * P:(qb + 1) * P], ident_b[:, :], above_b[:, :],
                                     start=False, stop=True).then_inc(smax_ready, 1)
                pe.wait_ge(nmax_ready, n + 1)
                for qb in range(TT):
                    ins = nc.tensor.transpose(psS[0:4 * NP, j % 2, qb * P:(qb + 1) * P],
                                              nparts[:, qb * 4:(qb + 1) * 4, :].rearrange("p c r -> p (c r)"), ident)
                ins.then_inc(shift_ps, 1)
                pe.wait_ge(shift_in, (n + 1) * 64)

            def scores(b, j, s):
                g = b * (NQ * SLOTS) + (j * SLOTS + s)
                if s == 0:
                    pe.wait_ge(stack_in[j], (b + 1) * 64)
                if later(g, 2):
                    pe.wait_ge(exp_done, g - 1)
                for c in (0, 2, 1, 3):
                    hh, gg = c // 2, c % 2
                    for kb in range(TT):
                        u, off = unit_of(kb, c)
                        if u != s:
                            continue
                        ins = nc.tensor.matmul(
                            psS[:, (j * SLOTS + s) % 2, off:off + T - kb * P],
                            stk[64 * hh:64 * hh + SROWS, j, gg, kb * P:(kb + 1) * P],
                            stq[64 * hh:64 * hh + SROWS, j, gg, kb * P:T], start=True, stop=True)
                ins.then_inc(s_ready, 1)

            def attend(b, j, kb):
                n = b * NQ + j
                if kb == 0:
                    pe.wait_ge(mask_done, n * SLOTS + SLOTS)
                    pe.wait_ge(v_ready, n + 1)
                    if later(n, 2):
                        pe.wait_ge(o_copied, n - 1)
                for c in range(4):
                    u, off = unit_of(kb, c)
                    ins = nc.tensor.matmul(psO[32 * c:32 * c + VW, j % 2, kb * P:T],
                                           vaug[:, kb, 4 * j + c, :],
                                           pt[:, j % 2, u * SW + off:u * SW + off + T - kb * P],
                                           start=(kb == 0), stop=(kb == TT - 1))
                if kb == TT - 1:
                    ins.then_inc(pv_done, 1)

            def quad_transposed(b, j, free, value):
                n = b * NQ + j
                pe.wait_ge(o_copied, n + 1)
                if free is not None:
                    pe.wait_ge(free, value)
                transposes(psC, [oT[:, j % 2, t * P:(t + 1) * P] for t in range(TT)]).then_inc(ot_done, 1)

            def heads_transposed(i):
                pe.wait_ge(on_done, (i + 1) * NQ)
                transposes(psC, [on[:, t, :] for t in range(TT)]).then_inc(op_done, 1)

            def output_projection(i):
                pe.wait_ge(onT_done, i + 1)
                for t in range(TT):
                    ins = nc.tensor.matmul(psC[:, t * D:(t + 1) * D], onT[:, t * P:(t + 1) * P], wproj[:, :],
                                           start=True, stop=True)
                ins.then_inc(pr_done, 1)

            def router_transposed(i, free, value):
                pe.wait_ge(xf1_ready, i + 1)
                pe.wait_ge(free, value)
                transposes(psC, [xf1[:, t, :] for t in range(TT)]).then_inc(xt_done, 1)

            def router_scores(i):
                pe.wait_ge(xfT_done, i + 1)
                for t in range(TT):
                    ins = nc.tensor.matmul(psC[:, t * NSC:(t + 1) * NSC], xfT[:, t * P:(t + 1) * P], wsc[:, :],
                                           start=True, stop=True)
                ins.then_inc(sc_done, 1)

            def body(b, exact):
                k = place(b)
                for s in range(NQ * SLOTS):
                    j = s // SLOTS
                    jj = (j + 1) % NQ
                    if exact and s % SLOTS == 0:
                        if j < NQ - 1 and k < B:
                            maxima(b, jj)
                        elif j == NQ - 1 and k < B - 1:
                            maxima(b + 1, jj)
                    if j < NQ - 1 and k < B:
                        scores(b, jj, s % SLOTS)
                    elif j == NQ - 1 and k < B - 1:
                        scores(b + 1, jj, s % SLOTS)
                    if s % SLOTS > 0 and k < B:
                        attend(b, j, s % SLOTS - 1)
                    if k < B - 3:
                        if s == 3:
                            norm_transposed(b + 3)
                        if s in (5, 7, 9, 11):
                            project(b + 3, (s - 5) // 2)
                    if k < B - 2:
                        if s == 13:
                            qk_transposed(b + 2, 0)
                        if s == 15:
                            qk_transposed(b + 2, 1)
                    if s == 1 and k >= 1:
                        quad_transposed(b - 1, 3, on_done, b * NQ - 1)
                    if s == 3 and k >= 1:
                        heads_transposed(b - 1)
                    if s == 5 and k >= 1:
                        output_projection(b - 1)
                    if s == 6 and k < B:
                        quad_transposed(b, 0, x1_done if k >= 1 else None, b)
                    if s == 11 and k < B:
                        quad_transposed(b, 1, on_done, b * NQ + 1)
                    if s == 13 and k >= 1:
                        if k < B:
                            router_transposed(b - 1, on_done, b * NQ + 2)
                        else:
                            router_transposed(b - 1, x1_done, b)
                    if s == 15 and k >= 1:
                        router_scores(b - 1)
                    if s == 17 and k < B:
                        if k >= 1:
                            quad_transposed(b, 2, sc_copied, b)
                        else:
                            quad_transposed(b, 2, on_done, b * NQ + 2)

            pe.wait_ge(const_in, 16)
            pe.wait_ge(w_in, 6 * 16)
            for i in range(3):
                norm_transposed(i)
                for t in range(TT):
                    project(i, t)
                if i >= 1:
                    qk_transposed(i - 1, 0)
                    qk_transposed(i - 1, 1)
            pe.wait_ge(wsc_ready, 1)
            pe.wait_ge(zeros_ready, 2)

            def main(exact):
                if exact:
                    maxima(0, 0)
                for s in range(SLOTS):
                    scores(0, 0, s)
                over_batches(pe, lambda b: body(b, exact))

            either(pe, main)

            pe.wait_ge(hot_ready, 1)
            for q in range(NT // 4):
                if q >= 2:
                    pe.wait_ge(hotT_ready, q - 1)
                bank = (psA, psC)[q % 2]
                for t in range(4):
                    ins = nc.tensor.transpose(bank[0:NTILE, t * P:(t + 1) * P], hot[:, 4 * q + t, :], ident)
                ins.then_inc(hot_done, 1)
            for q in range(NT // 2):
                pe.wait_ge(hotT_ready, q // 2 + 1)
                if q >= 4:
                    pe.wait_ge(got_copied, q - 3)
                for t in range(2):
                    ins = nc.tensor.matmul(psS[:, (q % 4) // 2, (q % 2) * 512 + t * 256:(q % 2) * 512 + t * 256 + TABW],
                                           hotT[:, (2 * q + t) * P:(2 * q + t + 1) * P], tab[:, :],
                                           start=True, stop=True)
                ins.then_inc(got_done, 1)

        @block.scalar
        def _(act):
            nc.scalar.preload_act_table_set("natural_log_exp_and_others")

            def rsqrt_start(out, tmp, in_, scale, eps, log_sem, done_sem, i):
                nc.scalar.activation(tmp, in_, ACT.Ln, bias=eps, scale=scale).then_inc(log_sem, 1)
                act.wait_ge(log_sem, i + 1)
                nc.scalar.activation(out, tmp, ACT.Exp, scale=-0.5).then_inc(done_sem, 1)

            def norm1(i):
                act.wait_ge(mv1, i + 1)
                rsqrt_start(lnr[:, 1, :], lnr[:, 0, :], mv[:, :, 1], 1.0, eps_ln, ln1, r01, i)

            def norm2(i):
                act.wait_ge(mv2, i + 1)
                rsqrt_start(lnrb[:, 1, :], lnrb[:, 0, :], mvb[:, :, 1], 1.0, eps_ln, ln2, r02, i)

            def norm_heads(i):
                act.wait_ge(ss_done, i + 1)
                rsqrt_start(rr[:, 1, :], rr[:, 5, :], rr[:, 0, :], 1.0 / HD, eps_rms, lnq, rq0, i)

            def copy_projected(i, t):
                act.wait_ge(z_done, i * TT + (t + 1))
                if t == 0 and later(i, 1):
                    act.wait_ge(zn_done, i)
                nc.scalar.activation(zqk[:, t, :], psA[:, 0:2 * D], ACT.Copy)
                nc.scalar.activation(vtok[:, i, t, :], psA[:, 2 * D:3 * D], ACT.Copy).then_inc(z_copied, 1)

            def exponentials(b, j, s):
                g = b * (NQ * SLOTS) + (j * SLOTS + s)
                act.wait_ge(s_ready, g + 1)
                if s == 0 and later(b * NQ + j, 2):
                    act.wait_ge(pv_done, b * NQ + (j - 1))
                nc.scalar.activation(pt[:, j % 2, s * SW:(s + 1) * SW], psS[:, (j * SLOTS + s) % 2, :],
                                     ACT.Exp).then_inc(exp_done, 1)

            def load_shift(b, j):
                n = b * NQ + j
                act.wait_ge(shift_ready, n + 1)
                for c in range(4):
                    hh, gg = c // 2, c % 2
                    act.dma_start(stq[64 * hh + ROWS:64 * hh + SROWS, j, gg, :], shift[c * NP:(c + 1) * NP, :])\
                       .then_inc(shift_in, 16)

            def body(b, exact):
                k = place(b)
                for s in range(NQ * SLOTS):
                    j = s // SLOTS
                    jj = (j + 1) % NQ
                    if exact and s % SLOTS == 0:
                        if j < NQ - 1 and k < B:
                            load_shift(b, jj)
                        elif j == NQ - 1 and k < B - 1:
                            load_shift(b + 1, jj)
                    if j < NQ - 1 and k < B:
                        exponentials(b, jj, s % SLOTS)
                    elif j == NQ - 1 and k < B - 1:
                        exponentials(b + 1, jj, s % SLOTS)
                    if k < B - 3:
                        if s == 1:
                            norm1(b + 3)
                        if s in (5, 7, 9, 11):
                            copy_projected(b + 3, (s - 5) // 2)
                        if s == 15:
                            norm_heads(b + 3)
                    if k >= 1:
                        if s == 4:
                            act.wait_ge(op_done, b)
                            nc.scalar.activation(onT[:, :], psC[:, :], ACT.Copy).then_inc(onT_done, 1)
                        if s == 8:
                            norm2(b - 1)
                        if s == 14:
                            act.wait_ge(xt_done, b)
                            nc.scalar.activation(xfT[:, :], psC[:, :], ACT.Copy).then_inc(xfT_done, 1)

            act.wait_ge(const_in, 16)
            for i in range(3):
                norm1(i)
                for t in range(TT):
                    copy_projected(i, t)
                norm_heads(i)

            def main(exact):
                if exact:
                    load_shift(0, 0)
                for s in range(SLOTS):
                    exponentials(0, 0, s)
                over_batches(act, lambda b: body(b, exact))

            either(act, main)

            act.wait_ge(sc_copied, B)
            nc.scalar.activation(ex.rearrange("p (t c) -> p t c", c=NCL), sc[:, :, 0:NCL], ACT.Exp,
                                 scale=nrt[:, 0:1]).then_inc(ex_done, 1)
            act.wait_ge(sel_ready, 1)
            nc.scalar.activation(ex, sel, ACT.Exp, scale=nrt[:, 0:1]).then_inc(ex_done, 1)
            act.wait_ge(hid_ready, 1)
            nc.scalar.activation(hid, hid, ACT.Gelu).then_inc(gelu_done, 1)
            for q in range(NT // 4):
                act.wait_ge(hot_done, q + 1)
                nc.scalar.activation(hotT[:, q * 4 * P:(q + 1) * 4 * P], (psA, psC)[q % 2][0:NTILE, :], ACT.Copy)\
                  .then_inc(hotT_ready, 1)
            act.wait_ge(cpre_ready, 1)
            nc.scalar.activation(comp[:, :, :], comp[:, :, :], ACT.Tanh).then_inc(tanh_done, 1)
            for q in range(NT // 2):
                act.wait_ge(got_done, q + 1)
                src = psS[:, (q % 4) // 2, (q % 2) * 512:(q % 2) * 512 + 512].rearrange("p (t n) -> p t n", t=2)
                nc.scalar.activation(got[:, 2 * q:2 * q + 2, :], src[:, :, 0:TABW], ACT.Copy).then_inc(got_copied, 1)
            for k in range(NT // G):
                act.wait_ge(mv3, k + 1)
                c = slice(k * G, (k + 1) * G)
                rsqrt_start(lnrc[:, 1, c], lnrc[:, 0, c], mvc[:, c, 1], 1.0, eps_ln, ln3, r03, k)

        @block.vector
        def _(dve):
            ncv = nc.vector

            def prepare():
                dve.wait_ge(const_in, 16)
                dve.wait_ge(w_in, 6 * 16)
                n = [0]

                def link(ins):
                    n[0] += 1
                    ins.then_inc(prep_dve, 1)
                    dve.wait_ge(prep_dve, n[0])
                ncv.tensor_scalar(sg[:, 0], sig[:, :], 0.3, None, ALU.is_gt)
                link(ncv.tensor_scalar(sg[:, 1], sig[:, :], -0.3, None, ALU.is_lt))
                link(ncv.tensor_tensor(sg[:, 2], sg[:, 0], sg[:, 1], ALU.subtract))
                link(ncv.tensor_tensor(sg[:, 0], sg[:, 2], sig[:, :], ALU.subtract))
                link(ncv.tensor_tensor(wsc[:, NCL:NCL + NTILE], sig[:, :], sg[:, 0], ALU.add))
                tiles = wsc[:, NCL:NCL + NTILE].rearrange("p (c t) -> p t c", t=TPC)
                link(ncv.tensor_tensor(csum[:, 0], tiles[:, 0], tiles[:, 1], ALU.add))
                for t in range(2, TPC):
                    link(ncv.tensor_tensor(csum[:, 0], csum[:, 0], tiles[:, t], ALU.add))
                ncv.tensor_scalar(csum[:, 1], csum[:, 0], 0.0, None, ALU.is_gt)
                link(ncv.tensor_scalar(sg[:, 0, 0:NCL], csum[:, 0], 0.0, None, ALU.is_lt))
                ncv.tensor_tensor(wsc[:, 0:NCL], csum[:, 1], sg[:, 0, 0:NCL], ALU.subtract).then_inc(wsc_ready, 1)
                link(ncv.tensor_scalar(nrt[:, 0:1], vec[:, V_TEMP:V_TEMP + 1], 1e-6, None, ALU.add))
                link(ncv.reciprocal(nrt[:, 1:2], nrt[:, 0:1]))
                ncv.tensor_scalar(nrt[:, 0:1], nrt[:, 1:2], -1.0, None, ALU.mult)
                ncv.tensor_tensor(dk[:, :], vec[:, V_KNOT + 1:V_KNOT + KNOTS], vec[:, V_KNOT:V_KNOT + KNOTS - 1],
                                  ALU.subtract)
                ncv.tensor_reduce(wabs[:, 0:1], vec[:, V_QW:V_QW + HD], axis=AX.X, op=ALU.max,
                                  apply_absolute_value=True)
                link(ncv.tensor_reduce(wabs[:, 1:2], vec[:, V_KW:V_KW + HD], axis=AX.X, op=ALU.max,
                                       apply_absolute_value=True))
                link(ncv.tensor_tensor(wabs[:, 2:3], wabs[:, 0:1], wabs[:, 1:2], ALU.mult))
                ncv.tensor_scalar(beyond[:, :], wabs[:, 2:3], SAFE / (HD * SCALE), None, ALU.is_gt)\
                   .then_inc(beyond_ready, 1)
                ncv.tensor_copy(ident_b[:, :], ident)
                link(ncv.tensor_scalar(xnT[:, 0:P], const[:, C_MIN:C_MIN + P], 0.0, MASKED, ALU.is_gt, ALU.mult))
                link(ncv.tensor_scalar(xnT[:, P:2 * P], ident, MASKED, None, ALU.mult))
                link(ncv.tensor_tensor(above_b[:, :], xnT[:, 0:P], xnT[:, P:2 * P], ALU.subtract))
                ncv.tensor_scalar(wsq[:, 0], vec[:, V_QW:V_QW + HD], SCALE, None, ALU.mult)
                link(ncv.tensor_copy(wsq[:, 1], vec[:, V_KW:V_KW + HD]))
                cos = const[:, C_COS:C_COS + TT * HD].rearrange("p (t d) -> p t d", t=TT)
                sin = const[:, C_SIN:C_SIN + TT * HD].rearrange("p (t d) -> p t d", t=TT)
                half = HD // 2
                for qk in range(2):
                    w = wsq[:, qk, :].unsqueeze(1)
                    ncv.tensor_tensor(cwt[:, :, qk, :], cos, w.broadcast_to([P, TT, HD]), ALU.mult)
                    ncv.tensor_tensor(swt[:, :, qk, 0:half], sin[:, :, 0:half],
                                      w[:, :, half:HD].broadcast_to([P, TT, half]), ALU.mult)
                    ins = ncv.tensor_tensor(swt[:, :, qk, half:HD], sin[:, :, half:HD],
                                            w[:, :, 0:half].broadcast_to([P, TT, half]), ALU.mult)
                ins.then_inc(rope_ready, 1)

            def carry():
                ncv.memset(gap[:, :], 0.0)

            def stats(src, st, m, stat_sem, mv_sem, i):
                for t in range(TT):
                    ins = ncv.bn_stats(st[:, t, :], src[:, t, :])
                ins.then_inc(stat_sem, 1)
                dve.wait_ge(stat_sem, i + 1)
                carry()
                for t in range(TT):
                    ins = ncv.bn_aggr(m[:, t, :], st[:, t, :])
                ins.then_inc(mv_sem, 1)

            def refine(v_in, scale, eps, r, buf, nw, i):
                ncv.tensor_scalar(buf[:, 2, :], v_in, scale, eps, ALU.mult, ALU.add)
                ncv.tensor_tensor(buf[:, 3, :], r, r, ALU.mult).then_inc(nw, 1)
                dve.wait_ge(nw, 3 * i + 1)
                ncv.scalar_tensor_tensor(buf[:, 2, :], buf[:, 2, :], -0.5, buf[:, 3, :], ALU.mult, ALU.mult)\
                   .then_inc(nw, 1)
                dve.wait_ge(nw, 3 * i + 2)
                return ncv.scalar_tensor_tensor(buf[:, 4, :], buf[:, 2, :], 1.5, r, ALU.add, ALU.mult)\
                    .then_inc(nw, 1)

            def norm1_stats(i):
                if isinstance(i, int) and i < 2:
                    dve.wait_ge((x0_in, x1_in)[i], 16)
                else:
                    dve.wait_ge(xr_in, 16 * (B - 2))
                stats(xs[:, i], st6, mv, stat1, mv1, i)

            def norm1(i):
                dve.wait_ge(r01, i + 1)
                refine(mv[:, :, 1], 1.0, EPS_LN, lnr[:, 1, :], lnr, nw1, i)
                dve.wait_ge(nw1, 3 * i + 3)
                if later(i, 1):
                    dve.wait_ge(t1_done, i)
                for t in range(TT):
                    ins = ncv.tensor_scalar(xn[:, t, :], xs[:, i, t, :], mv[:, t, 0:1], lnr[:, 4, t:t + 1],
                                            ALU.subtract, ALU.mult)
                ins.then_inc(xn_ready, 1)

            def copy_norm(i):
                dve.wait_ge(t1_done, i + 1)
                if later(i, 1):
                    dve.wait_ge(z_done, i * TT)
                ncv.tensor_copy(xnT[:, :], psA[:, :]).then_inc(xnT_done, 1)

            def head_sums(i):
                dve.wait_ge(sq_done, i + 1)
                if later(i, 1):
                    dve.wait_ge(nwq, 3 * i)
                ncv.tensor_reduce(rr[:, 0, :], sq[:, :, :].rearrange("p t (g d) -> p (t g) d", d=HD),
                                  axis=AX.X, op=ALU.add).then_inc(ss_done, 1)

            def head_norm(i):
                dve.wait_ge(rq0, i + 1)
                if later(i, 1):
                    dve.wait_ge(zn_done, i)
                refine(rr[:, 0, :], 1.0 / HD, EPS_RMS, rr[:, 1, :], rr, nwq, i)

            def split(i, qk):
                dve.wait_ge(kt_done, 2 * i + (qk + 1))
                if qk == 0 and later(i, 1):
                    dve.wait_ge(scr_done, 12 * 16 * i)
                    dve.wait_ge(parts_done, 2 * i)
                ncv.tensor_copy(parts[:, qk, 0, :], psA[:, :]).then_inc(p1_done, 1)
                dve.wait_ge(p1_done, 2 * i + (qk + 1))
                ncv.tensor_tensor(rest[:, qk, :], psA[:, :], parts[:, qk, 0, :], ALU.subtract).then_inc(rest_done, 1)
                dve.wait_ge(rest_done, 2 * i + (qk + 1))
                ncv.tensor_copy(parts[:, qk, 1, :], rest[:, qk, :]).then_inc(p2_done, 1)

            def maxima(b, j):
                n = b * NQ + j
                for e in range(4 * TT):
                    c, qb = e // TT, e % TT
                    dve.wait_ge(smax_ready, n * (4 * TT) + (e + 1))
                    if e == 0 and later(n, 1):
                        dve.wait_ge(nmax_ready, n)
                    ncv.tensor_reduce(nmax[:, 0, qb * 4 + c:qb * 4 + c + 1],
                                      psS[:, j % 2, (e % 2) * 512:(e % 2) * 512 + (qb + 1) * P],
                                      axis=AX.X, op=ALU.max, negate=True).then_inc(smax_read, 1)
                dve.wait_ge(smax_read, (n + 1) * (4 * TT))
                if later(n, 1):
                    dve.wait_ge(shift_ps, n)
                for r in range(NP):
                    if r < NP - 1:
                        ncv.tensor_copy(nmax_b[:, r, :], nmax[:, r, :]).then_inc(nmax_step, 1)
                        dve.wait_ge(nmax_step, n * 4 + (2 * r + 1))
                        ncv.tensor_copy(nparts[:, :, r], nmax_b[:, r, :])
                        dst = nmax[:, 1, :] if r == 0 else nparts[:, :, 2]
                        ins = ncv.tensor_tensor(dst, nmax[:, r, :], nmax_b[:, r, :], ALU.subtract)
                        ins.then_inc(nmax_step, 1)
                        dve.wait_ge(nmax_step, n * 4 + (2 * r + 2))
                ncv.memset(gap[:, :], 0.0).then_inc(nmax_ready, 1)
                dve.wait_ge(shift_ps, n + 1)
                if later(n, 1):
                    dve.wait_ge(shift_in, n * 64)
                ncv.tensor_copy(shift[:, :], psS[0:4 * NP, j % 2, 0:512]).then_inc(shift_ready, 1)

            def causal(b, j, s):
                g = b * (NQ * SLOTS) + (j * SLOTS + s)
                dve.wait_ge(exp_done, g + 1)
                w = pt[:, j % 2, s * SW:(s + 1) * SW]
                lim = const[:, C_MIN:C_MIN + P]
                if s == 2:
                    v = w.rearrange("p (a q) -> p a q", a=4)[:, :, 0:P]
                    m = lim.unsqueeze(1).broadcast_to([P, 4, P])
                    ncv.tensor_tensor(v, v, m, ALU.min).then_inc(mask_done, 1)
                    return
                v = w.rearrange("p (a q) -> p a q", a=2)
                m = lim.unsqueeze(1).broadcast_to([P, 2, P])
                ins = ncv.tensor_tensor(v[:, :, 0:P], v[:, :, 0:P], m, ALU.min)
                if s % 3 == 1:
                    ins = ncv.tensor_tensor(v[:, :, 384:512], v[:, :, 384:512], m, ALU.min)
                ins.then_inc(mask_done, 1)

            def copy_quad(b, j):
                n = b * NQ + j
                dve.wait_ge(pv_done, n + 1)
                if later(n, 2):
                    dve.wait_ge(ot_done, n - 1)
                ncv.tensor_copy(oT[:, j % 2, :], psO[:, j % 2, :]).then_inc(o_copied, 1)

            def normalise(b, j):
                n = b * NQ + j
                dve.wait_ge(ot_done, n + 1)
                o = psC[:, :].rearrange("p (t c w) -> p t c w", t=TT, w=VW)
                ncv.reciprocal(rec[:, :, :], o[:, :, :, HD]).then_inc(rec_done, 1)
                dve.wait_ge(rec_done, n + 1)
                if j == 0 and later(b, 1):
                    dve.wait_ge(op_done, b)
                ncv.tensor_tensor(on[:, :, 32 * j:32 * j + 32].rearrange("p t (c d) -> p t c d", d=HD),
                                  o[:, :, :, 0:HD], rec[:, :, :].unsqueeze(3).broadcast_to([P, TT, 4, HD]),
                                  ALU.mult).then_inc(on_done, 1)

            def residual(i):
                dve.wait_ge(pr_done, i + 1)
                ncv.tensor_tensor(xs[:, i], psC[:, :].rearrange("p (t d) -> p t d", t=TT), xs[:, i], ALU.add)\
                   .then_inc(x1_done, 1)
                dve.wait_ge(x1_done, i + 1)
                carry()
                stats(xs[:, i], st6b, mvb, stat2, mv2, i)

            def norm2(i):
                dve.wait_ge(r02, i + 1)
                refine(mvb[:, :, 1], 1.0, EPS_LN, lnrb[:, 1, :], lnrb, nw2, i)
                dve.wait_ge(nw2, 3 * i + 3)
                if later(i, 1):
                    dve.wait_ge(xt_done, i)
                    dve.wait_ge(xf_stored, i)
                for t in range(TT):
                    ins = ncv.tensor_scalar(xf1[:, t, :], xs[:, i, t, :], mvb[:, t, 0:1], lnrb[:, 4, t:t + 1],
                                            ALU.subtract, ALU.mult)
                ins.then_inc(xf1_ready, 1)

            def copy_scores(i):
                dve.wait_ge(sc_done, i + 1)
                ncv.tensor_copy(sc4[:, i], psC[:, 0:TT * NSC]).then_inc(sc_copied, 1)

            sc4 = sc[:, :, :].rearrange("p (b t) n -> p b (t n)", b=B)

            def body(b, exact):
                k = place(b)
                for s in range(NQ * SLOTS):
                    j = s // SLOTS
                    jj = (j + 1) % NQ
                    if exact and s % SLOTS == 0:
                        if j < NQ - 1 and k < B:
                            maxima(b, jj)
                        elif j == NQ - 1 and k < B - 1:
                            maxima(b + 1, jj)
                    if k < B - 3 and s == 0:
                        norm1_stats(b + 3)
                    if j < NQ - 1 and k < B:
                        causal(b, jj, s % SLOTS)
                    elif j == NQ - 1 and k < B - 1:
                        causal(b + 1, jj, s % SLOTS)
                    if k >= 1:
                        if s == 0:
                            copy_quad(b - 1, 3)
                        if s == 2:
                            normalise(b - 1, 3)
                        if s == 6:
                            residual(b - 1)
                        if s == 9:
                            norm2(b - 1)
                        if s == 16:
                            copy_scores(b - 1)
                    if k < B:
                        if s in (5, 10, 15):
                            copy_quad(b, s // SLOTS - 1)
                        if s == 7:
                            normalise(b, 0)
                        if s == 12:
                            normalise(b, 1)
                        if s == 18:
                            normalise(b, 2)
                    if k < B - 2:
                        if s == 14:
                            split(b + 2, 0)
                        if s == 16:
                            split(b + 2, 1)
                    if k < B - 3:
                        if s == 2:
                            norm1(b + 3)
                        if s == 4:
                            copy_norm(b + 3)
                        if s == 14:
                            head_sums(b + 3)
                        if s == 16:
                            head_norm(b + 3)

            prepare()
            for i in range(3):
                norm1_stats(i)
                norm1(i)
                copy_norm(i)
                head_sums(i)
                head_norm(i)
                if i >= 1:
                    split(i - 1, 0)
                    split(i - 1, 1)

            def main(exact):
                if exact:
                    maxima(0, 0)
                for s in range(SLOTS):
                    causal(0, 0, s)
                over_batches(dve, lambda b: body(b, exact))

            either(dve, main)

            n = [0]

            def link(ins):
                n[0] += 1
                ins.then_inc(tail_dve, 1)
                dve.wait_ge(tail_dve, n[0])

            def first_of_largest(src, dst):
                g3, e3, p3, d3 = (a.rearrange("p (t c) -> p t c", c=NCL) for a in (src, eq, pref, dst))
                link(ncv.tensor_reduce(top[:, :], g3, axis=AX.X, op=ALU.max))
                link(ncv.tensor_tensor(e3, g3, top[:, :].unsqueeze(2).broadcast_to([P, NT, NCL]), ALU.is_ge))
                link(ncv.tensor_tensor(p3, e3, const[:, C_PREF:C_PREF + 8].unsqueeze(1).broadcast_to([P, NT, NCL]),
                                       ALU.mult))
                link(ncv.tensor_reduce(top[:, :], p3, axis=AX.X, op=ALU.max))
                link(ncv.tensor_tensor(d3, p3, top[:, :].unsqueeze(2).broadcast_to([P, NT, NCL]), ALU.is_equal))

            def calibrate(r):
                dve.wait_ge(ex_done, r + 1)
                link(ncv.tensor_scalar(ex, ex, 1.0, None, ALU.add))
                link(ncv.reciprocal(gate, ex))
                ncv.tensor_scalar(u7, gate, float(KNOTS - 1), None, ALU.mult).then_inc(u7_ready, 1)
                dve.wait_ge(u7_ready, r + 1)
                link(ncv.tensor_tensor(step, u7.unsqueeze(2).broadcast_to([P, NG, KNOTS]),
                                       const[:, C_STEP:C_STEP + KNOTS].unsqueeze(1).broadcast_to([P, NG, KNOTS]),
                                       ALU.is_ge))
                link(ncv.tensor_tensor(cell, step[:, :, 0:KNOTS - 1], step[:, :, 1:KNOTS], ALU.subtract))
                dve.wait_ge(line_ready, r + 1)
                link(ncv.tensor_tensor(line, line,
                                       vec[:, V_KNOT:V_KNOT + KNOTS - 1].unsqueeze(1).broadcast_to([P, NG, KNOTS - 1]),
                                       ALU.add))
                link(ncv.tensor_tensor(cell, cell, line, ALU.mult))
                link(ncv.tensor_reduce(gate, cell, axis=AX.X, op=ALU.add))

            calibrate(0)
            first_of_largest(gate, hot_c)
            s4 = step[:, :, :].rearrange("p (t a) c -> p t a c", t=NT)
            c3 = hot_c.rearrange("p (t c) -> p t c", c=NCL)
            t3 = hot_t.rearrange("p (t c) -> p t c", c=NCL)
            link(ncv.tensor_tensor(s4, sc[:, :, NCL:NCL + NTILE].rearrange("p t (c a) -> p t a c", c=NCL),
                                   c3.unsqueeze(2).broadcast_to([P, NT, TPC, NCL]), ALU.mult))
            ncv.tensor_reduce(sel.rearrange("p (t a) -> p t a", a=TPC), s4, axis=AX.X, op=ALU.add)\
               .then_inc(sel_ready, 1)
            dve.wait_ge(prod_ready, 2)
            ncv.tensor_reduce(comp[:, 0, :], prod0, axis=AX.X, op=ALU.add)
            link(ncv.tensor_reduce(comp[:, 1, :], prod1, axis=AX.X, op=ALU.add))
            link(ncv.tensor_tensor(comp[:, :, :], comp[:, :, :],
                                   vec[:, V_B2:V_B2 + 2].unsqueeze(2).broadcast_to([P, 2, NT]), ALU.add))
            cpre = ncv.tensor_copy(mag[:, :], comp[:, 0, :])
            cpre.then_inc(cpre_ready, 1)
            calibrate(1)
            first_of_largest(gate, hot_t)
            ncv.tensor_tensor(hot[:, :, :].rearrange("p t (c a) -> p t c a", c=NCL),
                              c3.unsqueeze(3).broadcast_to([P, NT, NCL, TPC]),
                              t3.unsqueeze(2).broadcast_to([P, NT, NCL, TPC]), ALU.mult).then_inc(hot_ready, 1)
            dve.wait_ge(tanh_done, 1)
            dve.wait_ge(got_copied, NT // 2)
            w1 = got[:, :, 0:2 * GRID].rearrange("p t (a n) -> p a t n", a=2)
            for a in range(2):
                ins = ncv.tensor_tensor(m01[:, a], w1[:, a], comp[:, a, :].unsqueeze(2).broadcast_to([P, NT, GRID]),
                                        ALU.mult)
            link(ins)
            link(ncv.tensor_tensor(m01[:, 0], m01[:, 0], m01[:, 1], ALU.add))
            link(ncv.tensor_tensor(m01[:, 0], m01[:, 0], got[:, :, 2 * GRID:3 * GRID], ALU.add))
            link(ncv.tensor_scalar(m01[:, 0], m01[:, 0], 0.0, None, ALU.max))
            link(ncv.tensor_tensor(m01[:, 1], m01[:, 0], got[:, :, 3 * GRID:4 * GRID], ALU.mult))
            link(ncv.tensor_reduce(mag[:, :], m01[:, 1], axis=AX.X, op=ALU.add))
            link(ncv.tensor_tensor(mag[:, :], mag[:, :], got[:, :, 4 * GRID], ALU.add))
            link(ncv.tensor_scalar(mag[:, :], mag[:, :], vec[:, V_OS:V_OS + 1], None, ALU.mult))

            def spline_out(k):
                c = slice(k * G, (k + 1) * G)
                direction = got[:, c, 4 * GRID + 1:TABW]
                link(ncv.tensor_tensor(direction, direction, mag[:, c].unsqueeze(2).broadcast_to([P, G, D]), ALU.mult))
                link(ncv.tensor_tensor(xff[:, c, :], xff[:, c, :], direction, ALU.add))
                for t in range(k * G, (k + 1) * G):
                    ins = ncv.bn_stats(st6c[:, t, :], xff[:, t, :])
                ins.then_inc(stat3, 1)
                dve.wait_ge(stat3, k + 1)
                for t in range(k * G, (k + 1) * G):
                    ins = ncv.bn_aggr(mvc[:, t, :], st6c[:, t, :])
                ins.then_inc(mv3, 1)

            def norm3(k):
                c = slice(k * G, (k + 1) * G)
                dve.wait_ge(r03, k + 1)
                refine(mvc[:, c, 1], 1.0, EPS_LN, lnrc[:, 1, c], lnrc[:, :, c], nw3, k)
                dve.wait_ge(nw3, 3 * k + 3)
                for t in range(k * G, (k + 1) * G):
                    ins = ncv.tensor_scalar(xff[:, t, :], xff[:, t, :], mvc[:, t, 0:1], lnrc[:, 4, t:t + 1],
                                            ALU.subtract, ALU.mult)
                ins.then_inc(yn_ready, 1)

            def residual_out(k):
                c = slice(k * G, (k + 1) * G)
                dve.wait_ge(ygb_ready, k + 1)
                ncv.tensor_tensor(xsf[:, c, :], xsf[:, c, :], xff[:, c, :], ALU.add).then_inc(out_ready, 1)

            for k in range(NT // G):
                spline_out(k)
                norm3(k)
            for k in range(NT // G):
                residual_out(k)

        @block.gpsimd
        def _(pool):
            ncg = nc.gpsimd
            one = const[:, C_J + 1:C_J + 2].unsqueeze(1)
            ncg.memset(stk[:, :, :, :], 1.0)
            ncg.memset(stq[:, :, :, :], 0.0)
            ncg.memset(vaug[:, :, :, :], 0.0).then_inc(zeros_ready, 1)
            pool.wait_ge(const_in, 16)
            pool.wait_ge(zeros_ready, 1)
            ncg.memset(vaug[:, :, :, HD:HD + 1], 1.0).then_inc(zeros_ready, 1)
            pool.wait_ge(zeros_ready, 2)

            def squares(i):
                pool.wait_ge(z_copied, (i + 1) * TT)
                if later(i, 1):
                    pool.wait_ge(ss_done, i)
                ncg.tensor_tensor(sq[:, :, :], zqk[:, :, :], zqk[:, :, :], ALU.mult).then_inc(sq_done, 1)

            def rotate(i):
                pool.wait_ge(nwq, 3 * i + 3)
                if later(i, 1):
                    pool.wait_ge(qkr_done, i)
                groups = TT * 2 * H
                ncg.tensor_tensor(zn[:, :, :].rearrange("p t (g d) -> p (t g) d", d=HD),
                                  zqk[:, :, :].rearrange("p t (g d) -> p (t g) d", d=HD),
                                  rr[:, 4, :].unsqueeze(2).broadcast_to([P, groups, HD]), ALU.mult)\
                   .then_inc(zn_done, 1)
                pool.wait_ge(zn_done, i + 1)
                half = HD // 2
                z4 = zn[:, :, :].rearrange("p t (k h d) -> p (t k) h d", k=2, h=H)
                b4 = rb[:, :, :].rearrange("p t (k h d) -> p (t k) h d", k=2, h=H)
                q4 = qkr[:, :, :, :].rearrange("p t k (h d) -> p (t k) h d", h=H)
                cw = cwt[:, :, :, :].rearrange("p t k d -> p (t k) d").unsqueeze(2)
                sw = swt[:, :, :, :].rearrange("p t k d -> p (t k) d").unsqueeze(2)
                for a, c in ((0, half), (half, 0)):
                    ncg.tensor_tensor(b4[:, :, :, a:a + half], z4[:, :, :, c:c + half],
                                      sw[:, :, :, a:a + half].broadcast_to([P, 2 * TT, H, half]), ALU.mult)
                if later(i, 1):
                    pool.wait_ge(kt_done, 2 * i)
                ncg.tensor_tensor(q4, z4, cw.broadcast_to([P, 2 * TT, H, HD]), ALU.mult).then_inc(rope_a, 1)
                pool.wait_ge(rope_a, i + 1)
                ncg.tensor_tensor(q4, q4, b4, ALU.add).then_inc(qkr_done, 1)

            def split(i, qk):
                n = 2 * i + (qk + 1)
                pool.wait_ge(p2_done, n)
                ncg.tensor_tensor(parts[:, qk, 2, :], rest[:, qk, :], parts[:, qk, 1, :], ALU.subtract)\
                   .then_inc(parts_done, 1)

            def values(b, j):
                if later(b, 1):
                    pool.wait_ge(pv_done, b * NQ + (j - (NQ - 1)))
                else:
                    pool.wait_ge(z_copied, TT)
                v = vtok[:, b, :, 32 * j:32 * j + 32].rearrange("p t (c d) -> p t c d", d=HD)
                ncg.tensor_tensor(vaug[:, :, 4 * j:4 * j + 4, 0:HD], v,
                                  one.unsqueeze(1).broadcast_to([P, TT, 4, HD]), ALU.mult)\
                   .then_inc(v_ready, 1)

            def store_xf(i):
                pool.wait_ge(xf1_ready, i + 1)
                ncg.tensor_tensor(xf[:, i], xf1[:, :, :], one.broadcast_to([P, TT, D]), ALU.mult).then_inc(xf_stored, 1)

            def body(b):
                k = place(b)
                if 1 <= k:
                    store_xf(b - 1)
                if k < B - 1:
                    values(b + 1, 0)
                    values(b + 1, 1)
                if k < B - 3:
                    squares(b + 3)
                if k < B - 1:
                    values(b + 1, 2)
                if k < B - 2:
                    split(b + 2, 0)
                    split(b + 2, 1)
                if k < B - 3:
                    rotate(b + 3)
                if k < B - 1:
                    values(b + 1, 3)

            pool.wait_ge(rope_ready, 1)
            for i in range(3):
                squares(i)
                rotate(i)
                if i >= 1:
                    split(i - 1, 0)
                    split(i - 1, 1)
                if i == 1:
                    for j in range(NQ):
                        values(0, j)
            over_batches(pool, body)

            pool.wait_ge(sc_copied, B)
            ncg.tensor_tensor(hid, sc[:, :, NCL + NTILE:NSC],
                              vec[:, V_B1:V_B1 + COMP].unsqueeze(1).broadcast_to([P, NT, COMP]), ALU.add)\
               .then_inc(hid_ready, 1)

            def lines(r):
                pool.wait_ge(u7_ready, r + 1)
                shape = [P, NG, KNOTS - 1]
                ncg.tensor_tensor(line, u7.unsqueeze(2).broadcast_to(shape),
                                  const[:, C_J:C_J + KNOTS - 1].unsqueeze(1).broadcast_to(shape), ALU.subtract)\
                   .then_inc(tail_pool, 1)
                pool.wait_ge(tail_pool, r + 1)
                ncg.tensor_tensor(line, line, dk[:, :].unsqueeze(1).broadcast_to(shape), ALU.mult)\
                   .then_inc(line_ready, 1)

            lines(0)
            pool.wait_ge(gelu_done, 1)
            for a, prod in enumerate((prod0, prod1)):
                w2 = vec[:, V_W2 + a * COMP:V_W2 + (a + 1) * COMP]
                ncg.tensor_tensor(prod, hid, w2.unsqueeze(1).broadcast_to([P, NT, COMP]), ALU.mult)\
                   .then_inc(prod_ready, 1)
            lines(1)
            for k in range(NT // G):
                c = slice(k * G, (k + 1) * G)
                pool.wait_ge(yn_ready, k + 1)
                ncg.tensor_tensor(xff[:, c, :], xff[:, c, :],
                                  vec[:, V_GAM:V_GAM + D].unsqueeze(1).broadcast_to([P, G, D]), ALU.mult)\
                   .then_inc(tail_pool, 1)
                pool.wait_ge(tail_pool, 3 + k)
                ncg.tensor_tensor(xff[:, c, :], xff[:, c, :],
                                  vec[:, V_BET:V_BET + D].unsqueeze(1).broadcast_to([P, G, D]), ALU.add)\
                   .then_inc(ygb_ready, 1)


def shape_constants():
    c = np.zeros((P, NCONST), np.float32)
    p = np.arange(P)
    c[:, C_ID:C_ID + P] = np.eye(P)
    c[:, C_MIN:C_MIN + P] = np.where(p[None, :] >= p[:, None], BIG, 0.0)
    freqs = np.float32(THETA) ** (-np.arange(0, HD, 2, dtype=np.float32) / HD)
    ang = np.arange(T, dtype=np.float32)[:, None] * freqs[None, :]
    cos, sin = np.cos(ang).reshape(TT, P, HD // 2), np.sin(ang).reshape(TT, P, HD // 2)
    both = np.concatenate([cos, cos], -1).transpose(1, 0, 2)
    signed = np.concatenate([-sin, sin], -1).transpose(1, 0, 2)
    c[:, C_COS:C_COS + TT * HD] = both.reshape(P, -1)
    c[:, C_SIN:C_SIN + TT * HD] = signed.reshape(P, -1)
    c[:, C_STEP:C_STEP + KNOTS] = [-1, 1, 2, 3, 4, 5, 6, BIG]
    c[:, C_J:C_J + KNOTS] = np.arange(KNOTS)
    c[:, C_PREF:C_PREF + 8] = np.arange(8, 0, -1)
    c[:, C_EPS] = EPS_LN
    c[:, C_EPS + 1] = EPS_RMS
    return c


def kernel(**inputs):
    import concourse.bacc as bacc
    from concourse.bass_utils import run_bass_kernel_spmd

    a = {k: np.asarray(v) for k, v in inputs.items()}
    f = lambda name: a["L0_ffn_" + name]
    table = np.concatenate([f("spline_w1").reshape(NTILE, 2 * GRID), f("spline_b1"),
                            f("spline_w2").reshape(NTILE, GRID), f("spline_b2"), f("directions")], axis=1)
    vector = np.concatenate([a["L0_attn_q_norm_w"], a["L0_attn_k_norm_w"], f("knot_values"), f("temperature"),
                             f("compress_b1"), f("compress_w2").T.reshape(-1), f("compress_b2"),
                             f("norm_gamma"), f("norm_beta"), f("output_scale")])[None]
    arrays = {
        "x": a["L0_attn_x"],
        "w_qkv_t": a["L0_attn_w_qkv"].T,
        "w_proj_t": a["L0_attn_w_proj"].T,
        "signatures_t": f("signatures_raw").T,
        "compress_w1": f("compress_w1"),
        "table": table,
        "vector": vector,
        "shape_constants": shape_constants(),
    }
    arrays = {k: np.ascontiguousarray(v) for k, v in arrays.items()}
    nc = bacc.Bacc("TRN2", target_bir_lowering=False, num_devices=1)
    args = [nc.dram_tensor(k, v.shape, mybir.dt.from_np(v.dtype), kind="ExternalInput").ap()
            for k, v in arrays.items()]
    out = nc.dram_tensor("out", (B, T, D), F32, kind="ExternalOutput").ap()
    build(nc, *args, out)
    r = run_bass_kernel_spmd(nc, [arrays], core_ids=[0])
    return r.results[0]["out"]
```

```python
from contextlib import ExitStack

import numpy as np

import concourse.bass as bass
from concourse import mybir

F32 = mybir.dt.float32
BF16 = mybir.dt.bfloat16
ALU = mybir.AluOpType
ACT = mybir.ActivationFunctionType
AX = mybir.AxisListType

P = 128
B, T, D = 8, 512, 128
H, HD = 16, 8
TT = T // P
NT = B * TT
NQ = H // 4
NP = 3
ROWS = 6 * HD
SROWS = ROWS + NP
Q_PARTS = (0, 0, 0, 1, 1, 2)
K_PARTS = (0, 1, 2, 0, 1, 0)
SLOTS = 5
SW = 1024
VW = 32
NTILE, TPC, NCL = 64, 8, 8
GRID, COMP, KNOTS = 16, 32, 8
NSC = NCL + NTILE + COMP
TABW = 4 * GRID + 1 + D
EPS_LN, EPS_RMS = 1e-5, 1e-6
SCALE = HD ** -0.5
THETA = 32.0
BIG = 3.0e38
MASKED = -1.0e30
SAFE = 70.0
G = 16

C_ID = 0
C_MASK = C_ID + P
C_COS = C_MASK + P
C_SIN = C_COS + TT * HD
C_STEP = C_SIN + TT * HD
C_J = C_STEP + KNOTS
C_PREF = C_J + KNOTS
C_EPS = C_PREF + 8
NCONST = C_EPS + 2

V_QW = 0
V_KW = V_QW + HD
V_KNOT = V_KW + HD
V_TEMP = V_KNOT + KNOTS
V_B1 = V_TEMP + 1
V_W2 = V_B1 + COMP
V_B2 = V_W2 + 2 * COMP
V_GAM = V_B2 + 2
V_BET = V_GAM + D
V_OS = V_BET + D
NVEC = V_OS + 1


def unit_of(kb, c):
    hh, gg = c // 2, c % 2
    if kb == 0:
        return 3 * gg, 512 * hh
    if kb == 2:
        return 2, 512 * hh + 256 * gg
    return 3 * gg + 1, 512 * hh + (384 if kb == 3 else 0)


def build(nc, x_d, wqkv_d, wproj_d, sig_d, cw1_d, tab_d, vec_d, const_d, out_d):
    with ExitStack() as ctx:
        def sb(name, shape, dt=F32):
            return ctx.enter_context(nc.sbuf_tensor(name, shape, dt))

        def psum(name, shape):
            return ctx.enter_context(nc.psum_tensor(name, shape, F32))

        def sem(name):
            return ctx.enter_context(nc.semaphore(name))

        xs = sb("xs", [P, B, TT, D])
        xf = sb("xf", [P, B, TT, D])
        sc = sb("sc", [P, NT, NSC])
        vtok = sb("vtok", [P, B, TT, D])
        const = sb("const", [P, NCONST])
        vec = sb("vec", [P, NVEC])
        wqkv = sb("wqkv", [P, 3 * D])
        wproj = sb("wproj", [P, D])
        wsc = sb("wsc", [P, NSC])
        sig = sb("sig", [P, NTILE])
        sg = sb("sg", [P, 3, NTILE])
        csum = sb("csum", [P, 2, NCL])
        cwt = sb("cwt", [P, TT, 2, HD])
        swt = sb("swt", [P, TT, 2, HD])
        wsq = sb("wsq", [P, 2, HD])
        tab = sb("tab", [NTILE, TABW])
        st6 = sb("st6", [P, TT, 6])
        mv = sb("mv", [P, TT, 2])
        lnr = sb("lnr", [P, 6, TT])
        xn = sb("xn", [P, TT, D])
        xnT = sb("xnT", [P, T])
        zqk = sb("zqk", [P, TT, 2 * D])
        sq = sb("sq", [P, TT, 2 * D])
        rr = sb("rr", [P, 6, TT * 2 * H])
        zn = sb("zn", [P, TT, 2 * D])
        rb = sb("rb", [P, TT, 2 * D])
        qkr = sb("qkr", [P, TT, 2, D])
        parts = sb("parts", [P, 2, NP, T], BF16)
        rest = sb("rest", [P, 2, T])
        stq = sb("stq", [P, NQ, 2, T], BF16)
        stk = sb("stk", [P, NQ, 2, T], BF16)
        vaug = sb("vaug", [P, TT, H, VW])
        pt = sb("pt", [P, 2, SLOTS * SW])
        oT = sb("oT", [P, 2, T])
        rec = sb("rec", [P, TT, 4])
        on = sb("on", [P, TT, D])
        onT = sb("onT", [P, T])
        st6b = sb("st6b", [P, TT, 6])
        mvb = sb("mvb", [P, TT, 2])
        lnrb = sb("lnrb", [P, 6, TT])
        xf1 = sb("xf1", [P, TT, D])
        xfT = sb("xfT", [P, T])

        gap = sb("gap", [P, 1])
        ident_b = sb("ident_b", [P, P], BF16)
        mask_b = sb("mask_b", [P, P], BF16)
        wabs = sb("wabs", [P, 4])
        beyond = sb("beyond", [P, 1], mybir.dt.int32)
        nmax = sb("nmax", [P, 2, TT * 4])
        nmax_b = sb("nmax_b", [P, 2, TT * 4], BF16)
        nparts = sb("nparts", [P, TT * 4, NP])
        shift = sb("shift", [4 * NP, T], BF16)
        nrt = sb("nrt", [P, 2])
        dk = sb("dk", [P, KNOTS - 1])
        top = sb("top", [P, NT])
        comp = sb("comp", [P, 2, NT])
        mag = sb("mag", [P, NT])
        st6c = sb("st6c", [P, NT, 6])
        mvc = sb("mvc", [P, NT, 2])
        lnrc = sb("lnrc", [P, 6, NT])

        psS = psum("psS", [P, 2, SW])
        psO = psum("psO", [P, 2, 512])
        psA = psum("psA", [P, 512])
        psC = psum("psC", [P, 512])

        scratch = nc.dram_tensor("stacks", [B, 2, H, 6, HD, T], BF16, kind="Internal").ap()

        (const_in, w_in, x0_in, x1_in, xr_in, out_done, scr_done,
         wsc_ready, rope_ready, zeros_ready,
         stat1, mv1, ln1, r01, nw1, xn_ready, t1_done, xnT_done, z_done, z_copied, sq_done,
         ss_done, lnq, rq0, nwq, rq_done, zn_done, rope_a, rope_b, qkr_done,
         kt_done, p1_done, rest_done, p2_done, parts_done,
         s_ready, exp_done, masks_ready, v_ready, pv_done, o_copied, ot_done, rec_done, on_done,
         op_done, onT_done, pr_done, x1_done,
         stat2, mv2, ln2, r02, nw2, xf1_ready, xf_stored, xt_done, xfT_done, sc_done, sc_copied,
         beyond_ready, smax_ready, smax_read, nmax_step, nmax_ready, shift_ps, shift_ready, shift_in,
         prep_dve, tail_dve, tail_pool, ex_done, u7_ready, line_ready, sel_ready, hot_ready, hot_done,
         hotT_ready, got_done, got_copied, hid_ready, gelu_done, prod_ready, cpre_ready, tanh_done,
         stat3, mv3, ln3, r03, nw3, yn_ready, ygb_ready, out_ready) = [sem(n) for n in (
            "const_in w_in x0_in x1_in xr_in out_done scr_done "
            "wsc_ready rope_ready zeros_ready "
            "stat1 mv1 ln1 r01 nw1 xn_ready t1_done xnT_done z_done z_copied sq_done "
            "ss_done lnq rq0 nwq rq_done zn_done rope_a rope_b qkr_done "
            "kt_done p1_done rest_done p2_done parts_done "
            "s_ready exp_done masks_ready v_ready pv_done o_copied ot_done rec_done on_done "
            "op_done onT_done pr_done x1_done "
            "stat2 mv2 ln2 r02 nw2 xf1_ready xf_stored xt_done xfT_done sc_done sc_copied "
            "beyond_ready smax_ready smax_read nmax_step nmax_ready shift_ps shift_ready shift_in "
            "prep_dve tail_dve tail_pool ex_done u7_ready line_ready sel_ready hot_ready hot_done "
            "hotT_ready got_done got_copied hid_ready gelu_done prod_ready cpre_ready tanh_done "
            "stat3 mv3 ln3 r03 nw3 yn_ready ygb_ready out_ready").split()]
        stack_in = [sem(f"stack_in{j}") for j in range(NQ)]

        NG = NT * NCL
        ptf = pt[:, :, :].rearrange("p a n -> p (a n)")
        got = ptf[:, 0:NT * TABW].rearrange("p (t n) -> p t n", n=TABW)
        step = ptf[:, 0:NG * KNOTS].rearrange("p (g k) -> p g k", k=KNOTS)
        cell = ptf[:, 2048:2048 + NG * (KNOTS - 1)].rearrange("p (g k) -> p g k", k=KNOTS - 1)
        line = ptf[:, 4096:4096 + NG * (KNOTS - 1)].rearrange("p (g k) -> p g k", k=KNOTS - 1)
        hot = ptf[:, 8192:8192 + NT * NTILE].rearrange("p (t n) -> p t n", n=NTILE)
        hotT = vtok[:, :, :, :].rearrange("p b t d -> p (b t d)")[0:NTILE, :]
        zf = zqk[:, :, :].rearrange("p t d -> p (t d)")
        sf = sq[:, :, :].rearrange("p t d -> p (t d)")
        ex, u7, gate, eq = (zf[:, n * NG:(n + 1) * NG] for n in range(4))
        pref, hot_c, sel, hot_t = (sf[:, n * NG:(n + 1) * NG] for n in range(4))
        hid = zn[:, :, :].rearrange("p t (a n) -> p (t a) n", n=COMP)
        prod0 = rb[:, :, :].rearrange("p t (a n) -> p (t a) n", n=COMP)
        prod1 = qkr[:, :, :, :].rearrange("p t k (a n) -> p (t k a) n", n=COMP)
        m01 = rest[:, :, :].rearrange("p a (t n) -> p a t n", n=GRID)
        xsf = xs[:, :, :, :].rearrange("p b t d -> p (b t) d")
        xff = xf[:, :, :, :].rearrange("p b t d -> p (b t) d")
        z4 = zn[:, :, :].rearrange("p t (k h d) -> p (t k) h d", k=2, h=H)
        b4 = rb[:, :, :].rearrange("p t (k h d) -> p (t k) h d", k=2, h=H)
        q4 = qkr[:, :, :, :].rearrange("p t k (h d) -> p (t k) h d", h=H)
        cw = cwt[:, :, :, :].rearrange("p t k d -> p (t k) d").unsqueeze(2)
        sw = swt[:, :, :, :].rearrange("p t k d -> p (t k) d").unsqueeze(2)
        ident = const[:, C_ID:C_ID + P]
        eps_ln = const[:, C_EPS:C_EPS + 1]
        eps_rms = const[:, C_EPS + 1:C_EPS + 2]
        block = ctx.enter_context(nc.Block())

        def over_batches(eng, body):
            body(0)
            with eng.Fori(1, B - 3) as b:
                body(b)
            for b in range(B - 3, B + 1):
                body(b)

        def either(eng, main):
            eng.wait_ge(beyond_ready, 1)
            far = eng.value_load(beyond[0:1, 0:1], min_val=0, max_val=1)
            with eng.If(far > 0):
                main(True)
            with eng.Else():
                main(False)

        def place(b):
            return b if isinstance(b, int) else 1

        def later(i, n):
            return i >= n if isinstance(i, int) else True

        @block.sync
        def _(sp):
            sp.dma_start(const[:, :], const_d).then_inc(const_in, 16)
            sp.dma_start(xs[:, 0], x_d[0].rearrange("(t p) d -> p t d", p=P)).then_inc(x0_in, 16)
            sp.dma_start(vec[:, :], vec_d.broadcast_to([P, NVEC])).then_inc(w_in, 16)
            sp.dma_start(wqkv[:, :], wqkv_d).then_inc(w_in, 16)
            sp.dma_start(xs[:, 1], x_d[1].rearrange("(t p) d -> p t d", p=P)).then_inc(x1_in, 16)
            sp.dma_start(sig[:, :], sig_d).then_inc(w_in, 16)
            sp.dma_start(wproj[:, :], wproj_d).then_inc(w_in, 16)
            sp.dma_start(wsc[:, NCL + NTILE:NSC], cw1_d).then_inc(w_in, 16)
            sp.dma_start(tab[:, :], tab_d).then_inc(w_in, 16)
            for i in range(2, B):
                sp.dma_start(xs[:, i], x_d[i].rearrange("(t p) d -> p t d", p=P)).then_inc(xr_in, 16)

            def store_parts(i):
                for qk, rows in enumerate((Q_PARTS, K_PARTS)):
                    sp.wait_ge(parts_done, i * 2 + (qk + 1))
                    for r in range(6):
                        sp.dma_start(scratch[i, qk, :, r], parts[:, qk, rows[r], :]).then_inc(scr_done, 16)

            def load_stack(i, j):
                if later(i, 1):
                    sp.wait_ge(s_ready, (i - 1) * (NQ * SLOTS) + (j + 1) * SLOTS)
                for qk, st in ((0, stq), (1, stk)):
                    for hh in range(2):
                        h = 4 * j + 2 * hh
                        sp.dma_start(st[64 * hh:64 * hh + ROWS, j],
                                     scratch[i, qk, h:h + 2].rearrange("g r d t -> (r d) g t"))\
                          .then_inc(stack_in[j], 16)

            def load_stacks(i):
                sp.wait_ge(scr_done, (i + 1) * (12 * 16))
                for j in range(NQ):
                    load_stack(i, j)

            store_parts(0)
            sp.wait_ge(zeros_ready, 2)
            load_stacks(0)
            store_parts(1)

            def body(b):
                k = place(b)
                if k < B - 1:
                    load_stacks(b + 1)
                if k < B - 2:
                    store_parts(b + 2)

            over_batches(sp, body)
            for k in range(NT // G):
                sp.wait_ge(out_ready, k + 1)
                nb = G // TT
                for i in range(k * nb, (k + 1) * nb):
                    sp.dma_start(out_d[i].rearrange("(t p) d -> p t d", p=P), xs[:, i]).then_inc(out_done, 16)
            sp.wait_ge(out_done, B * 16)

        @block.tensor
        def _(pe):
            def transposes(dst, srcs):
                for t, s in enumerate(srcs):
                    ins = nc.tensor.transpose(dst[:, t * P:(t + 1) * P], s, ident)
                return ins

            def norm_transposed(i):
                pe.wait_ge(xn_ready, i + 1)
                if later(i, 2):
                    pe.wait_ge(rest_done, 2 * i)
                elif i == 1:
                    pe.wait_ge(z_copied, TT)
                transposes(psA, [xn[:, t, :] for t in range(TT)]).then_inc(t1_done, 1)

            def project(i, t):
                if t == 0:
                    pe.wait_ge(xnT_done, i + 1)
                else:
                    pe.wait_ge(z_copied, i * TT + t)
                nc.tensor.matmul(psA[:, 0:3 * D], xnT[:, t * P:(t + 1) * P], wqkv[:, :],
                                 start=True, stop=True).then_inc(z_done, 1)

            def qk_transposed(i, qk):
                if qk == 0:
                    pe.wait_ge(qkr_done, i + 1)
                    pe.wait_ge(z_copied, (i + 1 if later(i, 1) else 2) * TT)
                    if isinstance(i, int) and i == 1:
                        pe.wait_ge(rest_done, 2)
                else:
                    pe.wait_ge(rest_done, 2 * i + 1)
                transposes(psA, [qkr[:, t, qk, :] for t in range(TT)]).then_inc(kt_done, 1)

            def maxima(b, j):
                n = b * NQ + j
                pe.wait_ge(stack_in[j], (b + 1) * 64)
                if later(n, 1):
                    pe.wait_ge(exp_done, n * SLOTS - 1)
                for e in range(4 * TT):
                    c, qb = e // TT, e % TT
                    hh, gg = c // 2, c % 2
                    if later(n, 1) or e >= 2:
                        pe.wait_ge(smax_read, n * (4 * TT) + (e - 1))
                    bank = psS[:, j % 2, (e % 2) * 512:(e % 2) * 512 + 512]
                    nc.tensor.matmul(bank[:, 0:(qb + 1) * P],
                                     stq[64 * hh:64 * hh + ROWS, j, gg, qb * P:(qb + 1) * P],
                                     stk[64 * hh:64 * hh + ROWS, j, gg, 0:(qb + 1) * P], start=True, stop=False)
                    nc.tensor.matmul(bank[:, qb * P:(qb + 1) * P], mask_b[:, :], ident_b[:, :],
                                     start=False, stop=True).then_inc(smax_ready, 1)
                pe.wait_ge(nmax_ready, n + 1)
                for qb in range(TT):
                    ins = nc.tensor.transpose(psS[0:4 * NP, j % 2, qb * P:(qb + 1) * P],
                                              nparts[:, qb * 4:(qb + 1) * 4, :].rearrange("p c r -> p (c r)"), ident)
                ins.then_inc(shift_ps, 1)
                pe.wait_ge(shift_in, (n + 1) * 64)

            def scores(b, j, s):
                g = b * (NQ * SLOTS) + (j * SLOTS + s)
                if s == 0:
                    pe.wait_ge(stack_in[j], (b + 1) * 64)
                if later(g, 2):
                    pe.wait_ge(exp_done, g - 1)
                for c in (0, 2, 1, 3):
                    hh, gg = c // 2, c % 2
                    for kb in range(TT):
                        u, off = unit_of(kb, c)
                        if u != s:
                            continue
                        slot = psS[:, (j * SLOTS + s) % 2, :]
                        nc.tensor.matmul(slot[:, off:off + T - kb * P],
                                         stk[64 * hh:64 * hh + SROWS, j, gg, kb * P:(kb + 1) * P],
                                         stq[64 * hh:64 * hh + SROWS, j, gg, kb * P:T], start=True, stop=False)
                        ins = nc.tensor.matmul(slot[:, off:off + P], ident_b[:, :], mask_b[:, :],
                                               start=False, stop=True)
                ins.then_inc(s_ready, 1)

            def attend(b, j, kb):
                n = b * NQ + j
                if kb == 0:
                    pe.wait_ge(v_ready, n + 1)
                    if later(n, 2):
                        pe.wait_ge(o_copied, n - 1)
                    pe.wait_ge(exp_done, n * SLOTS + 4)
                if kb == 1:
                    pe.wait_ge(exp_done, n * SLOTS + 5)
                for c in range(4):
                    u, off = unit_of(kb, c)
                    ins = nc.tensor.matmul(psO[32 * c:32 * c + VW, j % 2, kb * P:T],
                                           vaug[:, kb, 4 * j + c, :],
                                           pt[:, j % 2, u * SW + off:u * SW + off + T - kb * P],
                                           start=(kb == 0), stop=(kb == TT - 1))
                if kb == TT - 1:
                    ins.then_inc(pv_done, 1)

            def quad_transposed(b, j, free, value):
                n = b * NQ + j
                pe.wait_ge(o_copied, n + 1)
                if free is not None:
                    pe.wait_ge(free, value)
                transposes(psC, [oT[:, j % 2, t * P:(t + 1) * P] for t in range(TT)]).then_inc(ot_done, 1)

            def heads_transposed(i):
                pe.wait_ge(on_done, (i + 1) * NQ)
                transposes(psC, [on[:, t, :] for t in range(TT)]).then_inc(op_done, 1)

            def output_projection(i):
                pe.wait_ge(onT_done, i + 1)
                for t in range(TT):
                    ins = nc.tensor.matmul(psC[:, t * D:(t + 1) * D], onT[:, t * P:(t + 1) * P], wproj[:, :],
                                           start=True, stop=True)
                ins.then_inc(pr_done, 1)

            def router_transposed(i, free, value):
                pe.wait_ge(xf1_ready, i + 1)
                pe.wait_ge(free, value)
                transposes(psC, [xf1[:, t, :] for t in range(TT)]).then_inc(xt_done, 1)

            def router_scores(i):
                pe.wait_ge(xfT_done, i + 1)
                for t in range(TT):
                    ins = nc.tensor.matmul(psC[:, t * NSC:(t + 1) * NSC], xfT[:, t * P:(t + 1) * P], wsc[:, :],
                                           start=True, stop=True)
                ins.then_inc(sc_done, 1)

            def body(b, exact):
                k = place(b)
                for s in range(NQ * SLOTS):
                    j = s // SLOTS
                    jj = (j + 1) % NQ
                    if exact and s % SLOTS == 0:
                        if j < NQ - 1 and k < B:
                            maxima(b, jj)
                        elif j == NQ - 1 and k < B - 1:
                            maxima(b + 1, jj)
                    if j < NQ - 1 and k < B:
                        scores(b, jj, s % SLOTS)
                    elif j == NQ - 1 and k < B - 1:
                        scores(b + 1, jj, s % SLOTS)
                    if s % SLOTS > 0 and k < B:
                        attend(b, j, (0, 2, 1, 3)[s % SLOTS - 1])
                    if k < B - 2:
                        if s == 0:
                            norm_transposed(b + 2)
                        if s in (2, 4, 6, 8):
                            project(b + 2, s // 2 - 1)
                        if s == 16:
                            qk_transposed(b + 2, 0)
                        if s == 18:
                            qk_transposed(b + 2, 1)
                    if s == 2 and k >= 1:
                        quad_transposed(b - 1, 3, on_done, b * NQ - 1)
                    if s == 5 and k >= 1:
                        heads_transposed(b - 1)
                    if s == 7 and k >= 1:
                        output_projection(b - 1)
                    if s == 9 and k < B:
                        quad_transposed(b, 0, x1_done if k >= 1 else None, b)
                    if s == 12 and k < B:
                        quad_transposed(b, 1, on_done, b * NQ + 1)
                    if s == 14 and k >= 1:
                        if k < B:
                            router_transposed(b - 1, on_done, b * NQ + 2)
                        else:
                            router_transposed(b - 1, x1_done, b)
                    if s == 16 and k >= 1:
                        router_scores(b - 1)
                    if s == 18 and k < B:
                        if k >= 1:
                            quad_transposed(b, 2, sc_copied, b)
                        else:
                            quad_transposed(b, 2, on_done, b * NQ + 2)

            pe.wait_ge(const_in, 16)
            pe.wait_ge(w_in, 6 * 16)
            for i in range(2):
                norm_transposed(i)
                for t in range(TT):
                    project(i, t)
            for i in range(2):
                qk_transposed(i, 0)
                qk_transposed(i, 1)
            pe.wait_ge(masks_ready, 1)
            pe.wait_ge(wsc_ready, 1)
            pe.wait_ge(zeros_ready, 2)

            def main(exact):
                if exact:
                    maxima(0, 0)
                for s in range(SLOTS):
                    scores(0, 0, s)
                over_batches(pe, lambda b: body(b, exact))

            either(pe, main)

            pe.wait_ge(hot_ready, 1)
            for q in range(NT // 4):
                if q >= 2:
                    pe.wait_ge(hotT_ready, q - 1)
                bank = (psA, psC)[q % 2]
                for t in range(4):
                    ins = nc.tensor.transpose(bank[0:NTILE, t * P:(t + 1) * P], hot[:, 4 * q + t, :], ident)
                ins.then_inc(hot_done, 1)
            for q in range(NT // 2):
                pe.wait_ge(hotT_ready, q // 2 + 1)
                if q >= 4:
                    pe.wait_ge(got_copied, q - 3)
                for t in range(2):
                    ins = nc.tensor.matmul(psS[:, (q % 4) // 2, (q % 2) * 512 + t * 256:(q % 2) * 512 + t * 256 + TABW],
                                           hotT[:, (2 * q + t) * P:(2 * q + t + 1) * P], tab[:, :],
                                           start=True, stop=True)
                ins.then_inc(got_done, 1)

        @block.scalar
        def _(act):
            nc.scalar.preload_act_table_set("natural_log_exp_and_others")

            def rsqrt_start(out, tmp, in_, scale, eps, log_sem, done_sem, i):
                nc.scalar.activation(tmp, in_, ACT.Ln, bias=eps, scale=scale).then_inc(log_sem, 1)
                act.wait_ge(log_sem, i + 1)
                nc.scalar.activation(out, tmp, ACT.Exp, scale=-0.5).then_inc(done_sem, 1)

            def norm1(i):
                act.wait_ge(mv1, i + 1)
                rsqrt_start(lnr[:, 1, :], lnr[:, 0, :], mv[:, :, 1], 1.0, eps_ln, ln1, r01, i)

            def norm2(i):
                act.wait_ge(mv2, i + 1)
                rsqrt_start(lnrb[:, 1, :], lnrb[:, 0, :], mvb[:, :, 1], 1.0, eps_ln, ln2, r02, i)

            def norm_heads(i):
                act.wait_ge(ss_done, 2 * i + 2)
                rsqrt_start(rr[:, 1, :], rr[:, 5, :], rr[:, 0, :], 1.0 / HD, eps_rms, lnq, rq0, i)

            def copy_projected(i, t):
                act.wait_ge(z_done, i * TT + (t + 1))
                if t == 0 and later(i, 1):
                    act.wait_ge(zn_done, i)
                nc.scalar.activation(zqk[:, t, :], psA[:, 0:2 * D], ACT.Copy)
                nc.scalar.activation(vtok[:, i, t, :], psA[:, 2 * D:3 * D], ACT.Copy).then_inc(z_copied, 1)

            def exponentials(b, j, s):
                g = b * (NQ * SLOTS) + (j * SLOTS + s)
                act.wait_ge(s_ready, g + 1)
                if s == 0 and later(b * NQ + j, 2):
                    act.wait_ge(pv_done, b * NQ + (j - 1))
                nc.scalar.activation(pt[:, j % 2, s * SW:(s + 1) * SW], psS[:, (j * SLOTS + s) % 2, :],
                                     ACT.Exp).then_inc(exp_done, 1)

            def load_shift(b, j):
                n = b * NQ + j
                act.wait_ge(shift_ready, n + 1)
                for c in range(4):
                    hh, gg = c // 2, c % 2
                    act.dma_start(stq[64 * hh + ROWS:64 * hh + SROWS, j, gg, :], shift[c * NP:(c + 1) * NP, :])\
                       .then_inc(shift_in, 16)

            def body(b, exact):
                k = place(b)
                for s in range(NQ * SLOTS):
                    j = s // SLOTS
                    jj = (j + 1) % NQ
                    if exact and s % SLOTS == 0:
                        if j < NQ - 1 and k < B:
                            load_shift(b, jj)
                        elif j == NQ - 1 and k < B - 1:
                            load_shift(b + 1, jj)
                    if j < NQ - 1 and k < B:
                        exponentials(b, jj, s % SLOTS)
                    elif j == NQ - 1 and k < B - 1:
                        exponentials(b + 1, jj, s % SLOTS)
                    if k < B - 2:
                        if s in (2, 4, 6, 8):
                            copy_projected(b + 2, s // 2 - 1)
                        if s == 10:
                            norm_heads(b + 2)
                    if k < B - 3 and s == 15:
                        norm1(b + 3)
                    if k >= 1:
                        if s == 6:
                            act.wait_ge(op_done, b)
                            nc.scalar.activation(onT[:, :], psC[:, :], ACT.Copy).then_inc(onT_done, 1)
                        if s == 11:
                            norm2(b - 1)
                        if s == 15:
                            act.wait_ge(xt_done, b)
                            nc.scalar.activation(xfT[:, :], psC[:, :], ACT.Copy).then_inc(xfT_done, 1)

            act.wait_ge(const_in, 16)
            norm1(0)
            for t in range(TT):
                copy_projected(0, t)
            norm1(1)
            norm_heads(0)
            for t in range(TT):
                copy_projected(1, t)
            norm_heads(1)
            norm1(2)

            def main(exact):
                if exact:
                    load_shift(0, 0)
                for s in range(SLOTS):
                    exponentials(0, 0, s)
                over_batches(act, lambda b: body(b, exact))

            either(act, main)

            act.wait_ge(sc_copied, B)
            nc.scalar.activation(ex.rearrange("p (t c) -> p t c", c=NCL), sc[:, :, 0:NCL], ACT.Exp,
                                 scale=nrt[:, 0:1]).then_inc(ex_done, 1)
            act.wait_ge(sel_ready, 1)
            nc.scalar.activation(ex, sel, ACT.Exp, scale=nrt[:, 0:1]).then_inc(ex_done, 1)
            act.wait_ge(hid_ready, 1)
            nc.scalar.activation(hid, hid, ACT.Gelu).then_inc(gelu_done, 1)
            for q in range(NT // 4):
                act.wait_ge(hot_done, q + 1)
                nc.scalar.activation(hotT[:, q * 4 * P:(q + 1) * 4 * P], (psA, psC)[q % 2][0:NTILE, :], ACT.Copy)\
                  .then_inc(hotT_ready, 1)
            act.wait_ge(cpre_ready, 1)
            nc.scalar.activation(comp[:, :, :], comp[:, :, :], ACT.Tanh).then_inc(tanh_done, 1)
            for q in range(NT // 2):
                act.wait_ge(got_done, q + 1)
                src = psS[:, (q % 4) // 2, (q % 2) * 512:(q % 2) * 512 + 512].rearrange("p (t n) -> p t n", t=2)
                nc.scalar.activation(got[:, 2 * q:2 * q + 2, :], src[:, :, 0:TABW], ACT.Copy).then_inc(got_copied, 1)
            for k in range(NT // G):
                act.wait_ge(mv3, k + 1)
                c = slice(k * G, (k + 1) * G)
                rsqrt_start(lnrc[:, 1, c], lnrc[:, 0, c], mvc[:, c, 1], 1.0, eps_ln, ln3, r03, k)

        @block.vector
        def _(dve):
            ncv = nc.vector

            def prepare():
                dve.wait_ge(const_in, 16)
                dve.wait_ge(w_in, 6 * 16)
                n = [0]

                def link(ins):
                    n[0] += 1
                    ins.then_inc(prep_dve, 1)
                    dve.wait_ge(prep_dve, n[0])
                ncv.tensor_scalar(sg[:, 0], sig[:, :], 0.3, None, ALU.is_gt)
                link(ncv.tensor_scalar(sg[:, 1], sig[:, :], -0.3, None, ALU.is_lt))
                link(ncv.tensor_tensor(sg[:, 2], sg[:, 0], sg[:, 1], ALU.subtract))
                link(ncv.tensor_tensor(sg[:, 0], sg[:, 2], sig[:, :], ALU.subtract))
                link(ncv.tensor_tensor(wsc[:, NCL:NCL + NTILE], sig[:, :], sg[:, 0], ALU.add))
                tiles = wsc[:, NCL:NCL + NTILE].rearrange("p (c t) -> p t c", t=TPC)
                link(ncv.tensor_tensor(csum[:, 0], tiles[:, 0], tiles[:, 1], ALU.add))
                for t in range(2, TPC):
                    link(ncv.tensor_tensor(csum[:, 0], csum[:, 0], tiles[:, t], ALU.add))
                ncv.tensor_scalar(csum[:, 1], csum[:, 0], 0.0, None, ALU.is_gt)
                link(ncv.tensor_scalar(sg[:, 0, 0:NCL], csum[:, 0], 0.0, None, ALU.is_lt))
                ncv.tensor_tensor(wsc[:, 0:NCL], csum[:, 1], sg[:, 0, 0:NCL], ALU.subtract).then_inc(wsc_ready, 1)
                link(ncv.tensor_scalar(nrt[:, 0:1], vec[:, V_TEMP:V_TEMP + 1], 1e-6, None, ALU.add))
                link(ncv.reciprocal(nrt[:, 1:2], nrt[:, 0:1]))
                ncv.tensor_scalar(nrt[:, 0:1], nrt[:, 1:2], -1.0, None, ALU.mult)
                ncv.tensor_tensor(dk[:, :], vec[:, V_KNOT + 1:V_KNOT + KNOTS], vec[:, V_KNOT:V_KNOT + KNOTS - 1],
                                  ALU.subtract)
                ncv.tensor_reduce(wabs[:, 0:1], vec[:, V_QW:V_QW + HD], axis=AX.X, op=ALU.max,
                                  apply_absolute_value=True)
                link(ncv.tensor_reduce(wabs[:, 1:2], vec[:, V_KW:V_KW + HD], axis=AX.X, op=ALU.max,
                                       apply_absolute_value=True))
                link(ncv.tensor_tensor(wabs[:, 2:3], wabs[:, 0:1], wabs[:, 1:2], ALU.mult))
                ncv.tensor_scalar(beyond[:, :], wabs[:, 2:3], SAFE / (HD * SCALE), None, ALU.is_gt)\
                   .then_inc(beyond_ready, 1)
                ncv.tensor_copy(ident_b[:, :], ident)
                ncv.tensor_copy(mask_b[:, :], const[:, C_MASK:C_MASK + P]).then_inc(masks_ready, 1)
                ncv.tensor_scalar(wsq[:, 0], vec[:, V_QW:V_QW + HD], SCALE, None, ALU.mult)
                link(ncv.tensor_copy(wsq[:, 1], vec[:, V_KW:V_KW + HD]))
                cos = const[:, C_COS:C_COS + TT * HD].rearrange("p (t d) -> p t d", t=TT)
                sin = const[:, C_SIN:C_SIN + TT * HD].rearrange("p (t d) -> p t d", t=TT)
                half = HD // 2
                for qk in range(2):
                    w = wsq[:, qk, :].unsqueeze(1)
                    ncv.tensor_tensor(cwt[:, :, qk, :], cos, w.broadcast_to([P, TT, HD]), ALU.mult)
                    ncv.tensor_tensor(swt[:, :, qk, 0:half], sin[:, :, 0:half],
                                      w[:, :, half:HD].broadcast_to([P, TT, half]), ALU.mult)
                    ins = ncv.tensor_tensor(swt[:, :, qk, half:HD], sin[:, :, half:HD],
                                            w[:, :, 0:half].broadcast_to([P, TT, half]), ALU.mult)
                ins.then_inc(rope_ready, 1)

            def carry():
                ncv.memset(gap[:, :], 0.0)

            def stats(src, st, m, stat_sem, mv_sem, i):
                for t in range(TT):
                    ins = ncv.bn_stats(st[:, t, :], src[:, t, :])
                ins.then_inc(stat_sem, 1)
                dve.wait_ge(stat_sem, i + 1)
                carry()
                for t in range(TT):
                    ins = ncv.bn_aggr(m[:, t, :], st[:, t, :])
                ins.then_inc(mv_sem, 1)

            def refine(v_in, scale, eps, r, buf, nw, i):
                ncv.tensor_scalar(buf[:, 2, :], v_in, scale, eps, ALU.mult, ALU.add)
                ncv.tensor_tensor(buf[:, 3, :], r, r, ALU.mult).then_inc(nw, 1)
                dve.wait_ge(nw, 3 * i + 1)
                ncv.scalar_tensor_tensor(buf[:, 2, :], buf[:, 2, :], -0.5, buf[:, 3, :], ALU.mult, ALU.mult)\
                   .then_inc(nw, 1)
                dve.wait_ge(nw, 3 * i + 2)
                return ncv.scalar_tensor_tensor(buf[:, 4, :], buf[:, 2, :], 1.5, r, ALU.add, ALU.mult)\
                    .then_inc(nw, 1)

            def norm1_stats(i):
                if isinstance(i, int) and i < 2:
                    dve.wait_ge((x0_in, x1_in)[i], 16)
                else:
                    dve.wait_ge(xr_in, 16 * (B - 2))
                stats(xs[:, i], st6, mv, stat1, mv1, i)

            def norm1(i):
                dve.wait_ge(r01, i + 1)
                refine(mv[:, :, 1], 1.0, EPS_LN, lnr[:, 1, :], lnr, nw1, i)
                dve.wait_ge(nw1, 3 * i + 3)
                if later(i, 1):
                    dve.wait_ge(t1_done, i)
                for t in range(TT):
                    ins = ncv.tensor_scalar(xn[:, t, :], xs[:, i, t, :], mv[:, t, 0:1], lnr[:, 4, t:t + 1],
                                            ALU.subtract, ALU.mult)
                ins.then_inc(xn_ready, 1)

            def copy_norm(i):
                dve.wait_ge(t1_done, i + 1)
                if later(i, 1):
                    dve.wait_ge(z_done, i * TT)
                ncv.tensor_copy(xnT[:, :], psA[:, :]).then_inc(xnT_done, 1)

            def head_sums(i, a):
                ts = slice(2 * a, 2 * a + 2)
                dve.wait_ge(z_copied, i * TT + (2 * a + 2))
                if later(i, 1):
                    dve.wait_ge(ss_done, 2 * i + (a - 1))
                ncv.tensor_tensor(sq[:, ts, :], zqk[:, ts, :], zqk[:, ts, :], ALU.mult).then_inc(sq_done, 1)
                dve.wait_ge(sq_done, 2 * i + (a + 1))
                if later(i, 1):
                    dve.wait_ge(nwq, 3 * i)
                n = 2 * 2 * H
                ncv.tensor_reduce(rr[:, 0, a * n:(a + 1) * n], sq[:, ts, :].rearrange("p t (g d) -> p (t g) d", d=HD),
                                  axis=AX.X, op=ALU.add).then_inc(ss_done, 1)

            def head_norm(i):
                dve.wait_ge(rq0, i + 1)
                if later(i, 1):
                    dve.wait_ge(zn_done, i)
                refine(rr[:, 0, :], 1.0 / HD, EPS_RMS, rr[:, 1, :], rr, nwq, i)
                dve.wait_ge(nwq, 3 * i + 3)
                if later(i, 1):
                    dve.wait_ge(rope_b, i)
                    dve.wait_ge(qkr_done, i)
                ncv.tensor_tensor(zn[:, :, :].rearrange("p t (g d) -> p (t g) d", d=HD),
                                  zqk[:, :, :].rearrange("p t (g d) -> p (t g) d", d=HD),
                                  rr[:, 4, :].unsqueeze(2).broadcast_to([P, TT * 2 * H, HD]), ALU.mult)\
                   .then_inc(zn_done, 1)

            def rotate_cos(i):
                dve.wait_ge(zn_done, i + 1)
                if later(i, 1):
                    dve.wait_ge(kt_done, 2 * i)
                ncv.tensor_tensor(q4, z4, cw.broadcast_to([P, 2 * TT, H, HD]), ALU.mult).then_inc(rope_a, 1)

            def rotate_sum(i):
                dve.wait_ge(rope_a, i + 1)
                dve.wait_ge(rope_b, i + 1)
                ncv.tensor_tensor(q4, q4, b4, ALU.add).then_inc(qkr_done, 1)

            def split(i, qk):
                dve.wait_ge(kt_done, 2 * i + (qk + 1))
                if qk == 0 and later(i, 1):
                    dve.wait_ge(scr_done, 12 * 16 * i)
                    dve.wait_ge(parts_done, 2 * i)
                ncv.tensor_copy(parts[:, qk, 0, :], psA[:, :]).then_inc(p1_done, 1)
                dve.wait_ge(p1_done, 2 * i + (qk + 1))
                ncv.tensor_tensor(rest[:, qk, :], psA[:, :], parts[:, qk, 0, :], ALU.subtract).then_inc(rest_done, 1)
                dve.wait_ge(rest_done, 2 * i + (qk + 1))
                ncv.tensor_copy(parts[:, qk, 1, :], rest[:, qk, :]).then_inc(p2_done, 1)

            def maxima(b, j):
                n = b * NQ + j
                for e in range(4 * TT):
                    c, qb = e // TT, e % TT
                    dve.wait_ge(smax_ready, n * (4 * TT) + (e + 1))
                    if e == 0 and later(n, 1):
                        dve.wait_ge(nmax_ready, n)
                    ncv.tensor_reduce(nmax[:, 0, qb * 4 + c:qb * 4 + c + 1],
                                      psS[:, j % 2, (e % 2) * 512:(e % 2) * 512 + (qb + 1) * P],
                                      axis=AX.X, op=ALU.max, negate=True).then_inc(smax_read, 1)
                dve.wait_ge(smax_read, (n + 1) * (4 * TT))
                if later(n, 1):
                    dve.wait_ge(shift_ps, n)
                for r in range(NP):
                    if r < NP - 1:
                        ncv.tensor_copy(nmax_b[:, r, :], nmax[:, r, :]).then_inc(nmax_step, 1)
                        dve.wait_ge(nmax_step, n * 4 + (2 * r + 1))
                        ncv.tensor_copy(nparts[:, :, r], nmax_b[:, r, :])
                        dst = nmax[:, 1, :] if r == 0 else nparts[:, :, 2]
                        ins = ncv.tensor_tensor(dst, nmax[:, r, :], nmax_b[:, r, :], ALU.subtract)
                        ins.then_inc(nmax_step, 1)
                        dve.wait_ge(nmax_step, n * 4 + (2 * r + 2))
                ncv.memset(gap[:, :], 0.0).then_inc(nmax_ready, 1)
                dve.wait_ge(shift_ps, n + 1)
                if later(n, 1):
                    dve.wait_ge(shift_in, n * 64)
                ncv.tensor_copy(shift[:, :], psS[0:4 * NP, j % 2, 0:512]).then_inc(shift_ready, 1)

            def copy_quad(b, j):
                n = b * NQ + j
                dve.wait_ge(pv_done, n + 1)
                if later(n, 2):
                    dve.wait_ge(ot_done, n - 1)
                ncv.tensor_copy(oT[:, j % 2, :], psO[:, j % 2, :]).then_inc(o_copied, 1)

            def normalise(b, j):
                n = b * NQ + j
                dve.wait_ge(ot_done, n + 1)
                o = psC[:, :].rearrange("p (t c w) -> p t c w", t=TT, w=VW)
                ncv.reciprocal(rec[:, :, :], o[:, :, :, HD]).then_inc(rec_done, 1)
                dve.wait_ge(rec_done, n + 1)
                if j == 0 and later(b, 1):
                    dve.wait_ge(op_done, b)
                ncv.tensor_tensor(on[:, :, 32 * j:32 * j + 32].rearrange("p t (c d) -> p t c d", d=HD),
                                  o[:, :, :, 0:HD], rec[:, :, :].unsqueeze(3).broadcast_to([P, TT, 4, HD]),
                                  ALU.mult).then_inc(on_done, 1)

            def residual(i):
                dve.wait_ge(pr_done, i + 1)
                ncv.tensor_tensor(xs[:, i], psC[:, :].rearrange("p (t d) -> p t d", t=TT), xs[:, i], ALU.add)\
                   .then_inc(x1_done, 1)

            def norm2_stats(i):
                dve.wait_ge(x1_done, i + 1)
                carry()
                stats(xs[:, i], st6b, mvb, stat2, mv2, i)

            def norm2(i):
                dve.wait_ge(r02, i + 1)
                refine(mvb[:, :, 1], 1.0, EPS_LN, lnrb[:, 1, :], lnrb, nw2, i)
                dve.wait_ge(nw2, 3 * i + 3)
                if later(i, 1):
                    dve.wait_ge(xt_done, i)
                    dve.wait_ge(xf_stored, i)
                for t in range(TT):
                    ins = ncv.tensor_scalar(xf1[:, t, :], xs[:, i, t, :], mvb[:, t, 0:1], lnrb[:, 4, t:t + 1],
                                            ALU.subtract, ALU.mult)
                ins.then_inc(xf1_ready, 1)

            def copy_scores(i):
                dve.wait_ge(sc_done, i + 1)
                ncv.tensor_copy(sc4[:, i], psC[:, 0:TT * NSC]).then_inc(sc_copied, 1)

            sc4 = sc[:, :, :].rearrange("p (b t) n -> p b (t n)", b=B)

            def body(b, exact):
                k = place(b)
                for s in range(NQ * SLOTS):
                    j = s // SLOTS
                    jj = (j + 1) % NQ
                    if exact and s % SLOTS == 0:
                        if j < NQ - 1 and k < B:
                            maxima(b, jj)
                        elif j == NQ - 1 and k < B - 1:
                            maxima(b + 1, jj)
                    if s == 0 and k >= 1:
                        copy_quad(b - 1, 3)
                    if s == 1 and k < B - 2:
                        copy_norm(b + 2)
                    if s == 3 and k >= 1:
                        normalise(b - 1, 3)
                    if s == 5:
                        if k < B:
                            copy_quad(b, 0)
                        if k < B - 2:
                            head_sums(b + 2, 0)
                    if s == 8 and k >= 1:
                        residual(b - 1)
                    if s == 9:
                        if k < B - 2:
                            head_sums(b + 2, 1)
                        if k >= 1:
                            norm2_stats(b - 1)
                    if s == 10 and k < B:
                        normalise(b, 0)
                        copy_quad(b, 1)
                    if s == 11 and k < B - 2:
                        head_norm(b + 2)
                        rotate_cos(b + 2)
                    if s == 12 and k >= 1:
                        norm2(b - 1)
                    if s == 13 and k < B:
                        normalise(b, 1)
                    if s == 14:
                        if k < B - 3:
                            norm1_stats(b + 3)
                        if k < B - 2:
                            rotate_sum(b + 2)
                    if s == 15 and k < B:
                        copy_quad(b, 2)
                    if s == 16 and k < B - 3:
                        norm1(b + 3)
                    if s == 17:
                        if k >= 1:
                            copy_scores(b - 1)
                        if k < B - 2:
                            split(b + 2, 0)
                    if s == 19:
                        if k < B - 2:
                            split(b + 2, 1)
                        if k < B:
                            normalise(b, 2)

            norm1_stats(0)
            norm1(0)
            copy_norm(0)
            prepare()
            norm1_stats(1)
            head_sums(0, 0)
            head_sums(0, 1)
            norm1(1)
            copy_norm(1)
            head_norm(0)
            rotate_cos(0)
            rotate_sum(0)
            split(0, 0)
            head_sums(1, 0)
            split(0, 1)
            head_sums(1, 1)
            head_norm(1)
            rotate_cos(1)
            norm1_stats(2)
            rotate_sum(1)
            norm1(2)
            split(1, 0)
            split(1, 1)

            def main(exact):
                if exact:
                    maxima(0, 0)
                over_batches(dve, lambda b: body(b, exact))

            either(dve, main)

            n = [0]

            def link(ins):
                n[0] += 1
                ins.then_inc(tail_dve, 1)
                dve.wait_ge(tail_dve, n[0])

            def first_of_largest(src, dst):
                g3, e3, p3, d3 = (a.rearrange("p (t c) -> p t c", c=NCL) for a in (src, eq, pref, dst))
                link(ncv.tensor_reduce(top[:, :], g3, axis=AX.X, op=ALU.max))
                link(ncv.tensor_tensor(e3, g3, top[:, :].unsqueeze(2).broadcast_to([P, NT, NCL]), ALU.is_ge))
                link(ncv.tensor_tensor(p3, e3, const[:, C_PREF:C_PREF + 8].unsqueeze(1).broadcast_to([P, NT, NCL]),
                                       ALU.mult))
                link(ncv.tensor_reduce(top[:, :], p3, axis=AX.X, op=ALU.max))
                link(ncv.tensor_tensor(d3, p3, top[:, :].unsqueeze(2).broadcast_to([P, NT, NCL]), ALU.is_equal))

            def calibrate(r):
                dve.wait_ge(ex_done, r + 1)
                link(ncv.tensor_scalar(ex, ex, 1.0, None, ALU.add))
                link(ncv.reciprocal(gate, ex))
                ncv.tensor_scalar(u7, gate, float(KNOTS - 1), None, ALU.mult).then_inc(u7_ready, 1)
                dve.wait_ge(u7_ready, r + 1)
                link(ncv.tensor_tensor(step, u7.unsqueeze(2).broadcast_to([P, NG, KNOTS]),
                                       const[:, C_STEP:C_STEP + KNOTS].unsqueeze(1).broadcast_to([P, NG, KNOTS]),
                                       ALU.is_ge))
                link(ncv.tensor_tensor(cell, step[:, :, 0:KNOTS - 1], step[:, :, 1:KNOTS], ALU.subtract))
                dve.wait_ge(line_ready, r + 1)
                link(ncv.tensor_tensor(line, line,
                                       vec[:, V_KNOT:V_KNOT + KNOTS - 1].unsqueeze(1).broadcast_to([P, NG, KNOTS - 1]),
                                       ALU.add))
                link(ncv.tensor_tensor(cell, cell, line, ALU.mult))
                link(ncv.tensor_reduce(gate, cell, axis=AX.X, op=ALU.add))

            calibrate(0)
            first_of_largest(gate, hot_c)
            s4 = step[:, :, :].rearrange("p (t a) c -> p t a c", t=NT)
            c3 = hot_c.rearrange("p (t c) -> p t c", c=NCL)
            t3 = hot_t.rearrange("p (t c) -> p t c", c=NCL)
            link(ncv.tensor_tensor(s4, sc[:, :, NCL:NCL + NTILE].rearrange("p t (c a) -> p t a c", c=NCL),
                                   c3.unsqueeze(2).broadcast_to([P, NT, TPC, NCL]), ALU.mult))
            ncv.tensor_reduce(sel.rearrange("p (t a) -> p t a", a=TPC), s4, axis=AX.X, op=ALU.add)\
               .then_inc(sel_ready, 1)
            dve.wait_ge(prod_ready, 2)
            ncv.tensor_reduce(comp[:, 0, :], prod0, axis=AX.X, op=ALU.add)
            link(ncv.tensor_reduce(comp[:, 1, :], prod1, axis=AX.X, op=ALU.add))
            link(ncv.tensor_tensor(comp[:, :, :], comp[:, :, :],
                                   vec[:, V_B2:V_B2 + 2].unsqueeze(2).broadcast_to([P, 2, NT]), ALU.add))
            cpre = ncv.tensor_copy(mag[:, :], comp[:, 0, :])
            cpre.then_inc(cpre_ready, 1)
            calibrate(1)
            first_of_largest(gate, hot_t)
            ncv.tensor_tensor(hot[:, :, :].rearrange("p t (c a) -> p t c a", c=NCL),
                              c3.unsqueeze(3).broadcast_to([P, NT, NCL, TPC]),
                              t3.unsqueeze(2).broadcast_to([P, NT, NCL, TPC]), ALU.mult).then_inc(hot_ready, 1)
            dve.wait_ge(tanh_done, 1)
            dve.wait_ge(got_copied, NT // 2)
            w1 = got[:, :, 0:2 * GRID].rearrange("p t (a n) -> p a t n", a=2)
            for a in range(2):
                ins = ncv.tensor_tensor(m01[:, a], w1[:, a], comp[:, a, :].unsqueeze(2).broadcast_to([P, NT, GRID]),
                                        ALU.mult)
            link(ins)
            link(ncv.tensor_tensor(m01[:, 0], m01[:, 0], m01[:, 1], ALU.add))
            link(ncv.tensor_tensor(m01[:, 0], m01[:, 0], got[:, :, 2 * GRID:3 * GRID], ALU.add))
            link(ncv.tensor_scalar(m01[:, 0], m01[:, 0], 0.0, None, ALU.max))
            link(ncv.tensor_tensor(m01[:, 1], m01[:, 0], got[:, :, 3 * GRID:4 * GRID], ALU.mult))
            link(ncv.tensor_reduce(mag[:, :], m01[:, 1], axis=AX.X, op=ALU.add))
            link(ncv.tensor_tensor(mag[:, :], mag[:, :], got[:, :, 4 * GRID], ALU.add))
            link(ncv.tensor_scalar(mag[:, :], mag[:, :], vec[:, V_OS:V_OS + 1], None, ALU.mult))

            def spline_out(k):
                c = slice(k * G, (k + 1) * G)
                direction = got[:, c, 4 * GRID + 1:TABW]
                link(ncv.tensor_tensor(direction, direction, mag[:, c].unsqueeze(2).broadcast_to([P, G, D]), ALU.mult))
                link(ncv.tensor_tensor(xff[:, c, :], xff[:, c, :], direction, ALU.add))
                for t in range(k * G, (k + 1) * G):
                    ins = ncv.bn_stats(st6c[:, t, :], xff[:, t, :])
                ins.then_inc(stat3, 1)
                dve.wait_ge(stat3, k + 1)
                for t in range(k * G, (k + 1) * G):
                    ins = ncv.bn_aggr(mvc[:, t, :], st6c[:, t, :])
                ins.then_inc(mv3, 1)

            def norm3(k):
                c = slice(k * G, (k + 1) * G)
                dve.wait_ge(r03, k + 1)
                refine(mvc[:, c, 1], 1.0, EPS_LN, lnrc[:, 1, c], lnrc[:, :, c], nw3, k)
                dve.wait_ge(nw3, 3 * k + 3)
                for t in range(k * G, (k + 1) * G):
                    ins = ncv.tensor_scalar(xff[:, t, :], xff[:, t, :], mvc[:, t, 0:1], lnrc[:, 4, t:t + 1],
                                            ALU.subtract, ALU.mult)
                ins.then_inc(yn_ready, 1)

            def residual_out(k):
                c = slice(k * G, (k + 1) * G)
                dve.wait_ge(ygb_ready, k + 1)
                ncv.tensor_tensor(xsf[:, c, :], xsf[:, c, :], xff[:, c, :], ALU.add).then_inc(out_ready, 1)

            for k in range(NT // G):
                spline_out(k)
                norm3(k)
            for k in range(NT // G):
                residual_out(k)

        @block.gpsimd
        def _(pool):
            ncg = nc.gpsimd
            one = const[:, C_J + 1:C_J + 2].unsqueeze(1)
            ncg.memset(stk[:, :, :, :], 1.0)
            ncg.memset(stq[:, :, :, :], 0.0)
            ncg.memset(vaug[:, :, :, :], 0.0).then_inc(zeros_ready, 1)
            pool.wait_ge(const_in, 16)
            pool.wait_ge(zeros_ready, 1)
            ncg.memset(vaug[:, :, :, HD:HD + 1], 1.0).then_inc(zeros_ready, 1)
            pool.wait_ge(zeros_ready, 2)

            def rotate_sin(i):
                pool.wait_ge(zn_done, i + 1)
                if later(i, 1):
                    pool.wait_ge(qkr_done, i)
                half = HD // 2
                for a, c in ((0, half), (half, 0)):
                    ins = ncg.tensor_tensor(b4[:, :, :, a:a + half], z4[:, :, :, c:c + half],
                                            sw[:, :, :, a:a + half].broadcast_to([P, 2 * TT, H, half]), ALU.mult)
                ins.then_inc(rope_b, 1)

            def split(i, qk):
                n = 2 * i + (qk + 1)
                pool.wait_ge(p2_done, n)
                ncg.tensor_tensor(parts[:, qk, 2, :], rest[:, qk, :], parts[:, qk, 1, :], ALU.subtract)\
                   .then_inc(parts_done, 1)

            def values(b, j):
                if later(b, 1):
                    pool.wait_ge(pv_done, b * NQ + (j - (NQ - 1)))
                else:
                    pool.wait_ge(z_copied, TT)
                v = vtok[:, b, :, 32 * j:32 * j + 32].rearrange("p t (c d) -> p t c d", d=HD)
                ncg.tensor_tensor(vaug[:, :, 4 * j:4 * j + 4, 0:HD], v,
                                  one.unsqueeze(1).broadcast_to([P, TT, 4, HD]), ALU.mult)\
                   .then_inc(v_ready, 1)

            def store_xf(i):
                pool.wait_ge(xf1_ready, i + 1)
                ncg.tensor_tensor(xf[:, i], xf1[:, :, :], one.broadcast_to([P, TT, D]), ALU.mult).then_inc(xf_stored, 1)

            def body(b):
                k = place(b)
                if 1 <= k < B:
                    values(b, 3)
                if k < B - 1:
                    values(b + 1, 0)
                    values(b + 1, 1)
                if k < B - 2:
                    rotate_sin(b + 2)
                if k >= 1:
                    store_xf(b - 1)
                if k < B - 1:
                    values(b + 1, 2)
                if k < B - 2:
                    split(b + 2, 0)
                    split(b + 2, 1)

            pool.wait_ge(rope_ready, 1)
            for j in range(NQ):
                values(0, j)
            for i in range(2):
                rotate_sin(i)
                split(i, 0)
                split(i, 1)
            over_batches(pool, body)

            pool.wait_ge(sc_copied, B)
            ncg.tensor_tensor(hid, sc[:, :, NCL + NTILE:NSC],
                              vec[:, V_B1:V_B1 + COMP].unsqueeze(1).broadcast_to([P, NT, COMP]), ALU.add)\
               .then_inc(hid_ready, 1)

            def lines(r):
                pool.wait_ge(u7_ready, r + 1)
                shape = [P, NG, KNOTS - 1]
                ncg.tensor_tensor(line, u7.unsqueeze(2).broadcast_to(shape),
                                  const[:, C_J:C_J + KNOTS - 1].unsqueeze(1).broadcast_to(shape), ALU.subtract)\
                   .then_inc(tail_pool, 1)
                pool.wait_ge(tail_pool, r + 1)
                ncg.tensor_tensor(line, line, dk[:, :].unsqueeze(1).broadcast_to(shape), ALU.mult)\
                   .then_inc(line_ready, 1)

            lines(0)
            pool.wait_ge(gelu_done, 1)
            for a, prod in enumerate((prod0, prod1)):
                w2 = vec[:, V_W2 + a * COMP:V_W2 + (a + 1) * COMP]
                ncg.tensor_tensor(prod, hid, w2.unsqueeze(1).broadcast_to([P, NT, COMP]), ALU.mult)\
                   .then_inc(prod_ready, 1)
            lines(1)
            for k in range(NT // G):
                c = slice(k * G, (k + 1) * G)
                pool.wait_ge(yn_ready, k + 1)
                ncg.tensor_tensor(xff[:, c, :], xff[:, c, :],
                                  vec[:, V_GAM:V_GAM + D].unsqueeze(1).broadcast_to([P, G, D]), ALU.mult)\
                   .then_inc(tail_pool, 1)
                pool.wait_ge(tail_pool, 3 + k)
                ncg.tensor_tensor(xff[:, c, :], xff[:, c, :],
                                  vec[:, V_BET:V_BET + D].unsqueeze(1).broadcast_to([P, G, D]), ALU.add)\
                   .then_inc(ygb_ready, 1)


def shape_constants():
    c = np.zeros((P, NCONST), np.float32)
    p = np.arange(P)
    c[:, C_ID:C_ID + P] = np.eye(P)
    c[:, C_MASK:C_MASK + P] = np.where(p[None, :] >= p[:, None], 0.0, MASKED)
    freqs = np.float32(THETA) ** (-np.arange(0, HD, 2, dtype=np.float32) / HD)
    ang = np.arange(T, dtype=np.float32)[:, None] * freqs[None, :]
    cos, sin = np.cos(ang).reshape(TT, P, HD // 2), np.sin(ang).reshape(TT, P, HD // 2)
    both = np.concatenate([cos, cos], -1).transpose(1, 0, 2)
    signed = np.concatenate([-sin, sin], -1).transpose(1, 0, 2)
    c[:, C_COS:C_COS + TT * HD] = both.reshape(P, -1)
    c[:, C_SIN:C_SIN + TT * HD] = signed.reshape(P, -1)
    c[:, C_STEP:C_STEP + KNOTS] = [-1, 1, 2, 3, 4, 5, 6, BIG]
    c[:, C_J:C_J + KNOTS] = np.arange(KNOTS)
    c[:, C_PREF:C_PREF + 8] = np.arange(8, 0, -1)
    c[:, C_EPS] = EPS_LN
    c[:, C_EPS + 1] = EPS_RMS
    return c


def kernel(**inputs):
    import concourse.bacc as bacc
    from concourse.bass_utils import run_bass_kernel_spmd

    a = {k: np.asarray(v) for k, v in inputs.items()}
    f = lambda name: a["L0_ffn_" + name]
    table = np.concatenate([f("spline_w1").reshape(NTILE, 2 * GRID), f("spline_b1"),
                            f("spline_w2").reshape(NTILE, GRID), f("spline_b2"), f("directions")], axis=1)
    vector = np.concatenate([a["L0_attn_q_norm_w"], a["L0_attn_k_norm_w"], f("knot_values"), f("temperature"),
                             f("compress_b1"), f("compress_w2").T.reshape(-1), f("compress_b2"),
                             f("norm_gamma"), f("norm_beta"), f("output_scale")])[None]
    arrays = {
        "x": a["L0_attn_x"],
        "w_qkv_t": a["L0_attn_w_qkv"].T,
        "w_proj_t": a["L0_attn_w_proj"].T,
        "signatures_t": f("signatures_raw").T,
        "compress_w1": f("compress_w1"),
        "table": table,
        "vector": vector,
        "shape_constants": shape_constants(),
    }
    arrays = {k: np.ascontiguousarray(v) for k, v in arrays.items()}
    nc = bacc.Bacc("TRN2", target_bir_lowering=False, num_devices=1)
    args = [nc.dram_tensor(k, v.shape, mybir.dt.from_np(v.dtype), kind="ExternalInput").ap()
            for k, v in arrays.items()]
    out = nc.dram_tensor("out", (B, T, D), F32, kind="ExternalOutput").ap()
    build(nc, *args, out)
    r = run_bass_kernel_spmd(nc, [arrays], core_ids=[0])
    return r.results[0]["out"]
```

```python
from contextlib import ExitStack

import numpy as np

import concourse.bass as bass
from concourse import mybir

F32 = mybir.dt.float32
BF16 = mybir.dt.bfloat16
ALU = mybir.AluOpType
ACT = mybir.ActivationFunctionType
AX = mybir.AxisListType

P = 128
B, T, D = 8, 512, 128
H, HD = 16, 8
TT = T // P
NT = B * TT
NQ = H // 4
NP = 3
ROWS = 6 * HD
SROWS = ROWS + NP
Q_PARTS = (0, 0, 0, 1, 1, 2)
K_PARTS = (0, 1, 2, 0, 1, 0)
SLOTS = 5
SW = 1024
VW = 32
NTILE, TPC, NCL = 64, 8, 8
GRID, COMP, KNOTS = 16, 32, 8
NSC = NCL + NTILE + COMP
NG = TT * NCL
LINKS = 23
TABW = 4 * GRID + 1 + D
EPS_LN, EPS_RMS = 1e-5, 1e-6
SCALE = HD ** -0.5
THETA = 32.0
BIG = 3.0e38
MASKED = -1.0e30
SAFE = 70.0
GROUPS = ((0, 4), (4, 6), (6, 7), (7, 8))
CHUNKS = ((0, 2), (2, 4), (4, 6), (6, 7), (7, 8))

C_ID = 0
C_MASK = C_ID + P
C_COS = C_MASK + P
C_SIN = C_COS + TT * HD
C_STEP = C_SIN + TT * HD
C_J = C_STEP + KNOTS
C_PREF = C_J + KNOTS
C_EPS = C_PREF + 8
NCONST = C_EPS + 2

V_QW = 0
V_KW = V_QW + HD
V_KNOT = V_KW + HD
V_TEMP = V_KNOT + KNOTS
V_B1 = V_TEMP + 1
V_W2 = V_B1 + COMP
V_B2 = V_W2 + 2 * COMP
V_GAM = V_B2 + 2
V_BET = V_GAM + D
V_OS = V_BET + D
NVEC = V_OS + 1


def unit_of(kb, c):
    hh, gg = c // 2, c % 2
    if kb == 0:
        return 3 * gg, 512 * hh
    if kb == 2:
        return 2, 512 * hh + 256 * gg
    return 3 * gg + 1, 512 * hh + (384 if kb == 3 else 0)


def build(nc, x_d, wqkv_d, wproj_d, sig_d, cw1_d, tab_d, vec_d, const_d, out_d):
    with ExitStack() as ctx:
        def sb(name, shape, dt=F32):
            return ctx.enter_context(nc.sbuf_tensor(name, shape, dt))

        def psum(name, shape):
            return ctx.enter_context(nc.psum_tensor(name, shape, F32))

        def sem(name):
            return ctx.enter_context(nc.semaphore(name))

        xs = sb("xs", [P, B, TT, D])
        xf = sb("xf", [P, B, TT, D])
        sc = sb("sc", [P, TT, NSC])
        vtok = sb("vtok", [P, 2, TT, D])
        const = sb("const", [P, NCONST])
        vec = sb("vec", [P, NVEC])
        wqkv = sb("wqkv", [P, 3 * D])
        wproj = sb("wproj", [P, D])
        wsc = sb("wsc", [P, NSC])
        sig = sb("sig", [P, NTILE])
        sg = sb("sg", [P, 3, NTILE])
        csum = sb("csum", [P, 2, NCL])
        cwt = sb("cwt", [P, TT, 2, HD])
        swt = sb("swt", [P, TT, 2, HD])
        wsq = sb("wsq", [P, 2, HD])
        tab = sb("tab", [P, TABW])
        st6 = sb("st6", [P, TT, 6])
        mv = sb("mv", [P, TT, 2])
        lnr = sb("lnr", [P, 6, TT])
        xn = sb("xn", [P, TT, D])
        xnT = sb("xnT", [P, T])
        zqk = sb("zqk", [P, TT, 2 * D])
        sq = sb("sq", [P, TT, 2 * D])
        rr = sb("rr", [P, 6, TT * 2 * H])
        zn = sb("zn", [P, TT, 2 * D])
        qkr = sb("qkr", [P, TT, 2, D])
        parts = sb("parts", [P, 2, NP, T], BF16)
        rest = sb("rest", [P, 2, T])
        stq = sb("stq", [P, NQ, 2, T], BF16)
        stk = sb("stk", [P, NQ, 2, T], BF16)
        vaug = sb("vaug", [P, TT, H, VW])
        pt = sb("pt", [P, 2, SLOTS * SW])
        oT = sb("oT", [P, 2, T])
        rec = sb("rec", [P, TT, 4])
        on = sb("on", [P, TT, D])
        turned = sb("turned", [P, T])
        st6b = sb("st6b", [P, TT, 6])
        mvb = sb("mvb", [P, TT, 2])
        lnrb = sb("lnrb", [P, 6, TT])
        xf1 = sb("xf1", [P, TT, D])
        got = sb("got", [P, B, TT, TABW])
        hid = sb("hid", [P, B, TT, COMP])
        ex, u7, gate, eq, pref, hot_c, sel, hot_t = (
            sb(n, [P, NG]) for n in "ex u7 gate eq pref hot_c sel hot_t".split())
        step = sb("step", [P, NG, KNOTS])
        cell = sb("cell", [P, NG, KNOTS - 1])
        line = sb("line", [P, NG, KNOTS - 1])
        best = sb("best", [P, TT])
        hot = sb("hot", [P, TT, NTILE])
        hotT = sb("hotT", [P, 2 * P])

        gap = sb("gap", [P, 1])
        ident_b = sb("ident_b", [P, P], BF16)
        mask_b = sb("mask_b", [P, P], BF16)
        wabs = sb("wabs", [P, 4])
        beyond = sb("beyond", [P, 1], mybir.dt.int32)
        nmax = sb("nmax", [P, 2, TT * 4])
        nmax_b = sb("nmax_b", [P, 2, TT * 4], BF16)
        nparts = sb("nparts", [P, TT * 4, NP])
        shift = sb("shift", [4 * NP, T], BF16)
        nrt = sb("nrt", [P, 2])
        dk = sb("dk", [P, KNOTS - 1])
        comp = sb("comp", [P, 2, NT])
        mag = sb("mag", [P, NT])
        st6c = sb("st6c", [P, NT, 6])
        mvc = sb("mvc", [P, NT, 2])
        lnrc = sb("lnrc", [P, 6, NT])

        psS = psum("psS", [P, 2, SW])
        psO = psum("psO", [P, 2, 512])
        psA = psum("psA", [P, 512])
        psC = psum("psC", [P, 512])

        scratch = nc.dram_tensor("stacks", [B, 2, H, HD, 6, T], BF16, kind="Internal").ap()

        (const_in, w_in, x0_in, x1_in, xr_in, out_done, scr_done,
         wsc_ready, rope_ready, zeros_ready,
         stat1, mv1, ln1, r01, nw1, xn_ready, t1_done, xnT_done, z_done, z_copied, sq_done,
         ss_done, lnq, rq0, nwq, rq_done, zn_done, rope_a, rope_b, qkr_done,
         kt_done, p1_done, rest_done, p2_done, parts_done,
         s_ready, exp_done, masks_ready, v_moved, v_ready, pv_done, o_copied, ot_done, rec_done, on_done,
         op_done, onT_done, pr_done, x1_done,
         stat2, mv2, ln2, r02, nw2, xf1_ready, xf_stored, xt_done, xfT_done, sc_done, sc_copied,
         beyond_ready, smax_ready, smax_read, nmax_step, nmax_ready, shift_ps, shift_ready, shift_in,
         prep_dve, end_step, scaled, weighted, mag_ready, y_ready, ex_done, gate_step, u7_ready, line_step, line_ready, sel_ready, hot_ready, hot_done,
         hotT_ready, got_done, got_copied, hid_ready, gelu_done, prod_ready, comp_ready, tanh_done,
         stat3, mv3, ln3, r03, nw3, yn_ready, centred, beta_in, out_ready, last_ready) = [sem(n) for n in (
            "const_in w_in x0_in x1_in xr_in out_done scr_done "
            "wsc_ready rope_ready zeros_ready "
            "stat1 mv1 ln1 r01 nw1 xn_ready t1_done xnT_done z_done z_copied sq_done "
            "ss_done lnq rq0 nwq rq_done zn_done rope_a rope_b qkr_done "
            "kt_done p1_done rest_done p2_done parts_done "
            "s_ready exp_done masks_ready v_moved v_ready pv_done o_copied ot_done rec_done on_done "
            "op_done onT_done pr_done x1_done "
            "stat2 mv2 ln2 r02 nw2 xf1_ready xf_stored xt_done xfT_done sc_done sc_copied "
            "beyond_ready smax_ready smax_read nmax_step nmax_ready shift_ps shift_ready shift_in "
            "prep_dve end_step scaled weighted mag_ready y_ready ex_done gate_step u7_ready line_step line_ready sel_ready hot_ready hot_done "
            "hotT_ready got_done got_copied hid_ready gelu_done prod_ready comp_ready tanh_done "
            "stat3 mv3 ln3 r03 nw3 yn_ready centred beta_in out_ready last_ready").split()]
        stack_in = [sem(f"stack_in{j}") for j in range(NQ)]

        hidf = hid[:, :, :, :].rearrange("p b t n -> p (b t) n")
        gotf = got[:, :, :, :].rearrange("p b t n -> p (b t) n")
        prod0 = zn[:, :, :].rearrange("p t (a n) -> p (t a) n", n=COMP)
        prod1 = qkr[:, :, :, :].rearrange("p t k (a n) -> p (t k a) n", n=COMP)
        m01 = rest[:, :, :].rearrange("p a (t n) -> p a t n", n=GRID)
        xsf = xs[:, :, :, :].rearrange("p b t d -> p (b t) d")
        xff = xf[:, :, :, :].rearrange("p b t d -> p (b t) d")
        z4 = zn[:, :, :].rearrange("p t (k h d) -> p (t k) h d", k=2, h=H)
        b4 = sq[:, :, :].rearrange("p t (k h d) -> p (t k) h d", k=2, h=H)
        q4 = qkr[:, :, :, :].rearrange("p t k (h d) -> p (t k) h d", h=H)
        cw = cwt[:, :, :, :].rearrange("p t k d -> p (t k) d").unsqueeze(2)
        sw = swt[:, :, :, :].rearrange("p t k d -> p (t k) d").unsqueeze(2)
        ident = const[:, C_ID:C_ID + P]
        eps_ln = const[:, C_EPS:C_EPS + 1]
        eps_rms = const[:, C_EPS + 1:C_EPS + 2]
        block = ctx.enter_context(nc.Block())

        def over_batches(eng, body):
            for b in range(2):
                body(b)
            with eng.Fori(2, B - 3) as b:
                body(b)
            for b in range(B - 3, B):
                body(b)

        def either(eng, main):
            eng.wait_ge(beyond_ready, 1)
            far = eng.value_load(beyond[0:1, 0:1], min_val=0, max_val=1)
            with eng.If(far > 0):
                main(True)
            with eng.Else():
                main(False)

        def tiles_of(batches):
            return slice(batches[0] * TT, batches[1] * TT)

        def place(b):
            return b if isinstance(b, int) else 2

        def later(i, n):
            return i >= n if isinstance(i, int) else True

        def norm_bank(i):
            return psS[:, 0, 512 * i:512 * i + 512] if isinstance(i, int) and i < 2 else psA[:, :]

        def projection_bank(i, t):
            return (psA[:, :], psC[:, :], psO[:, 0], psO[:, 1])[t] if isinstance(i, int) and i < 2 else psA[:, :]

        def heads_bank(i, qk):
            if isinstance(i, int) and i == 0:
                return psS[:, 1, 512 * qk:512 * qk + 512]
            return psC[:, :] if isinstance(i, int) and i == 1 and qk == 1 else psA[:, :]

        @block.sync
        def _(sp):
            sp.dma_start(const[:, :], const_d).then_inc(const_in, 16)
            sp.dma_start(xs[:, 0], x_d[0].rearrange("(t p) d -> p t d", p=P)).then_inc(x0_in, 16)
            sp.dma_start(vec[:, :], vec_d.broadcast_to([P, NVEC])).then_inc(w_in, 16)
            sp.dma_start(wqkv[:, :], wqkv_d).then_inc(w_in, 16)
            sp.dma_start(xs[:, 1], x_d[1].rearrange("(t p) d -> p t d", p=P)).then_inc(x1_in, 16)
            sp.dma_start(sig[:, :], sig_d).then_inc(w_in, 16)
            sp.dma_start(wproj[:, :], wproj_d).then_inc(w_in, 16)
            sp.dma_start(wsc[:, NCL + NTILE:NSC], cw1_d).then_inc(w_in, 16)
            sp.dma_start(tab[0:NTILE, :], tab_d).then_inc(w_in, 16)
            sp.dma_start(tab[NTILE:P, :], tab_d).then_inc(w_in, 16)
            for i in range(2, B):
                sp.dma_start(xs[:, i], x_d[i].rearrange("(t p) d -> p t d", p=P)).then_inc(xr_in, 16)

            def store_parts(i):
                for qk in range(2):
                    sp.wait_ge(parts_done, i * 2 + (qk + 1))
                    rows = scratch[i, qk].rearrange("h d r t -> (h d) r t")
                    for first, n in ((0, 3), (3, 2), (5, 1)):
                        if qk == 0:
                            src = parts[:, 0, Q_PARTS[first]].unsqueeze(1).broadcast_to([P, n, T])
                        else:
                            src = parts[:, 1, K_PARTS[first]:K_PARTS[first] + n, :]
                        sp.dma_start(rows[:, first:first + n, :], src).then_inc(scr_done, 16)

            def load_stack(i, j):
                if later(i, 1):
                    sp.wait_ge(s_ready, (i - 1) * (NQ * SLOTS) + (j + 1) * SLOTS)
                for qk, st in ((0, stq), (1, stk)):
                    for hh in range(2):
                        h = 4 * j + 2 * hh
                        sp.dma_start(st[64 * hh:64 * hh + ROWS, j],
                                     scratch[i, qk, h:h + 2].rearrange("g d r t -> (d r) g t"))\
                          .then_inc(stack_in[j], 16)

            def load_stacks(i):
                sp.wait_ge(scr_done, (i + 1) * (6 * 16))
                for j in range(NQ):
                    load_stack(i, j)

            store_parts(0)
            sp.wait_ge(zeros_ready, 2)
            load_stacks(0)
            store_parts(1)

            def body(b):
                k = place(b)
                if k < B - 1:
                    load_stacks(b + 1)
                if k < B - 2:
                    store_parts(b + 2)

            over_batches(sp, body)
            for k, (lo, hi) in enumerate(CHUNKS):
                if k < 3:
                    sp.wait_ge(out_ready, k + 1)
                else:
                    sp.wait_ge(last_ready, k - 2)
                for i in range(lo, hi):
                    sp.dma_start(out_d[i].rearrange("(t p) d -> p t d", p=P), xs[:, i]).then_inc(out_done, 16)
            sp.wait_ge(out_done, B * 16)

        @block.tensor
        def _(pe):
            def transposes(dst, srcs):
                for t, s in enumerate(srcs):
                    ins = nc.tensor.transpose(dst[:, t * P:(t + 1) * P], s, ident)
                return ins

            def norm_transposed(i):
                pe.wait_ge(xn_ready, i + 1)
                if later(i, 2):
                    pe.wait_ge(rest_done, 2 * i)
                transposes(norm_bank(i), [xn[:, t, :] for t in range(TT)]).then_inc(t1_done, 1)

            def project(i, t):
                if t == 0:
                    pe.wait_ge(xnT_done, i + 1)
                if isinstance(i, int) and i < 2:
                    if i == 1:
                        pe.wait_ge(z_copied, t + 1)
                elif t > 0:
                    pe.wait_ge(z_copied, i * TT + t)
                nc.tensor.matmul(projection_bank(i, t)[:, 0:3 * D], xnT[:, t * P:(t + 1) * P], wqkv[:, :],
                                 start=True, stop=True).then_inc(z_done, 1)

            def qk_transposed(i, qk):
                if qk == 0:
                    pe.wait_ge(qkr_done, i + 1)
                    if later(i, 1):
                        pe.wait_ge(z_copied, (i + 1) * TT)
                    if later(i, 4):
                        pe.wait_ge(got_copied, 2 * i - 6)
                elif later(i, 2):
                    pe.wait_ge(rest_done, 2 * i + 1)
                transposes(heads_bank(i, qk), [qkr[:, t, qk, :] for t in range(TT)]).then_inc(kt_done, 1)

            def maxima(b, j):
                n = b * NQ + j
                pe.wait_ge(stack_in[j], (b + 1) * 64)
                if later(n, 1):
                    pe.wait_ge(exp_done, n * SLOTS - 1)
                for e in range(4 * TT):
                    c, qb = e // TT, e % TT
                    hh, gg = c // 2, c % 2
                    if later(n, 1) or e >= 2:
                        pe.wait_ge(smax_read, n * (4 * TT) + (e - 1))
                    bank = psS[:, j % 2, (e % 2) * 512:(e % 2) * 512 + 512]
                    nc.tensor.matmul(bank[:, 0:(qb + 1) * P],
                                     stq[64 * hh:64 * hh + ROWS, j, gg, qb * P:(qb + 1) * P],
                                     stk[64 * hh:64 * hh + ROWS, j, gg, 0:(qb + 1) * P], start=True, stop=False)
                    nc.tensor.matmul(bank[:, qb * P:(qb + 1) * P], mask_b[:, :], ident_b[:, :],
                                     start=False, stop=True).then_inc(smax_ready, 1)
                pe.wait_ge(nmax_ready, n + 1)
                for qb in range(TT):
                    ins = nc.tensor.transpose(psS[0:4 * NP, j % 2, qb * P:(qb + 1) * P],
                                              nparts[:, qb * 4:(qb + 1) * 4, :].rearrange("p c r -> p (c r)"), ident)
                ins.then_inc(shift_ps, 1)
                pe.wait_ge(shift_in, (n + 1) * 64)

            def scores(b, j, s):
                g = b * (NQ * SLOTS) + (j * SLOTS + s)
                if s == 0:
                    pe.wait_ge(stack_in[j], (b + 1) * 64)
                if later(g, 2):
                    pe.wait_ge(exp_done, g - 1)
                for c in (0, 2, 1, 3):
                    hh, gg = c // 2, c % 2
                    for kb in range(TT):
                        u, off = unit_of(kb, c)
                        if u != s:
                            continue
                        slot = psS[:, (j * SLOTS + s) % 2, :]
                        nc.tensor.matmul(slot[:, off:off + T - kb * P],
                                         stk[64 * hh:64 * hh + SROWS, j, gg, kb * P:(kb + 1) * P],
                                         stq[64 * hh:64 * hh + SROWS, j, gg, kb * P:T], start=True, stop=False)
                        ins = nc.tensor.matmul(slot[:, off:off + P], ident_b[:, :], mask_b[:, :],
                                               start=False, stop=True)
                ins.then_inc(s_ready, 1)

            def attend(b, j, kb):
                n = b * NQ + j
                if kb == 0:
                    pe.wait_ge(v_ready, n + 1)
                    if later(n, 2):
                        pe.wait_ge(o_copied, n - 1)
                    pe.wait_ge(exp_done, n * SLOTS + 4)
                if kb == 1:
                    pe.wait_ge(exp_done, n * SLOTS + 5)
                for c in range(4):
                    u, off = unit_of(kb, c)
                    ins = nc.tensor.matmul(psO[32 * c:32 * c + VW, j % 2, kb * P:T],
                                           vaug[:, kb, 4 * j + c, :],
                                           pt[:, j % 2, u * SW + off:u * SW + off + T - kb * P],
                                           start=(kb == 0), stop=(kb == TT - 1))
                if kb == TT - 1:
                    ins.then_inc(pv_done, 1)

            def quad_transposed(b, j, free, value):
                n = b * NQ + j
                pe.wait_ge(o_copied, n + 1)
                pe.wait_ge(free, value)
                transposes(psC, [oT[:, j % 2, t * P:(t + 1) * P] for t in range(TT)]).then_inc(ot_done, 1)

            def heads_transposed(i):
                pe.wait_ge(on_done, (i + 1) * NQ)
                transposes(psC, [on[:, t, :] for t in range(TT)]).then_inc(op_done, 1)

            def output_projection(i):
                pe.wait_ge(onT_done, i + 1)
                for t in range(TT):
                    ins = nc.tensor.matmul(psC[:, t * D:(t + 1) * D], turned[:, t * P:(t + 1) * P], wproj[:, :],
                                           start=True, stop=True)
                ins.then_inc(pr_done, 1)

            def router_transposed(i, free, value):
                pe.wait_ge(xf1_ready, i + 1)
                pe.wait_ge(free, value)
                transposes(psC, [xf1[:, t, :] for t in range(TT)]).then_inc(xt_done, 1)

            def router_scores(i):
                pe.wait_ge(xfT_done, i + 1)
                for t in range(TT):
                    ins = nc.tensor.matmul(psC[:, t * NSC:(t + 1) * NSC], turned[:, t * P:(t + 1) * P], wsc[:, :],
                                           start=True, stop=True)
                ins.then_inc(sc_done, 1)

            def hot_transposed(i):
                pe.wait_ge(hot_ready, i + 1)
                if isinstance(i, int) and i >= B - 4:
                    pe.wait_ge(rest_done, 2 * B)
                else:
                    pe.wait_ge(z_copied, (i + 5) * TT)
                if later(i, 1):
                    pe.wait_ge(got_copied, 2 * i)
                transposes(psA, [hot[:, 2 * u:2 * u + 2, :].rearrange("p t n -> p (t n)") for u in range(2)])\
                    .then_inc(hot_done, 1)

            def gather(i, a, bank=psA):
                if a == 0:
                    pe.wait_ge(hotT_ready, i + 1)
                elif bank is psA:
                    pe.wait_ge(got_copied, 2 * i + 1)
                else:
                    pe.wait_ge(sc_copied, B)
                half = slice(NTILE * a, NTILE * (a + 1))
                for u in range(2):
                    ins = nc.tensor.matmul(bank[:, u * 256:u * 256 + TABW], hotT[half, u * P:(u + 1) * P], tab[half, :],
                                           start=True, stop=True)
                ins.then_inc(got_done, 1)

            def body(b, exact):
                k = place(b)
                for s in range(NQ * SLOTS):
                    j = s // SLOTS
                    bb, jj = (b, j + 1) if j < NQ - 1 else (b + 1, 0)
                    if j < NQ - 1 or k < B - 1:
                        if exact and s % SLOTS == 0:
                            maxima(bb, jj)
                        scores(bb, jj, s % SLOTS)
                    if s % SLOTS > 0:
                        attend(b, j, (0, 2, 1, 3)[s % SLOTS - 1])
                    if k < B - 2:
                        if s == 1:
                            norm_transposed(b + 2)
                        if s in (3, 5, 7, 9):
                            project(b + 2, (s - 3) // 2)
                        if s == 17:
                            qk_transposed(b + 2, 0)
                        if s == 19:
                            qk_transposed(b + 2, 1)
                    if k >= 2:
                        if s == 11:
                            hot_transposed(b - 2)
                        if s in (13, 15):
                            gather(b - 2, (s - 13) // 2)
                    if k >= 1:
                        if s == 1:
                            quad_transposed(b - 1, 3, on_done, b * NQ - 1)
                        if s == 3:
                            heads_transposed(b - 1)
                        if s == 5:
                            output_projection(b - 1)
                        if s == 10:
                            router_transposed(b - 1, on_done, b * NQ + 1)
                        if s == 12:
                            router_scores(b - 1)
                    if s == 7:
                        quad_transposed(b, 0, *((x1_done, b) if k >= 1 else (rest_done, 4)))
                    if s == 14:
                        if k >= 1:
                            quad_transposed(b, 1, sc_copied, b)
                        else:
                            quad_transposed(b, 1, on_done, 1)
                    if s == 17:
                        quad_transposed(b, 2, on_done, b * NQ + 2)

            def last_ones():
                i = B - 1
                quad_transposed(i, 3, on_done, B * NQ - 1)
                heads_transposed(i)
                output_projection(i)
                router_transposed(i, x1_done, B)
                router_scores(i)
                hot_transposed(i - 1)
                gather(i - 1, 0)
                gather(i - 1, 1)
                hot_transposed(i)
                gather(i, 0)
                gather(i, 1, psC)

            pe.wait_ge(const_in, 16)
            pe.wait_ge(w_in, 7 * 16)
            for i in range(2):
                norm_transposed(i)
                for t in range(TT):
                    project(i, t)
            for i in range(2):
                qk_transposed(i, 0)
                qk_transposed(i, 1)
            pe.wait_ge(masks_ready, 1)
            pe.wait_ge(rest_done, 2)
            pe.wait_ge(wsc_ready, 1)
            pe.wait_ge(zeros_ready, 2)

            def main(exact):
                if exact:
                    maxima(0, 0)
                for s in range(SLOTS):
                    scores(0, 0, s)
                over_batches(pe, lambda b: body(b, exact))

            either(pe, main)
            last_ones()

        @block.scalar
        def _(act):
            def exp_tables():
                nc.scalar.preload_act_table_set("natural_log_exp_and_others")

            exp_tables()

            def rsqrt_start(out, tmp, in_, scale, eps, log_sem, done_sem, i):
                nc.scalar.activation(tmp, in_, ACT.Ln, bias=eps, scale=scale).then_inc(log_sem, 1)
                act.wait_ge(log_sem, i + 1)
                nc.scalar.activation(out, tmp, ACT.Exp, scale=-0.5).then_inc(done_sem, 1)

            def norm1(i):
                act.wait_ge(mv1, i + 1)
                rsqrt_start(lnr[:, 1, :], lnr[:, 0, :], mv[:, :, 1], 1.0, eps_ln, ln1, r01, i)

            def norm2(i):
                act.wait_ge(mv2, i + 1)
                rsqrt_start(lnrb[:, 1, :], lnrb[:, 0, :], mvb[:, :, 1], 1.0, eps_ln, ln2, r02, i)

            def norm_heads(i):
                act.wait_ge(ss_done, 2 * i + 2)
                rsqrt_start(rr[:, 1, :], rr[:, 5, :], rr[:, 0, :], 1.0 / HD, eps_rms, lnq, rq0, i)

            def copy_projected(i, t):
                act.wait_ge(z_done, i * TT + (t + 1))
                if t == 0 and later(i, 1):
                    act.wait_ge(zn_done, i)
                    act.wait_ge(v_moved, i)
                bank = projection_bank(i, t)
                nc.scalar.activation(zqk[:, t, :], bank[:, 0:2 * D], ACT.Copy)
                nc.scalar.activation(vtok[:, 0, t, :], bank[:, 2 * D:3 * D], ACT.Copy).then_inc(z_copied, 1)

            def exponentials(b, j, s):
                g = b * (NQ * SLOTS) + (j * SLOTS + s)
                act.wait_ge(s_ready, g + 1)
                if s == 0 and later(b * NQ + j, 2):
                    act.wait_ge(pv_done, b * NQ + (j - 1))
                nc.scalar.activation(pt[:, j % 2, s * SW:(s + 1) * SW], psS[:, (j * SLOTS + s) % 2, :],
                                     ACT.Exp).then_inc(exp_done, 1)

            def copy_heads(i):
                act.wait_ge(op_done, i + 1)
                nc.scalar.activation(turned[:, :], psC[:, :], ACT.Copy).then_inc(onT_done, 1)

            def copy_router(i):
                act.wait_ge(xt_done, i + 1)
                nc.scalar.activation(turned[:, :], psC[:, :], ACT.Copy).then_inc(xfT_done, 1)

            def gate_exp(i, r):
                if r == 0:
                    act.wait_ge(sc_copied, i + 1)
                    if later(i, 1):
                        act.wait_ge(u7_ready, 2 * i)
                    nc.scalar.activation(ex[:, :].rearrange("p (t c) -> p t c", c=NCL), sc[:, :, 0:NCL], ACT.Exp,
                                         scale=nrt[:, 0:1]).then_inc(ex_done, 1)
                else:
                    act.wait_ge(sel_ready, i + 1)
                    nc.scalar.activation(ex[:, :], sel[:, :], ACT.Exp, scale=nrt[:, 0:1]).then_inc(ex_done, 1)

            def copy_hot(i):
                act.wait_ge(hot_done, i + 1)
                nc.scalar.activation(hotT[:, :], psA[:, 0:2 * P], ACT.Copy).then_inc(hotT_ready, 1)

            def copy_got(i, a, bank=psA):
                act.wait_ge(got_done, 2 * i + (a + 1))
                src = bank[:, :].rearrange("p (t n) -> p t n", t=2)
                nc.scalar.activation(got[:, i, a:TT:2, :], src[:, :, 0:TABW], ACT.Copy).then_inc(got_copied, 1)

            def gelu(g):
                c = tiles_of(GROUPS[g])
                act.wait_ge(hid_ready, GROUPS[g][1])
                nc.scalar.activation(hidf[:, c, :], hidf[:, c, :], ACT.Gelu).then_inc(gelu_done, 1)

            def tanh(g):
                c = tiles_of(GROUPS[g])
                act.wait_ge(comp_ready, g + 1)
                nc.scalar.activation(comp[:, :, c], comp[:, :, c], ACT.Tanh).then_inc(tanh_done, 1)

            def last_norm(k):
                c = tiles_of(CHUNKS[k])
                act.wait_ge(mv3, k + 1)
                rsqrt_start(lnrc[:, 1, c], lnrc[:, 0, c], mvc[:, c, 1], 1.0, eps_ln, ln3, r03, k)

            def load_shift(b, j):
                n = b * NQ + j
                act.wait_ge(shift_ready, n + 1)
                for c in range(4):
                    hh, gg = c // 2, c % 2
                    act.dma_start(stq[64 * hh + ROWS:64 * hh + SROWS, j, gg, :], shift[c * NP:(c + 1) * NP, :])\
                       .then_inc(shift_in, 16)

            def body(b, exact):
                k = place(b)
                for s in range(NQ * SLOTS):
                    j = s // SLOTS
                    bb, jj = (b, j + 1) if j < NQ - 1 else (b + 1, 0)
                    if j < NQ - 1 or k < B - 1:
                        if exact and s % SLOTS == 0:
                            load_shift(bb, jj)
                        exponentials(bb, jj, s % SLOTS)
                    if k < B - 2:
                        if s in (3, 5, 7, 9):
                            copy_projected(b + 2, (s - 3) // 2)
                        if s == 11:
                            norm_heads(b + 2)
                    if k < B - 3 and s == 8:
                        norm1(b + 3)
                    if k >= 2:
                        if s == 12:
                            copy_hot(b - 2)
                        if s in (13, 15):
                            copy_got(b - 2, (s - 13) // 2)
                    if k >= 1:
                        if s == 4:
                            copy_heads(b - 1)
                        if s == 7:
                            norm2(b - 1)
                        if s == 11:
                            copy_router(b - 1)
                        if s == 14:
                            gate_exp(b - 1, 0)
                        if s == 19 and k < B - 1:
                            gate_exp(b - 1, 1)
                    if (k, s) == (B - 2, 0):
                        gelu(0)
                        exp_tables()
                    if (k, s) == (B - 2, 18):
                        tanh(0)
                        gelu(1)
                        exp_tables()
                    if (k, s) == (B - 1, 9):
                        last_norm(0)
                    if (k, s) == (B - 1, 14):
                        tanh(1)
                        gelu(2)
                        exp_tables()

            def last_ones():
                i = B - 1
                copy_heads(i)
                gate_exp(i - 1, 1)
                last_norm(1)
                norm2(i)
                copy_router(i)
                copy_hot(i - 1)
                gate_exp(i, 0)
                copy_got(i - 1, 0)
                copy_got(i - 1, 1)
                gelu(3)
                nc.scalar.preload_act_table_set("exp_and_others")
                tanh(2)
                gate_exp(i, 1)
                tanh(3)
                exp_tables()
                last_norm(2)
                copy_hot(i)
                copy_got(i, 0)
                copy_got(i, 1, psC)
                last_norm(3)
                last_norm(4)

            act.wait_ge(const_in, 16)
            norm1(0)
            norm1(1)
            for t in range(TT):
                copy_projected(0, t)
            norm_heads(0)
            for t in range(TT):
                copy_projected(1, t)
            norm_heads(1)
            norm1(2)

            def main(exact):
                if exact:
                    load_shift(0, 0)
                for s in range(SLOTS):
                    exponentials(0, 0, s)
                over_batches(act, lambda b: body(b, exact))

            either(act, main)
            last_ones()

        @block.vector
        def _(dve):
            ncv = nc.vector

            def prepare():
                dve.wait_ge(const_in, 16)
                dve.wait_ge(w_in, 7 * 16)
                n = [0]

                def link(ins):
                    n[0] += 1
                    ins.then_inc(prep_dve, 1)
                    dve.wait_ge(prep_dve, n[0])
                ncv.tensor_scalar(sg[:, 0], sig[:, :], 0.3, None, ALU.is_gt)
                link(ncv.tensor_scalar(sg[:, 1], sig[:, :], -0.3, None, ALU.is_lt))
                link(ncv.tensor_tensor(sg[:, 2], sg[:, 0], sg[:, 1], ALU.subtract))
                link(ncv.tensor_tensor(sg[:, 0], sg[:, 2], sig[:, :], ALU.subtract))
                link(ncv.tensor_tensor(wsc[:, NCL:NCL + NTILE], sig[:, :], sg[:, 0], ALU.add))
                tiles = wsc[:, NCL:NCL + NTILE].rearrange("p (c t) -> p t c", t=TPC)
                link(ncv.tensor_tensor(csum[:, 0], tiles[:, 0], tiles[:, 1], ALU.add))
                for t in range(2, TPC):
                    link(ncv.tensor_tensor(csum[:, 0], csum[:, 0], tiles[:, t], ALU.add))
                ncv.tensor_scalar(csum[:, 1], csum[:, 0], 0.0, None, ALU.is_gt)
                link(ncv.tensor_scalar(sg[:, 0, 0:NCL], csum[:, 0], 0.0, None, ALU.is_lt))
                ncv.tensor_tensor(wsc[:, 0:NCL], csum[:, 1], sg[:, 0, 0:NCL], ALU.subtract).then_inc(wsc_ready, 1)
                link(ncv.tensor_scalar(nrt[:, 0:1], vec[:, V_TEMP:V_TEMP + 1], 1e-6, None, ALU.add))
                link(ncv.reciprocal(nrt[:, 1:2], nrt[:, 0:1]))
                ncv.tensor_scalar(nrt[:, 0:1], nrt[:, 1:2], -1.0, None, ALU.mult)
                ncv.tensor_tensor(dk[:, :], vec[:, V_KNOT + 1:V_KNOT + KNOTS], vec[:, V_KNOT:V_KNOT + KNOTS - 1],
                                  ALU.subtract)
                ncv.tensor_reduce(wabs[:, 0:1], vec[:, V_QW:V_QW + HD], axis=AX.X, op=ALU.max,
                                  apply_absolute_value=True)
                link(ncv.tensor_reduce(wabs[:, 1:2], vec[:, V_KW:V_KW + HD], axis=AX.X, op=ALU.max,
                                       apply_absolute_value=True))
                link(ncv.tensor_tensor(wabs[:, 2:3], wabs[:, 0:1], wabs[:, 1:2], ALU.mult))
                ncv.tensor_scalar(beyond[:, :], wabs[:, 2:3], SAFE / (HD * SCALE), None, ALU.is_gt)\
                   .then_inc(beyond_ready, 1)
                ncv.tensor_copy(ident_b[:, :], ident)
                ncv.tensor_copy(mask_b[:, :], const[:, C_MASK:C_MASK + P]).then_inc(masks_ready, 1)
                ncv.tensor_scalar(wsq[:, 0], vec[:, V_QW:V_QW + HD], SCALE, None, ALU.mult)
                link(ncv.tensor_copy(wsq[:, 1], vec[:, V_KW:V_KW + HD]))
                cos = const[:, C_COS:C_COS + TT * HD].rearrange("p (t d) -> p t d", t=TT)
                sin = const[:, C_SIN:C_SIN + TT * HD].rearrange("p (t d) -> p t d", t=TT)
                half = HD // 2
                for qk in range(2):
                    w = wsq[:, qk, :].unsqueeze(1)
                    ncv.tensor_tensor(cwt[:, :, qk, :], cos, w.broadcast_to([P, TT, HD]), ALU.mult)
                    ncv.tensor_tensor(swt[:, :, qk, 0:half], sin[:, :, 0:half],
                                      w[:, :, half:HD].broadcast_to([P, TT, half]), ALU.mult)
                    ins = ncv.tensor_tensor(swt[:, :, qk, half:HD], sin[:, :, half:HD],
                                            w[:, :, 0:half].broadcast_to([P, TT, half]), ALU.mult)
                ins.then_inc(rope_ready, 1)

            def carry():
                ncv.memset(gap[:, :], 0.0)

            def stats(src, st, m, stat_sem, mv_sem, i):
                for t in range(TT):
                    ins = ncv.bn_stats(st[:, t, :], src[:, t, :])
                ins.then_inc(stat_sem, 1)
                dve.wait_ge(stat_sem, i + 1)
                carry()
                for t in range(TT):
                    ins = ncv.bn_aggr(m[:, t, :], st[:, t, :])
                ins.then_inc(mv_sem, 1)

            def refine(v_in, scale, eps, r, buf, nw, i):
                ncv.tensor_scalar(buf[:, 2, :], v_in, scale, eps, ALU.mult, ALU.add)
                ncv.tensor_tensor(buf[:, 3, :], r, r, ALU.mult).then_inc(nw, 1)
                dve.wait_ge(nw, 3 * i + 1)
                ncv.scalar_tensor_tensor(buf[:, 2, :], buf[:, 2, :], -0.5, buf[:, 3, :], ALU.mult, ALU.mult)\
                   .then_inc(nw, 1)
                dve.wait_ge(nw, 3 * i + 2)
                return ncv.scalar_tensor_tensor(buf[:, 4, :], buf[:, 2, :], 1.5, r, ALU.add, ALU.mult)\
                    .then_inc(nw, 1)

            def norm1_stats(i):
                if isinstance(i, int) and i < 2:
                    dve.wait_ge((x0_in, x1_in)[i], 16)
                else:
                    dve.wait_ge(xr_in, 16 * (B - 2))
                stats(xs[:, i], st6, mv, stat1, mv1, i)

            def norm1(i):
                dve.wait_ge(r01, i + 1)
                refine(mv[:, :, 1], 1.0, EPS_LN, lnr[:, 1, :], lnr, nw1, i)
                dve.wait_ge(nw1, 3 * i + 3)
                if later(i, 1):
                    dve.wait_ge(t1_done, i)
                for t in range(TT):
                    ins = ncv.tensor_scalar(xn[:, t, :], xs[:, i, t, :], mv[:, t, 0:1], lnr[:, 4, t:t + 1],
                                            ALU.subtract, ALU.mult)
                ins.then_inc(xn_ready, 1)

            def copy_norm(i):
                dve.wait_ge(t1_done, i + 1)
                if later(i, 1):
                    dve.wait_ge(z_done, i * TT)
                ncv.tensor_copy(xnT[:, :], norm_bank(i)).then_inc(xnT_done, 1)

            def head_sums(i, a):
                ts = slice(2 * a, 2 * a + 2)
                dve.wait_ge(z_copied, i * TT + (2 * a + 2))
                if later(i, 1):
                    dve.wait_ge(ss_done, 2 * i + (a - 1))
                ncv.tensor_tensor(sq[:, ts, :], zqk[:, ts, :], zqk[:, ts, :], ALU.mult).then_inc(sq_done, 1)
                dve.wait_ge(sq_done, 2 * i + (a + 1))
                if later(i, 1):
                    dve.wait_ge(nwq, 3 * i)
                n = 2 * 2 * H
                ncv.tensor_reduce(rr[:, 0, a * n:(a + 1) * n], sq[:, ts, :].rearrange("p t (g d) -> p (t g) d", d=HD),
                                  axis=AX.X, op=ALU.add).then_inc(ss_done, 1)

            def head_norm(i):
                dve.wait_ge(rq0, i + 1)
                if later(i, 1):
                    dve.wait_ge(zn_done, i)
                refine(rr[:, 0, :], 1.0 / HD, EPS_RMS, rr[:, 1, :], rr, nwq, i)
                dve.wait_ge(nwq, 3 * i + 3)
                if later(i, 1):
                    dve.wait_ge(rope_b, i)
                    dve.wait_ge(qkr_done, i)
                ncv.tensor_tensor(zn[:, :, :].rearrange("p t (g d) -> p (t g) d", d=HD),
                                  zqk[:, :, :].rearrange("p t (g d) -> p (t g) d", d=HD),
                                  rr[:, 4, :].unsqueeze(2).broadcast_to([P, TT * 2 * H, HD]), ALU.mult)\
                   .then_inc(zn_done, 1)

            def rotate_cos(i):
                dve.wait_ge(zn_done, i + 1)
                if later(i, 1):
                    dve.wait_ge(kt_done, 2 * i)
                ncv.tensor_tensor(q4, z4, cw.broadcast_to([P, 2 * TT, H, HD]), ALU.mult).then_inc(rope_a, 1)

            def rotate_sum(i):
                dve.wait_ge(rope_a, i + 1)
                dve.wait_ge(rope_b, i + 1)
                ncv.tensor_tensor(q4, q4, b4, ALU.add).then_inc(qkr_done, 1)

            def split(i, qk):
                dve.wait_ge(kt_done, 2 * i + (qk + 1))
                if qk == 0 and later(i, 1):
                    dve.wait_ge(scr_done, 6 * 16 * i)
                    dve.wait_ge(parts_done, 2 * i)
                bank = heads_bank(i, qk)
                ncv.tensor_copy(parts[:, qk, 0, :], bank).then_inc(p1_done, 1)
                dve.wait_ge(p1_done, 2 * i + (qk + 1))
                ncv.tensor_tensor(rest[:, qk, :], bank, parts[:, qk, 0, :], ALU.subtract).then_inc(rest_done, 1)
                dve.wait_ge(rest_done, 2 * i + (qk + 1))
                ncv.tensor_copy(parts[:, qk, 1, :], rest[:, qk, :]).then_inc(p2_done, 1)

            def maxima(b, j):
                n = b * NQ + j
                for e in range(4 * TT):
                    c, qb = e // TT, e % TT
                    dve.wait_ge(smax_ready, n * (4 * TT) + (e + 1))
                    if e == 0 and later(n, 1):
                        dve.wait_ge(nmax_ready, n)
                    ncv.tensor_reduce(nmax[:, 0, qb * 4 + c:qb * 4 + c + 1],
                                      psS[:, j % 2, (e % 2) * 512:(e % 2) * 512 + (qb + 1) * P],
                                      axis=AX.X, op=ALU.max, negate=True).then_inc(smax_read, 1)
                dve.wait_ge(smax_read, (n + 1) * (4 * TT))
                if later(n, 1):
                    dve.wait_ge(shift_ps, n)
                for r in range(NP):
                    if r < NP - 1:
                        ncv.tensor_copy(nmax_b[:, r, :], nmax[:, r, :]).then_inc(nmax_step, 1)
                        dve.wait_ge(nmax_step, n * 4 + (2 * r + 1))
                        ncv.tensor_copy(nparts[:, :, r], nmax_b[:, r, :])
                        dst = nmax[:, 1, :] if r == 0 else nparts[:, :, 2]
                        ins = ncv.tensor_tensor(dst, nmax[:, r, :], nmax_b[:, r, :], ALU.subtract)
                        ins.then_inc(nmax_step, 1)
                        dve.wait_ge(nmax_step, n * 4 + (2 * r + 2))
                ncv.memset(gap[:, :], 0.0).then_inc(nmax_ready, 1)
                dve.wait_ge(shift_ps, n + 1)
                if later(n, 1):
                    dve.wait_ge(shift_in, n * 64)
                ncv.tensor_copy(shift[:, :], psS[0:4 * NP, j % 2, 0:512]).then_inc(shift_ready, 1)

            def copy_quad(b, j):
                n = b * NQ + j
                dve.wait_ge(pv_done, n + 1)
                if later(n, 2):
                    dve.wait_ge(ot_done, n - 1)
                ncv.tensor_copy(oT[:, j % 2, :], psO[:, j % 2, :]).then_inc(o_copied, 1)

            def normalise(b, j):
                n = b * NQ + j
                dve.wait_ge(ot_done, n + 1)
                o = psC[:, :].rearrange("p (t c w) -> p t c w", t=TT, w=VW)
                ncv.reciprocal(rec[:, :, :], o[:, :, :, HD]).then_inc(rec_done, 1)
                dve.wait_ge(rec_done, n + 1)
                if j == 0 and later(b, 1):
                    dve.wait_ge(op_done, b)
                ncv.tensor_tensor(on[:, :, 32 * j:32 * j + 32].rearrange("p t (c d) -> p t c d", d=HD),
                                  o[:, :, :, 0:HD], rec[:, :, :].unsqueeze(3).broadcast_to([P, TT, 4, HD]),
                                  ALU.mult).then_inc(on_done, 1)

            def residual(i):
                dve.wait_ge(pr_done, i + 1)
                ncv.tensor_tensor(xs[:, i], psC[:, :].rearrange("p (t d) -> p t d", t=TT), xs[:, i], ALU.add)\
                   .then_inc(x1_done, 1)

            def norm2_stats(i):
                dve.wait_ge(x1_done, i + 1)
                carry()
                stats(xs[:, i], st6b, mvb, stat2, mv2, i)

            def norm2(i):
                dve.wait_ge(r02, i + 1)
                refine(mvb[:, :, 1], 1.0, EPS_LN, lnrb[:, 1, :], lnrb, nw2, i)
                dve.wait_ge(nw2, 3 * i + 3)
                if later(i, 1):
                    dve.wait_ge(xt_done, i)
                    dve.wait_ge(xf_stored, i)
                for t in range(TT):
                    ins = ncv.tensor_scalar(xf1[:, t, :], xs[:, i, t, :], mvb[:, t, 0:1], lnrb[:, 4, t:t + 1],
                                            ALU.subtract, ALU.mult)
                ins.then_inc(xf1_ready, 1)

            def copy_scores(i):
                dve.wait_ge(sc_done, i + 1)
                if later(i, 1):
                    dve.wait_ge(hid_ready, i)
                    dve.wait_ge(ex_done, 2 * i)
                ncv.tensor_copy(sc[:, :, :].rearrange("p t n -> p (t n)"), psC[:, 0:TT * NSC]).then_inc(sc_copied, 1)

            def link(ins, i, n):
                ins.then_inc(gate_step, 1)
                dve.wait_ge(gate_step, i * LINKS + n)

            def gates_start(i, r):
                n = r * 12
                dve.wait_ge(ex_done, 2 * i + (r + 1))
                link(ncv.tensor_scalar(ex[:, :], ex[:, :], 1.0, None, ALU.add), i, n + 1)
                link(ncv.reciprocal(gate[:, :], ex[:, :]), i, n + 2)
                ncv.tensor_scalar(u7[:, :], gate[:, :], float(KNOTS - 1), None, ALU.mult).then_inc(u7_ready, 1)

            def gates_finish(i, r, dst):
                n = r * 12
                shape = [P, NG, KNOTS]
                dve.wait_ge(u7_ready, 2 * i + (r + 1))
                link(ncv.tensor_tensor(step[:, :, :], u7[:, :].unsqueeze(2).broadcast_to(shape),
                                       const[:, C_STEP:C_STEP + KNOTS].unsqueeze(1).broadcast_to(shape),
                                       ALU.is_ge), i, n + 3)
                link(ncv.tensor_tensor(cell[:, :, :], step[:, :, 0:KNOTS - 1], step[:, :, 1:KNOTS], ALU.subtract),
                     i, n + 4)
                dve.wait_ge(line_ready, 2 * i + (r + 1))
                link(ncv.tensor_tensor(cell[:, :, :], cell[:, :, :], line[:, :, :], ALU.mult), i, n + 5)
                link(ncv.tensor_reduce(gate[:, :], cell[:, :, :], axis=AX.X, op=ALU.add), i, n + 6)
                g3, e3, p3, d3 = (a[:, :].rearrange("p (t c) -> p t c", c=NCL) for a in (gate, eq, pref, dst))
                each = best[:, :].unsqueeze(2).broadcast_to([P, TT, NCL])
                link(ncv.tensor_reduce(best[:, :], g3, axis=AX.X, op=ALU.max), i, n + 7)
                link(ncv.tensor_tensor(e3, g3, each, ALU.is_ge), i, n + 8)
                link(ncv.tensor_tensor(p3, e3, const[:, C_PREF:C_PREF + 8].unsqueeze(1).broadcast_to([P, TT, NCL]),
                                       ALU.mult), i, n + 9)
                link(ncv.tensor_reduce(best[:, :], p3, axis=AX.X, op=ALU.max), i, n + 10)
                link(ncv.tensor_tensor(d3, p3, each, ALU.is_equal), i, n + 11)

            def choose_cluster(i):
                gates_finish(i, 0, hot_c)
                c3 = hot_c[:, :].rearrange("p (t c) -> p t c", c=NCL)
                s4 = step[:, :, :].rearrange("p (t a) c -> p t a c", t=TT)
                link(ncv.tensor_tensor(s4, sc[:, :, NCL:NCL + NTILE].rearrange("p t (c a) -> p t a c", c=NCL),
                                       c3.unsqueeze(2).broadcast_to([P, TT, TPC, NCL]), ALU.mult), i, 12)
                ncv.tensor_reduce(sel[:, :].rearrange("p (t a) -> p t a", a=TPC), s4, axis=AX.X, op=ALU.add)\
                   .then_inc(sel_ready, 1)

            def choose_tile(i):
                gates_finish(i, 1, hot_t)
                c3 = hot_c[:, :].rearrange("p (t c) -> p t c", c=NCL)
                t3 = hot_t[:, :].rearrange("p (t c) -> p t c", c=NCL)
                if later(i, 1):
                    dve.wait_ge(hot_done, i)
                ncv.tensor_tensor(hot[:, :, :].rearrange("p t (c a) -> p t c a", c=NCL),
                                  c3.unsqueeze(3).broadcast_to([P, TT, NCL, TPC]),
                                  t3.unsqueeze(2).broadcast_to([P, TT, NCL, TPC]), ALU.mult).then_inc(hot_ready, 1)

            n = [0]

            def chain(ins):
                n[0] += 1
                ins.then_inc(end_step, 1)
                dve.wait_ge(end_step, n[0])

            def compress(g):
                c = tiles_of(GROUPS[g])
                dve.wait_ge(prod_ready, 2 * g + 2)
                ncv.tensor_reduce(comp[:, 0, c], prod0[:, c, :], axis=AX.X, op=ALU.add)
                chain(ncv.tensor_reduce(comp[:, 1, c], prod1[:, c, :], axis=AX.X, op=ALU.add))
                shape = [P, 2, c.stop - c.start]
                ncv.tensor_tensor(comp[:, :, c], comp[:, :, c],
                                  vec[:, V_B2:V_B2 + 2].unsqueeze(2).broadcast_to(shape), ALU.add)\
                   .then_inc(comp_ready, 1)

            def splines(g):
                c = tiles_of(GROUPS[g])
                m0, m1, m = m01[:, 0, c], m01[:, 1, c], mag[:, c]
                dve.wait_ge(tanh_done, g + 1)
                dve.wait_ge(got_copied, 2 * GROUPS[g][1])
                if g == 0:
                    dve.wait_ge(parts_done, 2 * B)
                w1 = gotf[:, c, 0:2 * GRID].rearrange("p t (a n) -> p a t n", a=2)
                for a in range(2):
                    ins = ncv.tensor_tensor(m01[:, a, c], w1[:, a],
                                            comp[:, a, c].unsqueeze(2).broadcast_to([P, c.stop - c.start, GRID]),
                                            ALU.mult)
                chain(ins)
                chain(ncv.tensor_tensor(m0, m0, m1, ALU.add))
                chain(ncv.tensor_tensor(m0, m0, gotf[:, c, 2 * GRID:3 * GRID], ALU.add))
                chain(ncv.tensor_scalar(m0, m0, 0.0, None, ALU.max))
                chain(ncv.tensor_tensor(m1, m0, gotf[:, c, 3 * GRID:4 * GRID], ALU.mult))
                chain(ncv.tensor_reduce(m, m1, axis=AX.X, op=ALU.add))
                chain(ncv.tensor_tensor(m, m, gotf[:, c, 4 * GRID], ALU.add))
                ncv.tensor_scalar(m, m, vec[:, V_OS:V_OS + 1], None, ALU.mult).then_inc(mag_ready, 1)

            def spline_out(k):
                c = tiles_of(CHUNKS[k])
                dve.wait_ge(mag_ready, k)
                for t in range(c.start, c.stop):
                    ins = ncv.scalar_tensor_tensor(xff[:, t, :], gotf[:, t, 4 * GRID + 1:TABW], mag[:, t:t + 1],
                                                   xff[:, t, :], ALU.mult, ALU.add)
                ins.then_inc(y_ready, 1)

            def end_stats(k):
                c = tiles_of(CHUNKS[k])
                dve.wait_ge(y_ready, k + 1)
                for t in range(c.start, c.stop):
                    ins = ncv.bn_stats(st6c[:, t, :], xff[:, t, :])
                ins.then_inc(stat3, 1)
                dve.wait_ge(stat3, k + 1)
                for t in range(c.start, c.stop):
                    ins = ncv.bn_aggr(mvc[:, t, :], st6c[:, t, :])
                ins.then_inc(mv3, 1)

            def norm3(k):
                c = tiles_of(CHUNKS[k])
                dve.wait_ge(r03, k + 1)
                refine(mvc[:, c, 1], 1.0, EPS_LN, lnrc[:, 1, c], lnrc[:, :, c], nw3, k)
                dve.wait_ge(nw3, 3 * k + 3)
                for t in range(c.start, c.stop):
                    ins = ncv.tensor_scalar(xff[:, t, :], xff[:, t, :], mvc[:, t, 0:1], lnrc[:, 4, t:t + 1],
                                            ALU.subtract, ALU.mult)
                ins.then_inc(yn_ready, 1)

            def centre(k):
                c = tiles_of(CHUNKS[k])
                dve.wait_ge(mv3, k + 1)
                for t in range(c.start, c.stop):
                    ins = ncv.scalar_tensor_tensor(xff[:, t, :], xff[:, t, :], mvc[:, t, 0:1],
                                                   vec[:, V_GAM:V_GAM + D], ALU.subtract, ALU.mult)
                ins.then_inc(centred, 1)

            def finish(k):
                c = tiles_of(CHUNKS[k])
                dve.wait_ge(r03, k + 1)
                refine(mvc[:, c, 1], 1.0, EPS_LN, lnrc[:, 1, c], lnrc[:, :, c], nw3, k)
                dve.wait_ge(nw3, 3 * k + 3)
                dve.wait_ge(centred, k - 2)
                dve.wait_ge(beta_in, k + 1)
                for t in range(c.start, c.stop):
                    ins = ncv.scalar_tensor_tensor(xsf[:, t, :], xff[:, t, :], lnrc[:, 4, t:t + 1], xsf[:, t, :],
                                                   ALU.mult, ALU.add)
                ins.then_inc(last_ready, 1)

            def body(b, exact):
                k = place(b)
                for s in range(NQ * SLOTS):
                    j = s // SLOTS
                    bb, jj = (b, j + 1) if j < NQ - 1 else (b + 1, 0)
                    if exact and s % SLOTS == 0 and (j < NQ - 1 or k < B - 1):
                        maxima(bb, jj)
                    if s == 0:
                        if k >= 1:
                            copy_quad(b - 1, 3)
                        if k >= 2:
                            gates_start(b - 2, 1)
                    if s == 1:
                        if k < B - 2:
                            copy_norm(b + 2)
                        if k >= 1:
                            normalise(b - 1, 3)
                    if s == 3 and k >= 2:
                        choose_tile(b - 2)
                    if s == 5:
                        copy_quad(b, 0)
                        if k >= 1:
                            residual(b - 1)
                            norm2_stats(b - 1)
                        if k < B - 2:
                            head_sums(b + 2, 0)
                    if s == 7:
                        if k < B - 3:
                            norm1_stats(b + 3)
                        normalise(b, 0)
                    if s == 8 and k >= 1:
                        norm2(b - 1)
                    if s == 9:
                        if k < B - 2:
                            head_sums(b + 2, 1)
                        if k < B - 3:
                            norm1(b + 3)
                    if s == 10:
                        copy_quad(b, 1)
                    if s == 11 and k < B - 2:
                        head_norm(b + 2)
                        rotate_cos(b + 2)
                    if s == 13 and k >= 1:
                        copy_scores(b - 1)
                    if s == 15:
                        normalise(b, 1)
                        if k >= 1:
                            gates_start(b - 1, 0)
                        copy_quad(b, 2)
                        if k < B - 2:
                            rotate_sum(b + 2)
                    if s == 16 and 1 <= k < B - 1:
                        choose_cluster(b - 1)
                    if s == 18:
                        if k < B - 2:
                            split(b + 2, 0)
                        normalise(b, 2)
                    if s == 19 and k < B - 2:
                        split(b + 2, 1)
                    if (k, s) == (B - 2, 8):
                        compress(0)
                    if (k, s) == (B - 1, 0):
                        splines(0)
                    if (k, s) == (B - 1, 8):
                        end_stats(0)
                    if (k, s) == (B - 1, 10):
                        compress(1)
                    if (k, s) == (B - 1, 13):
                        norm3(0)

            def last_ones():
                i = B - 1
                copy_quad(i, 3)
                choose_cluster(i - 1)
                normalise(i, 3)
                gates_start(i - 1, 1)
                splines(1)
                end_stats(1)
                residual(i)
                norm2_stats(i)
                norm2(i)
                choose_tile(i - 1)
                copy_scores(i)
                gates_start(i, 0)
                norm3(1)
                choose_cluster(i)
                compress(2)
                gates_start(i, 1)
                end_stats(2)
                compress(3)
                choose_tile(i)
                norm3(2)
                splines(2)
                spline_out(3)
                end_stats(3)
                centre(3)
                splines(3)
                spline_out(4)
                end_stats(4)
                finish(3)
                centre(4)
                finish(4)

            norm1_stats(0)
            norm1(0)
            copy_norm(0)
            norm1_stats(1)
            prepare()
            norm1(1)
            head_sums(0, 0)
            head_sums(0, 1)
            copy_norm(1)
            head_norm(0)
            rotate_cos(0)
            rotate_sum(0)
            split(0, 0)
            split(0, 1)
            head_sums(1, 0)
            head_sums(1, 1)
            head_norm(1)
            rotate_cos(1)
            norm1_stats(2)
            rotate_sum(1)
            split(1, 0)
            split(1, 1)
            norm1(2)

            def main(exact):
                n[0] = 0
                if exact:
                    maxima(0, 0)
                over_batches(dve, lambda b: body(b, exact))

            either(dve, main)
            last_ones()

        @block.gpsimd
        def _(pool):
            ncg = nc.gpsimd
            one = const[:, C_J + 1:C_J + 2].unsqueeze(1)
            ncg.memset(stk[:, :, :, :], 1.0)
            ncg.memset(stq[:, :, :, :], 0.0)
            ncg.memset(vaug[:, :, :, :], 0.0).then_inc(zeros_ready, 1)
            pool.wait_ge(const_in, 16)
            pool.wait_ge(zeros_ready, 1)
            ncg.memset(vaug[:, :, :, HD:HD + 1], 1.0).then_inc(zeros_ready, 1)
            pool.wait_ge(zeros_ready, 2)

            def rotate_sin(i):
                pool.wait_ge(zn_done, i + 1)
                if later(i, 1):
                    pool.wait_ge(qkr_done, i)
                half = HD // 2
                for a, c in ((0, half), (half, 0)):
                    ins = ncg.tensor_tensor(b4[:, :, :, a:a + half], z4[:, :, :, c:c + half],
                                            sw[:, :, :, a:a + half].broadcast_to([P, 2 * TT, H, half]), ALU.mult)
                ins.then_inc(rope_b, 1)

            def split(i, qk):
                n = 2 * i + (qk + 1)
                pool.wait_ge(p2_done, n)
                ncg.tensor_tensor(parts[:, qk, 2, :], rest[:, qk, :], parts[:, qk, 1, :], ALU.subtract)\
                   .then_inc(parts_done, 1)

            def values(b, j):
                if later(b, 1):
                    pool.wait_ge(pv_done, b * NQ + (j - (NQ - 1)))
                pool.wait_ge(v_moved, b + 1)
                v = vtok[:, 1, :, 32 * j:32 * j + 32].rearrange("p t (c d) -> p t c d", d=HD)
                ncg.tensor_tensor(vaug[:, :, 4 * j:4 * j + 4, 0:HD], v,
                                  one.unsqueeze(1).broadcast_to([P, TT, 4, HD]), ALU.mult)\
                   .then_inc(v_ready, 1)

            def move_values(i):
                pool.wait_ge(z_copied, (i + 1) * TT)
                if later(i, 1):
                    pool.wait_ge(v_ready, i * NQ)
                ncg.tensor_tensor(vtok[:, 1], vtok[:, 0], one.broadcast_to([P, TT, D]), ALU.mult).then_inc(v_moved, 1)

            def lines(i, r):
                n = 2 * (2 * i + r)
                shape = [P, NG, KNOTS - 1]
                pool.wait_ge(u7_ready, 2 * i + (r + 1))
                ncg.tensor_tensor(line[:, :, :], u7[:, :].unsqueeze(2).broadcast_to(shape),
                                  const[:, C_J:C_J + KNOTS - 1].unsqueeze(1).broadcast_to(shape), ALU.subtract)\
                   .then_inc(line_step, 1)
                pool.wait_ge(line_step, n + 1)
                ncg.tensor_tensor(line[:, :, :], line[:, :, :], dk[:, :].unsqueeze(1).broadcast_to(shape), ALU.mult)\
                   .then_inc(line_step, 1)
                pool.wait_ge(line_step, n + 2)
                ncg.tensor_tensor(line[:, :, :], line[:, :, :],
                                  vec[:, V_KNOT:V_KNOT + KNOTS - 1].unsqueeze(1).broadcast_to(shape), ALU.add)\
                   .then_inc(line_ready, 1)

            def hidden(i):
                pool.wait_ge(sc_copied, i + 1)
                ncg.tensor_tensor(hid[:, i], sc[:, :, NCL + NTILE:NSC],
                                  vec[:, V_B1:V_B1 + COMP].unsqueeze(1).broadcast_to([P, TT, COMP]), ALU.add)\
                   .then_inc(hid_ready, 1)

            def store_xf(i):
                pool.wait_ge(xf1_ready, i + 1)
                ncg.tensor_tensor(xf[:, i], xf1[:, :, :], one.broadcast_to([P, TT, D]), ALU.mult).then_inc(xf_stored, 1)

            def products(g):
                c = tiles_of(GROUPS[g])
                pool.wait_ge(gelu_done, g + 1)
                if g == 0:
                    pool.wait_ge(kt_done, 2 * B)
                for a, prod in enumerate((prod0, prod1)):
                    w2 = vec[:, V_W2 + a * COMP:V_W2 + (a + 1) * COMP]
                    ncg.tensor_tensor(prod[:, c, :], hidf[:, c, :],
                                      w2.unsqueeze(1).broadcast_to([P, c.stop - c.start, COMP]), ALU.mult)\
                       .then_inc(prod_ready, 1)

            def add_beta(k):
                c = tiles_of(CHUNKS[k])
                pool.wait_ge(xf1_ready, CHUNKS[k][1])
                ncg.tensor_tensor(xsf[:, c, :], xsf[:, c, :],
                                  vec[:, V_BET:V_BET + D].unsqueeze(1).broadcast_to([P, c.stop - c.start, D]), ALU.add)\
                   .then_inc(beta_in, 1)

            def scale(k):
                c = tiles_of(CHUNKS[k])
                pool.wait_ge(yn_ready, k + 1)
                ncg.tensor_tensor(xff[:, c, :], xff[:, c, :],
                                  vec[:, V_GAM:V_GAM + D].unsqueeze(1).broadcast_to([P, c.stop - c.start, D]), ALU.mult)\
                   .then_inc(scaled, 1)

            def spline_out(k, group):
                c = tiles_of(CHUNKS[k])
                direction = gotf[:, c, 4 * GRID + 1:TABW]
                pool.wait_ge(mag_ready, group + 1)
                ncg.tensor_tensor(direction, direction,
                                  mag[:, c].unsqueeze(2).broadcast_to([P, c.stop - c.start, D]), ALU.mult)\
                   .then_inc(weighted, 1)
                pool.wait_ge(weighted, k + 1)
                ncg.tensor_tensor(xff[:, c, :], xff[:, c, :], direction, ALU.add).then_inc(y_ready, 1)

            def residual_out(k):
                c = tiles_of(CHUNKS[k])
                pool.wait_ge(scaled, k + 1)
                pool.wait_ge(beta_in, k + 1)
                ncg.tensor_tensor(xsf[:, c, :], xsf[:, c, :], xff[:, c, :], ALU.add).then_inc(out_ready, 1)

            def body(b):
                k = place(b)
                if k >= 1:
                    values(b, 3)
                if k < B - 1:
                    move_values(b + 1)
                if k >= 2:
                    lines(b - 2, 1)
                if k == B - 2:
                    add_beta(0)
                    add_beta(1)
                if k == B - 1:
                    products(1)
                    spline_out(0, 0)
                if k < B - 1:
                    values(b + 1, 0)
                if k == B - 2:
                    products(0)
                if k >= 1:
                    store_xf(b - 1)
                if k == B - 1:
                    spline_out(1, 0)
                if k < B - 1:
                    values(b + 1, 1)
                if k < B - 2:
                    rotate_sin(b + 2)
                if k >= 1:
                    hidden(b - 1)
                if k < B - 1:
                    values(b + 1, 2)
                if k >= 1:
                    lines(b - 1, 0)
                if k == B - 1:
                    products(2)
                    scale(0)
                if k < B - 2:
                    split(b + 2, 0)
                    split(b + 2, 1)

            def last_ones():
                i = B - 1
                lines(i - 1, 1)
                add_beta(2)
                spline_out(2, 1)
                store_xf(i)
                hidden(i)
                lines(i, 0)
                products(3)
                add_beta(3)
                add_beta(4)
                lines(i, 1)
                residual_out(0)
                scale(1)
                residual_out(1)
                scale(2)
                residual_out(2)

            pool.wait_ge(rope_ready, 1)
            move_values(0)
            rotate_sin(0)
            split(0, 0)
            split(0, 1)
            for j in range(NQ):
                values(0, j)
            rotate_sin(1)
            split(1, 0)
            split(1, 1)
            over_batches(pool, body)
            last_ones()


def shape_constants():
    c = np.zeros((P, NCONST), np.float32)
    p = np.arange(P)
    c[:, C_ID:C_ID + P] = np.eye(P)
    c[:, C_MASK:C_MASK + P] = np.where(p[None, :] >= p[:, None], 0.0, MASKED)
    freqs = np.float32(THETA) ** (-np.arange(0, HD, 2, dtype=np.float32) / HD)
    ang = np.arange(T, dtype=np.float32)[:, None] * freqs[None, :]
    cos, sin = np.cos(ang).reshape(TT, P, HD // 2), np.sin(ang).reshape(TT, P, HD // 2)
    both = np.concatenate([cos, cos], -1).transpose(1, 0, 2)
    signed = np.concatenate([-sin, sin], -1).transpose(1, 0, 2)
    c[:, C_COS:C_COS + TT * HD] = both.reshape(P, -1)
    c[:, C_SIN:C_SIN + TT * HD] = signed.reshape(P, -1)
    c[:, C_STEP:C_STEP + KNOTS] = [-1, 1, 2, 3, 4, 5, 6, BIG]
    c[:, C_J:C_J + KNOTS] = np.arange(KNOTS)
    c[:, C_PREF:C_PREF + 8] = np.arange(8, 0, -1)
    c[:, C_EPS] = EPS_LN
    c[:, C_EPS + 1] = EPS_RMS
    return c


def kernel(**inputs):
    import concourse.bacc as bacc
    from concourse.bass_utils import run_bass_kernel_spmd

    a = {k: np.asarray(v) for k, v in inputs.items()}
    f = lambda name: a["L0_ffn_" + name]
    table = np.concatenate([f("spline_w1").reshape(NTILE, 2 * GRID), f("spline_b1"),
                            f("spline_w2").reshape(NTILE, GRID), f("spline_b2"), f("directions")], axis=1)
    vector = np.concatenate([a["L0_attn_q_norm_w"], a["L0_attn_k_norm_w"], f("knot_values"), f("temperature"),
                             f("compress_b1"), f("compress_w2").T.reshape(-1), f("compress_b2"),
                             f("norm_gamma"), f("norm_beta"), f("output_scale")])[None]
    arrays = {
        "x": a["L0_attn_x"],
        "w_qkv_t": a["L0_attn_w_qkv"].T,
        "w_proj_t": a["L0_attn_w_proj"].T,
        "signatures_t": f("signatures_raw").T,
        "compress_w1": f("compress_w1"),
        "table": table,
        "vector": vector,
        "shape_constants": shape_constants(),
    }
    arrays = {k: np.ascontiguousarray(v) for k, v in arrays.items()}
    nc = bacc.Bacc("TRN2", target_bir_lowering=False, num_devices=1)
    args = [nc.dram_tensor(k, v.shape, mybir.dt.from_np(v.dtype), kind="ExternalInput").ap()
            for k, v in arrays.items()]
    out = nc.dram_tensor("out", (B, T, D), F32, kind="ExternalOutput").ap()
    build(nc, *args, out)
    r = run_bass_kernel_spmd(nc, [arrays], core_ids=[0])
    return r.results[0]["out"]
```
